# Optimizing a Trainium2 kernel written in Bass

```python
import numpy as np
import jax
import jax.numpy as jnp

def _softmax(x, axis=-1):
    return jax.nn.softmax(x, axis=axis)

def _gelu(x):
    return jax.nn.gelu(x, approximate=True)

def _silu(x):
    return jax.nn.silu(x)

def _sigmoid(x):
    return jax.nn.sigmoid(x)

def _layernorm(x, axis=-1, eps=1e-05):
    m = jnp.mean(x, axis=axis, keepdims=True)
    v = jnp.var(x, axis=axis, keepdims=True)
    return (x - m) / jnp.sqrt(v + eps)

def _scatter_add(tgt, idx, src, axis=0):
    return tgt.at[idx].add(src)

def _segment_sum(src, seg, n):
    return jax.ops.segment_sum(src, seg, n)
kernel_name = 'mk_vit_tower_d2_tok_img256_r4_a5bd7a'

def setup_inputs(seed: int=0):
    np.random.seed(seed)
    _w = jnp.asarray

    def _rec_inputs():
        import jax
        import jax.numpy as jnp
        _rk = jax.random.key(seed)
        x = -0.000202321 + 1.00025 * jax.random.normal(jax.random.fold_in(_rk, 1), (4, 64, 56, 56), jnp.float32)
        return x
    x = _rec_inputs()

    def _L0_tok_setup():
        import jax, jax.numpy as jnp
        import numpy as np
        B, C, H, W = (8, 64, 56, 56)
        K = 3

        def _unfold3x3(x):
            b, c, h, w = x.shape
            xp = jnp.pad(x, ((0, 0), (0, 0), (1, 1), (1, 1)))
            patches = jnp.stack([xp[:, :, i:i + h, j:j + w] for i in range(K) for j in range(K)], axis=2)
            return patches.reshape(b, c * K * K, h * w).transpose(0, 2, 1)
        key = jax.random.key(seed)
        ks = jax.random.split(key, 8)
        d = C * K * K
        s1 = 1.0 / np.sqrt(d)
        s2 = 1.0 / np.sqrt(C)
        return {'x': jax.random.normal(ks[0], (B, C, H, W), jnp.float32), 'W1': jax.random.uniform(ks[1], (d, C), jnp.float32, -s1, s1), 'b1': jax.random.uniform(ks[2], (C,), jnp.float32, -s1, s1), 'W2': jax.random.uniform(ks[3], (C, d), jnp.float32, -s2, s2), 'b2': jax.random.uniform(ks[4], (d,), jnp.float32, -s2, s2), 'W3': jax.random.uniform(ks[5], (d, C), jnp.float32, -s1, s1), 'b3': jax.random.uniform(ks[6], (C,), jnp.float32, -s1, s1)}
    _L0_tok_all = _L0_tok_setup()
    _L0_tok_in = {k: v for k, v in _L0_tok_all.items() if k in ('W1', 'b1', 'W2', 'b2', 'W3', 'b3')}
    del _L0_tok_all

    def _L0_attn_setup():
        import jax, jax.numpy as jnp
        import numpy as np
        B, T, D = (4, 512, 64)
        W_LORA, A_LORA, G_LORA = (64, 64, 128)
        DECAY_SCALE = -0.6065306597126334
        EPS = D * 1e-05

        def _forward(x, x_mix, W_r, W_k, W_v, W_o, A_w, B_w, b_w, A_a, B_a, b_a, A_g, B_g, k_k, k_a, r_k, gn_w, gn_b):
            b, t, d = x.shape
            shifted = jnp.pad(x, ((0, 0), (1, 0), (0, 0)))[:, :-1]
            delta = shifted - x
            xr, xw, xk, xv, xa, xg = [x + delta * x_mix[i] for i in range(6)]
            r = xr @ W_r
            w = DECAY_SCALE * jax.nn.sigmoid(jnp.tanh(xw @ A_w) @ B_w + b_w)
            k = xk @ W_k
            v = xv @ W_v
            a = jax.nn.sigmoid(xa @ A_a @ B_a + b_a)
            g = jax.nn.sigmoid(xg @ A_g) @ B_g
            kk = k * k_k
            kk = kk / jnp.maximum(jnp.linalg.norm(kk, axis=-1, keepdims=True), 1e-12)
            k = k * (1.0 + (a - 1.0) * k_a)
            decay = jnp.exp(w)

            def step(S, inp):
                r_t, dec_t, k_t, v_t, kk_t, a_t = inp
                b_t = kk_t * a_t
                sa = jnp.einsum('bvk,bk->bv', S, -kk_t)
                S = S * dec_t[:, None, :] + sa[:, :, None] * b_t[:, None, :] + v_t[:, :, None] * k_t[:, None, :]
                o_t = jnp.einsum('bvk,bk->bv', S, r_t)
                return (S, o_t)
            tm = lambda z: jnp.swapaxes(z, 0, 1)
            S0 = jnp.zeros((b, d, d), x.dtype)
            _, o = jax.lax.scan(step, S0, (tm(r), tm(decay), tm(k), tm(v), tm(kk), tm(a)))
            o = jnp.swapaxes(o, 0, 1)
            mu = jnp.mean(o, axis=-1, keepdims=True)
            var = jnp.var(o, axis=-1, keepdims=True)
            o = (o - mu) * jax.lax.rsqrt(var + EPS) * gn_w + gn_b
            o = o + jnp.sum(r * k * r_k, axis=-1, keepdims=True) * v
            return o * g @ W_o
        key = jax.random.key(seed)
        ks = jax.random.split(key, 20)
        n = jax.random.normal
        p = {}
        p['x'] = n(ks[0], (B, T, D), jnp.float32)
        p['x_mix'] = n(ks[1], (6, D), jnp.float32) * 0.1
        s = 1.0 / np.sqrt(D).astype(np.float32)
        p['W_r'] = n(ks[2], (D, D), jnp.float32) * s
        p['W_k'] = n(ks[3], (D, D), jnp.float32) * s
        p['W_v'] = n(ks[4], (D, D), jnp.float32) * s
        p['W_o'] = n(ks[5], (D, D), jnp.float32) * s
        p['A_w'] = n(ks[6], (D, W_LORA), jnp.float32) * s
        p['B_w'] = n(ks[7], (W_LORA, D), jnp.float32) / np.sqrt(W_LORA).astype(np.float32)
        p['b_w'] = n(ks[8], (D,), jnp.float32) * 0.5
        p['A_a'] = n(ks[9], (D, A_LORA), jnp.float32) * s
        p['B_a'] = n(ks[10], (A_LORA, D), jnp.float32) / np.sqrt(A_LORA).astype(np.float32)
        p['b_a'] = n(ks[11], (D,), jnp.float32) * 0.1
        p['A_g'] = n(ks[12], (D, G_LORA), jnp.float32) * s
        p['B_g'] = n(ks[13], (G_LORA, D), jnp.float32) / np.sqrt(G_LORA).astype(np.float32)
        p['k_k'] = n(ks[14], (D,), jnp.float32) * 0.5 + 0.85
        p['k_a'] = n(ks[15], (D,), jnp.float32) * 0.1 + 1.0
        p['r_k'] = n(ks[16], (D,), jnp.float32) * 0.1
        p['gn_w'] = jnp.ones((D,), jnp.float32)
        p['gn_b'] = jnp.zeros((D,), jnp.float32)
        return p
    _L0_attn_all = _L0_attn_setup()
    _L0_attn_in = {k: v for k, v in _L0_attn_all.items() if k in ('x_mix', 'W_r', 'W_k', 'W_v', 'W_o', 'A_w', 'B_w', 'b_w', 'A_a', 'B_a', 'b_a', 'A_g', 'B_g', 'k_k', 'k_a', 'r_k', 'gn_w', 'gn_b')}
    del _L0_attn_all

    def _L0_ffn_setup():
        import jax, jax.numpy as jnp
        import numpy as np
        B, T, D, H, E = (16, 1024, 64, 128, 8)
        key = jax.random.key(seed)
        ks = jax.random.split(key, 5)
        x = jax.random.normal(ks[0], (B, T, D), dtype=jnp.float32)
        gate_w = jax.random.normal(ks[1], (D, E), dtype=jnp.float32) * 0.02
        gate_b = jnp.zeros((E,), dtype=jnp.float32)
        W1 = jax.random.normal(ks[2], (E, D, H), dtype=jnp.float32) * 0.02
        b1 = jnp.zeros((E, H), dtype=jnp.float32)
        W2 = jax.random.normal(ks[3], (E, H, D), dtype=jnp.float32) * 0.02
        b2 = jnp.zeros((E, D), dtype=jnp.float32)
        return {'x': x, 'gate_w': gate_w, 'gate_b': gate_b, 'W1': W1, 'b1': b1, 'W2': W2, 'b2': b2}
    _L0_ffn_all = _L0_ffn_setup()
    _L0_ffn_in = {k: v for k, v in _L0_ffn_all.items() if k in ('gate_w', 'gate_b', 'W1', 'b1', 'W2', 'b2')}
    del _L0_ffn_all

    def _L1_attn_setup():
        import jax, jax.numpy as jnp
        import numpy as np
        TEMPERATURE = 1.0
        W_BLEND = 0.8
        EPS = 1e-12

        def _l2norm(x):
            n = jnp.sqrt(jnp.sum(x * x, axis=-1, keepdims=True))
            return x / jnp.maximum(n, EPS)
        key = jax.random.key(seed)
        feats = jax.random.normal(key, (4, 512, 64), dtype=jnp.float32)
        return {'feats': feats}
    _L1_attn_all = _L1_attn_setup()
    _L1_attn_in = {k: v for k, v in _L1_attn_all.items() if k in ()}
    del _L1_attn_all

    def _L1_ffn_setup():
        import math
        import jax, jax.numpy as jnp
        import numpy as np
        CAPACITY_FACTOR = 1.25
        key = jax.random.key(seed)
        ks = jax.random.split(key, 5)
        B, L, D, F, E = (8, 2048, 64, 256, 8)
        h = jax.random.normal(ks[0], (B, L, D), dtype=jnp.float32)
        gate_w = jax.random.normal(ks[1], (D, E), dtype=jnp.float32) * 0.02
        gate_b = jnp.zeros((E,), dtype=jnp.float32)
        w1 = jax.random.normal(ks[2], (E, D, F), dtype=jnp.float32) * (1.0 / math.sqrt(D))
        b1 = jnp.zeros((E, F), dtype=jnp.float32)
        w2 = jax.random.normal(ks[3], (E, F, D), dtype=jnp.float32) * (1.0 / math.sqrt(F))
        b2 = jnp.zeros((E, D), dtype=jnp.float32)
        return {'h': h, 'gate_w': gate_w, 'gate_b': gate_b, 'w1': w1, 'b1': b1, 'w2': w2, 'b2': b2}
    _L1_ffn_all = _L1_ffn_setup()
    _L1_ffn_in = {k: v for k, v in _L1_ffn_all.items() if k in ('gate_w', 'gate_b', 'w1', 'b1', 'w2', 'b2')}
    del _L1_ffn_all
    return {'x': x, 'L0_tok_W1': _L0_tok_in['W1'], 'L0_tok_b1': _L0_tok_in['b1'], 'L0_tok_W2': _L0_tok_in['W2'], 'L0_tok_b2': _L0_tok_in['b2'], 'L0_tok_W3': _L0_tok_in['W3'], 'L0_tok_b3': _L0_tok_in['b3'], 'L0_attn_x_mix': _L0_attn_in['x_mix'], 'L0_attn_W_r': _L0_attn_in['W_r'], 'L0_attn_W_k': _L0_attn_in['W_k'], 'L0_attn_W_v': _L0_attn_in['W_v'], 'L0_attn_W_o': _L0_attn_in['W_o'], 'L0_attn_A_w': _L0_attn_in['A_w'], 'L0_attn_B_w': _L0_attn_in['B_w'], 'L0_attn_b_w': _L0_attn_in['b_w'], 'L0_attn_A_a': _L0_attn_in['A_a'], 'L0_attn_B_a': _L0_attn_in['B_a'], 'L0_attn_b_a': _L0_attn_in['b_a'], 'L0_attn_A_g': _L0_attn_in['A_g'], 'L0_attn_B_g': _L0_attn_in['B_g'], 'L0_attn_k_k': _L0_attn_in['k_k'], 'L0_attn_k_a': _L0_attn_in['k_a'], 'L0_attn_r_k': _L0_attn_in['r_k'], 'L0_attn_gn_w': _L0_attn_in['gn_w'], 'L0_attn_gn_b': _L0_attn_in['gn_b'], 'L0_ffn_gate_w': _L0_ffn_in['gate_w'], 'L0_ffn_gate_b': _L0_ffn_in['gate_b'], 'L0_ffn_W1': _L0_ffn_in['W1'], 'L0_ffn_b1': _L0_ffn_in['b1'], 'L0_ffn_W2': _L0_ffn_in['W2'], 'L0_ffn_b2': _L0_ffn_in['b2'], 'L1_ffn_gate_w': _L1_ffn_in['gate_w'], 'L1_ffn_gate_b': _L1_ffn_in['gate_b'], 'L1_ffn_w1': _L1_ffn_in['w1'], 'L1_ffn_b1': _L1_ffn_in['b1'], 'L1_ffn_w2': _L1_ffn_in['w2'], 'L1_ffn_b2': _L1_ffn_in['b2']}

def reference(x, L0_tok_W1, L0_tok_b1, L0_tok_W2, L0_tok_b2, L0_tok_W3, L0_tok_b3, L0_attn_x_mix, L0_attn_W_r, L0_attn_W_k, L0_attn_W_v, L0_attn_W_o, L0_attn_A_w, L0_attn_B_w, L0_attn_b_w, L0_attn_A_a, L0_attn_B_a, L0_attn_b_a, L0_attn_A_g, L0_attn_B_g, L0_attn_k_k, L0_attn_k_a, L0_attn_r_k, L0_attn_gn_w, L0_attn_gn_b, L0_ffn_gate_w, L0_ffn_gate_b, L0_ffn_W1, L0_ffn_b1, L0_ffn_W2, L0_ffn_b2, L1_ffn_gate_w, L1_ffn_gate_b, L1_ffn_w1, L1_ffn_b1, L1_ffn_w2, L1_ffn_b2):
    import jax
    import jax.numpy as jnp

    def _L0_tok_ref(x, W1, b1, W2, b2, W3, b3):
        import jax, jax.numpy as jnp
        import numpy as np
        B, C, H, W = (8, 64, 56, 56)
        K = 3

        def _unfold3x3(x):
            b, c, h, w = x.shape
            xp = jnp.pad(x, ((0, 0), (0, 0), (1, 1), (1, 1)))
            patches = jnp.stack([xp[:, :, i:i + h, j:j + w] for i in range(K) for j in range(K)], axis=2)
            return patches.reshape(b, c * K * K, h * w).transpose(0, 2, 1)
        t = _unfold3x3(x)
        h1 = jax.nn.relu(jnp.einsum('bld,dc->blc', t, W1) + b1)
        s = jax.nn.sigmoid(jnp.einsum('blc,cd->bld', h1, W2) + b2)
        out = jnp.einsum('bld,dc->blc', t * s, W3) + b3
        return out

    def _L0_attn_ref(x, x_mix, W_r, W_k, W_v, W_o, A_w, B_w, b_w, A_a, B_a, b_a, A_g, B_g, k_k, k_a, r_k, gn_w, gn_b):
        import jax, jax.numpy as jnp
        import numpy as np
        B, T, D = (4, 512, 64)
        W_LORA, A_LORA, G_LORA = (64, 64, 128)
        DECAY_SCALE = -0.6065306597126334
        EPS = D * 1e-05

        def _forward(x, x_mix, W_r, W_k, W_v, W_o, A_w, B_w, b_w, A_a, B_a, b_a, A_g, B_g, k_k, k_a, r_k, gn_w, gn_b):
            b, t, d = x.shape
            shifted = jnp.pad(x, ((0, 0), (1, 0), (0, 0)))[:, :-1]
            delta = shifted - x
            xr, xw, xk, xv, xa, xg = [x + delta * x_mix[i] for i in range(6)]
            r = xr @ W_r
            w = DECAY_SCALE * jax.nn.sigmoid(jnp.tanh(xw @ A_w) @ B_w + b_w)
            k = xk @ W_k
            v = xv @ W_v
            a = jax.nn.sigmoid(xa @ A_a @ B_a + b_a)
            g = jax.nn.sigmoid(xg @ A_g) @ B_g
            kk = k * k_k
            kk = kk / jnp.maximum(jnp.linalg.norm(kk, axis=-1, keepdims=True), 1e-12)
            k = k * (1.0 + (a - 1.0) * k_a)
            decay = jnp.exp(w)

            def step(S, inp):
                r_t, dec_t, k_t, v_t, kk_t, a_t = inp
                b_t = kk_t * a_t
                sa = jnp.einsum('bvk,bk->bv', S, -kk_t)
                S = S * dec_t[:, None, :] + sa[:, :, None] * b_t[:, None, :] + v_t[:, :, None] * k_t[:, None, :]
                o_t = jnp.einsum('bvk,bk->bv', S, r_t)
                return (S, o_t)
            tm = lambda z: jnp.swapaxes(z, 0, 1)
            S0 = jnp.zeros((b, d, d), x.dtype)
            _, o = jax.lax.scan(step, S0, (tm(r), tm(decay), tm(k), tm(v), tm(kk), tm(a)))
            o = jnp.swapaxes(o, 0, 1)
            mu = jnp.mean(o, axis=-1, keepdims=True)
            var = jnp.var(o, axis=-1, keepdims=True)
            o = (o - mu) * jax.lax.rsqrt(var + EPS) * gn_w + gn_b
            o = o + jnp.sum(r * k * r_k, axis=-1, keepdims=True) * v
            return o * g @ W_o
        return _forward(x, x_mix, W_r, W_k, W_v, W_o, A_w, B_w, b_w, A_a, B_a, b_a, A_g, B_g, k_k, k_a, r_k, gn_w, gn_b)

    def _L0_ffn_ref(x, gate_w, gate_b, W1, b1, W2, b2):
        import jax, jax.numpy as jnp
        import numpy as np
        B, T, D, H, E = (16, 1024, 64, 128, 8)
        Bb, Tt, Dd = x.shape
        Ee = gate_w.shape[1]
        xf = x.reshape(-1, Dd)
        N = xf.shape[0]
        logits = xf @ gate_w + gate_b
        probs = jax.nn.softmax(logits, axis=-1)
        top2_vals, top2_idx = jax.lax.top_k(probs, 2)
        cw = jnp.zeros((N, Ee), dtype=xf.dtype).at[jnp.arange(N)[:, None], top2_idx].add(top2_vals)

        def step(acc, params):
            w1, bb1, w2, bb2, we = params
            h = jax.nn.gelu(xf @ w1 + bb1, approximate=False)
            y = h @ w2 + bb2
            return (acc + we[:, None] * y, None)
        out, _ = jax.lax.scan(step, jnp.zeros_like(xf), (W1, b1, W2, b2, cw.T))
        return out.reshape(Bb, Tt, Dd)

    def _L1_attn_ref(feats):
        import jax, jax.numpy as jnp
        import numpy as np
        TEMPERATURE = 1.0
        W_BLEND = 0.8
        EPS = 1e-12

        def _l2norm(x):
            n = jnp.sqrt(jnp.sum(x * x, axis=-1, keepdims=True))
            return x / jnp.maximum(n, EPS)
        B, N, C = feats.shape
        f = _l2norm(feats.reshape(B * N, C))
        scores = jnp.matmul(f, f.T) / TEMPERATURE
        attn = jax.nn.softmax(scores, axis=-1)
        feats_att = jnp.matmul(attn, f)
        feats_fcm = f * W_BLEND + feats_att * (1.0 - W_BLEND)
        return _l2norm(feats_fcm.reshape(B, N, C))

    def _L1_ffn_ref(h, gate_w, gate_b, w1, b1, w2, b2):
        import math
        import jax, jax.numpy as jnp
        import numpy as np
        CAPACITY_FACTOR = 1.25
        B, L, D = h.shape
        E = gate_w.shape[1]
        T = B * L
        C = max(1, math.ceil(CAPACITY_FACTOR * T / E))
        x = h.reshape(T, D)
        logits = x @ gate_w + gate_b
        probs = jax.nn.softmax(logits, axis=-1)
        idx = jnp.argmax(probs, axis=-1)
        prb = jnp.take_along_axis(probs, idx[:, None], axis=1)[:, 0]
        one_hot = jax.nn.one_hot(idx, E, dtype=jnp.float32)
        pos = (jnp.cumsum(one_hot, axis=0) * one_hot).sum(-1).astype(jnp.int32) - 1
        kept = pos < C
        pos_safe = jnp.where(kept, pos, C)
        buf = jnp.zeros((E, C, D), dtype=h.dtype).at[idx, pos_safe].set(x, mode='drop')
        hmid = jax.nn.relu(jnp.einsum('ecd,edf->ecf', buf, w1) + b1[:, None, :])
        ybuf = jnp.einsum('ecf,efd->ecd', hmid, w2) + b2[:, None, :]
        pos_g = jnp.minimum(pos, C - 1)
        y_tok = ybuf[idx, pos_g] * (prb * kept)[:, None]
        y = y_tok.reshape(B, L, D)
        y = jnp.nan_to_num(y, nan=0.0, posinf=10000.0, neginf=-10000.0)
        return y
    h = _L0_tok_ref(x, L0_tok_W1, L0_tok_b1, L0_tok_W2, L0_tok_b2, L0_tok_W3, L0_tok_b3)
    h = h + _L0_attn_ref(_layernorm(h, axis=-1), L0_attn_x_mix, L0_attn_W_r, L0_attn_W_k, L0_attn_W_v, L0_attn_W_o, L0_attn_A_w, L0_attn_B_w, L0_attn_b_w, L0_attn_A_a, L0_attn_B_a, L0_attn_b_a, L0_attn_A_g, L0_attn_B_g, L0_attn_k_k, L0_attn_k_a, L0_attn_r_k, L0_attn_gn_w, L0_attn_gn_b)
    h = h + _L0_ffn_ref(_layernorm(h, axis=-1), L0_ffn_gate_w, L0_ffn_gate_b, L0_ffn_W1, L0_ffn_b1, L0_ffn_W2, L0_ffn_b2)
    h = h + _L1_attn_ref(_layernorm(h, axis=-1))
    h = h + _L1_ffn_ref(_layernorm(h, axis=-1), L1_ffn_gate_w, L1_ffn_gate_b, L1_ffn_w1, L1_ffn_b1, L1_ffn_w2, L1_ffn_b2)
    return h

_drawn_inputs = setup_inputs


def setup_inputs(seed=0):
    import zlib

    import numpy as np

    out = dict(_drawn_inputs(seed))
    spreads = {'L0_attn_gn_w': (1.0, 0.2),
     'L0_attn_gn_b': (0.0, 0.1),
     'L0_ffn_gate_b': (0.0, 0.1),
     'L0_ffn_b1': (0.0, 0.67),
     'L0_ffn_b2': (0.0, 0.1),
     'L1_ffn_gate_b': (0.0, 0.1),
     'L1_ffn_b1': (0.0, 0.583),
     'L1_ffn_b2': (0.0, 0.407)}
    factors = {'L0_tok_b1': 3.649, 'L0_ffn_W1': 4.594, 'L0_ffn_W2': 4.377}
    for name, (base, spread) in spreads.items():
        noise = np.random.default_rng([zlib.crc32(name.encode()), seed]).standard_normal(out[name].shape)
        drawn = base * np.exp(spread * noise) if base else spread * noise
        out[name] = jnp.asarray(drawn.astype(out[name].dtype))
    for name, factor in factors.items():
        out[name] = (out[name] * factor).astype(out[name].dtype)
    return out
```

```python
from contextlib import ExitStack, contextmanager
import numpy as np
from concourse import bass, mybir
F32 = mybir.dt.float32
F16 = mybir.dt.float16
U32 = mybir.dt.uint32
ALU = mybir.AluOpType
ACT = mybir.ActivationFunctionType
AX = mybir.AxisListType

BATCH, CH, IMG = 4, 64, 56
D = CH
SEQ = IMG * IMG
TOK = BATCH * SEQ
NTT = TOK // 128
GRP = 7
NG = NTT // GRP
QB = GRP * 128
QH = QB // 2
LN_EPS = 1e-5
N_EPS = 1e-12
FMAX = 3.4028234663852886e38

PAD = IMG + 2
ROWS = 8
TILE = ROWS * IMG
NT = IMG // ROWS
SUB = TILE // 4
TAPS = [(0, 0), (0, 1), (1, 0), (1, 1), (2, 0), (2, 1), (0, 2), (1, 2), (2, 2)]
NCH = 5

GN_EPS = D * 1e-5
DECAY = -0.6065306597126334
CS = 64
NIT = NTT // 2
LEVELS = 5

EX = 8
F1 = 128
F2 = 256
CAP = -(-5 * TOK // (4 * EX))
CU = 4
UT = CAP // CU
ST = 5
SR = UT // ST

FS = 64.0
BLEND = 0.8


@contextmanager
def semaphore(nc, name):
    s = nc.alloc_semaphore(name=name)
    yield s
    nc.gpsimd.sem_clear(s)
    nc.release_semaphore(s)


def constants():
    s, t = np.meshgrid(np.arange(128), np.arange(128), indexing="ij")
    same = s // CS == t // CS
    up, upi = same & (s < t), same & (s <= t)
    c = {"tri": np.concatenate([upi, same & (s > t)], 1),
         "ind": np.stack([np.arange(128) // CS == k for k in range(2)], 1),
         "mask": np.concatenate([up, upi, up, upi], 1),
         "neg0": -np.concatenate([(s % 2 == 1) & (t == s - 1), (t % 2 == 1) & (s == t - 1)], 1).astype(np.float32),
         "lev": np.concatenate([(s >> (l + 1) == t >> (l + 1)) & ((t >> l) & 1 == 1) & ((s >> l) & 1 == 0)
                                for l in range(1, LEVELS + 1)], 1),
         "eye": s == t,
         "keep": np.tile((np.arange(1, TOK // CS + 1) % (SEQ // CS) != 0)[None], (D, 1))}
    return {k: np.ascontiguousarray(v.astype(np.float32)) for k, v in c.items()}


def linker(eng, sem, base=0):
    n = [0]

    def link(ins):
        n[0] += 1
        ins.then_inc(sem, 1)
        eng.wait_ge(sem, base + n[0])
    link.count = n
    return link


def bc(ap, n):
    p, g = ap.shape
    return ap.rearrange("p (g a) -> p g a", a=1).broadcast_to([p, g, n])


def rep(ap, n):
    p, c = ap.shape
    return ap.rearrange("p (a c) -> p a c", a=1).broadcast_to([p, n, c])


def norm_features(nc, h, Z2, eye):
    with ExitStack() as ctx:
        sb = lambda name, shape, dt=F32: ctx.enter_context(nc.sbuf_tensor(name, shape, dt))
        sem = lambda name: ctx.enter_context(semaphore(nc, name))
        hin = sb("B0_hin", [128, 2, GRP, D])
        xc = sb("B0_xc", [128, 2, GRP, D])
        sq = sb("B0_sq", [128, GRP, D])
        st = sb("B0_st", [128, 2, 4, GRP])
        pT = ctx.enter_context(nc.psum_tensor("B0_pT", [128, 2, 512], F32))
        s_in = [sem(f"B0_h_in{k}") for k in range(2)]
        s_free, s_link, s_var, s_sqrt = sem("B0_h_used"), sem("B0_step"), sem("B0_var"), sem("B0_root")
        s_x, s_T, s_ev, s_z, s_sh = sem("B0_normed"), sem("B0_transposed"), sem("B0_features"), sem("B0_starts"), sem("B0_shifted")
        hv = h.rearrange("(g j p) c -> g p j c", p=128, j=GRP)
        block = ctx.enter_context(nc.Block())

        @block.sync
        def _(sp):
            for k in range(2):
                sp.dma_start(hin[:, k], hv[k]).then_inc(s_in[k], 16)
            with sp.Fori(0, NG // 2 - 1) as g:
                for k in range(2):
                    sp.wait_ge(s_free, 2 * g + k + 1)
                    sp.dma_start(hin[:, k], hv[2 * g + 2 + k]).then_inc(s_in[k], 16)
            for b in range(BATCH):
                sp.wait_ge(s_ev, 2 + min(NG, -(-(b + 1) * SEQ // QB)))
                sp.dma_start(Z2[D:2 * D, b * SEQ + 1:(b + 1) * SEQ], Z2[0:D, b * SEQ:(b + 1) * SEQ - 1]).then_inc(s_sh, 16)
            sp.wait_ge(s_sh, 16 * BATCH)

        @block.gpsimd
        def _(pool):
            for b in range(BATCH):
                m = pool.memset(Z2[D:2 * D, b * SEQ:b * SEQ + 1], 0.0)
            m.then_inc(s_z, 1)

        LINKS = 6

        @block.vector
        def _(dve):
            with dve.Fori(0, NG // 2) as gg:
                for k in range(2):
                    g = 2 * gg + k
                    link = linker(dve, s_link, g * LINKS)
                    S = lambda i: st[:, k, i, :]
                    dve.wait_ge(s_in[k], 16 * gg + 16)
                    dve.wait_ge(s_T, g + 1)
                    link(dve.tensor_reduce(S(0), hin[:, k], AX.X, ALU.add))
                    link(dve.tensor_scalar(S(1), S(0), 1.0 / D, None, ALU.mult))
                    link(dve.tensor_tensor(xc[:, k], hin[:, k], bc(S(1), D), ALU.subtract))
                    dve.sem_inc(s_free, 1)
                    link(dve.tensor_tensor(sq[:, :, :], xc[:, k], xc[:, k], ALU.mult))
                    link(dve.tensor_reduce(S(2), sq[:, :, :], AX.X, ALU.add))
                    link(dve.tensor_scalar(S(2), S(2), 1.0 / D, LN_EPS, ALU.mult, ALU.add))
                    dve.reciprocal(S(3), S(2)).then_inc(s_var, 1)
                    dve.wait_ge(s_sqrt, g + 1)
                    dve.tensor_tensor(xc[:, k], xc[:, k], bc(S(3), D), ALU.mult).then_inc(s_x, 1)
                    assert link.count[0] == LINKS

        @block.tensor
        def _(pe):
            pe.sem_inc(s_T, 2)
            with pe.Fori(0, NG // 2) as gg:
                for k in range(2):
                    g = 2 * gg + k
                    pe.wait_ge(s_x, g + 1)
                    pe.wait_ge(s_ev, g + 1)
                    for j in range(GRP // 2):
                        pe.transpose(pT[:, k, j * 128:j * 128 + 128], xc[:, k, 2 * j:2 * j + 2, :], eye[:, :])
                    m = pe.transpose(pT[0:D, k, 384:512], xc[:, k, GRP - 1, :], eye[:, :])
                    m.then_inc(s_T, 1)

        @block.scalar
        def _(act):
            act.preload_act_table(ACT.Sqrt)
            act.sem_inc(s_ev, 2)
            with act.Fori(0, NG // 2) as gg:
                for k in range(2):
                    g = 2 * gg + k
                    act.wait_ge(s_var, g + 1)
                    act.activation(st[:, k, 3, :], st[:, k, 3, :], ACT.Sqrt).then_inc(s_sqrt, 1)
                    act.wait_ge(s_T, g + 3)
                    z = Z2[0:D, bass.ds(g * QB, QB)]
                    pairs = lambda x: z[:, 0:768].rearrange("p (j x n) -> p x j n", x=2, n=128)[:, x]
                    act.activation(pairs(0), pT[0:D, k, 0:384].rearrange("p (j n) -> p j n", n=128), ACT.Copy)
                    act.activation(pairs(1), pT[D:128, k, 0:384].rearrange("p (j n) -> p j n", n=128), ACT.Copy)
                    act.activation(z[:, 768:896], pT[0:D, k, 384:512], ACT.Copy).then_inc(s_ev, 1)


def project(nc, w, Z2, rkv, rn):
    with ExitStack() as ctx:
        sb = lambda name, shape, dt=F32: ctx.enter_context(nc.sbuf_tensor(name, shape, dt))
        sem = lambda name: ctx.enter_context(semaphore(nc, name))
        zs = sb("P_zs", [128, 2, QB])
        kk = sb("P_kk", [128, GRP, D])
        pR = ctx.enter_context(nc.psum_tensor("P_pR", [128, 2, 4, 512], F32))
        s_zs, s_p, s_rkv, s_kk, s_n, s_end, s_root = (sem("P_" + x) for x in (
            "tile_moved", "projected", "rows_copied", "keys_scaled", "norms", "norms_done", "root"))
        block = ctx.enter_context(nc.Block())

        @block.scalar
        def _(act):
            act.preload_act_table(ACT.Sqrt)
            with act.Fori(0, NG // 2) as gg:
                for k in range(2):
                    g = 2 * gg + k
                    act.wait_ge(s_p, g + 1)
                    act.activation(zs[:, k, :], Z2[:, bass.ds(g * QB, QB)], ACT.Copy).then_inc(s_zs, 1)
            act.wait_ge(s_end, 1)
            act.activation(rn[:, :], rn[:, :], ACT.Sqrt).then_inc(s_root, 1)

        @block.tensor
        def _(pe):
            pe.sem_inc(s_p, 2)
            with pe.Fori(0, NG // 2) as gg:
                for k in range(2):
                    g = 2 * gg + k
                    pe.wait_ge(s_zs, g + 1)
                    pe.wait_ge(s_rkv, g + 1)
                    for j in range(GRP):
                        m = pe.matmul(pR[:, k, j // 2, (j % 2) * 192:(j % 2) * 192 + 192],
                                      zs[:, k, j * 128:j * 128 + 128], w["rkv"][:, :], start=True, stop=True)
                    m.then_inc(s_p, 1)

        @block.vector
        def _(dve):
            dve.sem_inc(s_rkv, 2)
            with dve.Fori(0, NG // 2) as gg:
                for k in range(2):
                    g = 2 * gg + k
                    dve.wait_ge(s_p, g + 3)
                    dve.tensor_copy(rkv[:, bass.ds(g * GRP, 6), :].rearrange("p (b j) c -> p b j c", j=2),
                                    pR[:, k, 0:3, 0:384].rearrange("p b (j c) -> p b j c", j=2))
                    dve.tensor_copy(rkv[:, bass.ds(g * GRP + 6, 1), :].rearrange("p a c -> p (a c)"),
                                    pR[:, k, 3, 0:192]).then_inc(s_rkv, 1)
                    dve.wait_ge(s_rkv, g + 3)
                    dve.tensor_tensor(kk[:, :, :], rkv[:, bass.ds(g * GRP, GRP), D:2 * D], rep(w["k_k"][:, :], GRP),
                                      ALU.mult).then_inc(s_kk, 1)
                    dve.wait_ge(s_kk, 2 * g + 1)
                    dve.tensor_tensor(kk[:, :, :], kk[:, :, :], kk[:, :, :], ALU.mult).then_inc(s_kk, 1)
                    dve.wait_ge(s_kk, 2 * g + 2)
                    dve.tensor_reduce(rn[:, bass.ds(g * GRP, GRP)], kk[:, :, :], AX.X, ALU.add).then_inc(s_n, 1)
                    dve.wait_ge(s_n, g + 1)
            dve.sem_inc(s_end, 1)
            dve.wait_ge(s_root, 1)
            dve.tensor_scalar(rn[:, :], rn[:, :], N_EPS, None, ALU.max).then_inc(s_end, 1)
            dve.wait_ge(s_end, 2)
            dve.reciprocal(rn[:, :], rn[:, :]).then_inc(s_end, 1)


def recurrence(nc, w, c, Z2, rkv, gate_, rn):
    with ExitStack() as ctx:
        sb = lambda name, shape, dt=F32: ctx.enter_context(nc.sbuf_tensor(name, shape, dt))
        sem = lambda name: ctx.enter_context(semaphore(nc, "R_" + name))
        hid = sb("R_hid", [128, 256])
        gh = sb("R_gh", [128, 256])
        wa = sb("R_wa", [128, 2, 128])
        lw = sb("R_lw", [128, 2, D])
        a_ = sb("R_a", [128, 2, D])
        ex = sb("R_ex", [128, 2, D])
        eP = sb("R_eP", [128, 2, D])
        eN = sb("R_eN", [128, 2, D])
        eS = sb("R_eS", [128, 2, D])
        eX = sb("R_eX", [128, 2, D])
        kn = sb("R_kn", [128, 2, D])
        kp = sb("R_kp", [128, 2, D])
        bt = sb("R_bt", [128, 2, D])
        rk = sb("R_rk", [128, 2, D])
        rs = sb("R_rs", [128, 2])
        V = sb("R_V", [128, 2, 2, D])
        DC = sb("R_DC", [D, 2, 4])
        QN = sb("R_QN", [128, 2, 2, 128])
        RBK = sb("R_QRBK", [128, 4, 2, D])
        Bh = sb("R_Bh", [128, 2, 2, 2, D])
        Kh = sb("R_Kh", [128, 2, 2, 2, D])
        FT = sb("R_FT", [D, 2, 2, 512])
        PM = sb("R_PM", [128, 2, 2, 512])
        ML = sb("R_ML", [128, LEVELS, 2, 128])
        XX = sb("R_XX", [128, 2, 2, 128])
        XT = sb("R_XT", [128, 2, 2, 128])
        Ys = sb("R_Ys", [128, 2, 128])
        WU = sb("R_WU", [128, 2, 128])
        RpT = sb("R_RpT", [D, 256])
        GT = sb("R_GT", [D, 4, D])
        Z = sb("R_Z", [D, 4, D])
        bank = [ctx.enter_context(nc.psum_tensor(f"R_b{i}", [128, 512], F32)) for i in range(8)]
        pH = bank[0]
        pW = bank[1][:, 0:384].rearrange("p (t c) -> p t c", t=2)
        pN = bank[1][:, 384:512].rearrange("p (t c) -> p t c", t=2)
        pC = bank[2][:, 0:256].rearrange("p (t c) -> p t c", t=2)
        pD = bank[2][0:D, 256:260]
        pO = bank[2][:, 264:392].rearrange("p (t c) -> p t c", t=2)
        pT = bank[3:5]
        pL = bank[5][:, 0:256].rearrange("p (t c) -> p t c", t=2)
        pZ = bank[6][0:D, 0:256].rearrange("p (n c) -> p n c", n=4)
        pY = bank[5][:, 256:512].rearrange("p (t c) -> p t c", t=2)
        pWU = bank[6][:, 256:512].rearrange("p (t c) -> p t c", t=2)
        pX = bank[7][:, :].rearrange("p (t x c) -> p t x c", t=2, x=2)
        pR = bank[0][0:D, 0:256]
        pG = bank[0][0:D, 256:512].rearrange("p (n c) -> p n c", n=4)
        (s_hp, s_hid, s_gs, s_wp, s_wa, s_th, s_V, s_g, s_lw, s_cum, s_ex, s_exp, s_el, s_T, s_FT, s_prod, s_mask,
         s_ML, s_X, s_Y, s_Ys, s_pX, s_pN, s_QN, s_pWU, s_WU, s_pRG, s_RG, s_pZ, s_Z, s_pO, s_O, s_dve, s_xl, s_xw, s_dI, s_pO0, s_qn) = (
            sem(x) for x in ("hidden", "hidden_copied", "gate_hidden", "lora", "lora_biased", "lora_tanh", "v_copied",
                             "gate_stored", "log_decay", "cumulated", "exclusive", "exponentials", "scaled", "turned",
                             "turned_copied", "products", "masked", "level_masks", "inverse", "inner", "inner_copied",
                             "merge", "nv", "nv_copied", "wu", "wu_copied", "rg", "rg_copied", "state_sum", "state",
                             "out", "out_stored", "token_step", "first_blocks", "first_blocks_turned", "decay_diagonal", "first_state_used", "q_copied"))
        block = ctx.enter_context(nc.Block())

        def wait(eng, s, n):
            if not (isinstance(n, int) and n <= 0):
                eng.wait_ge(s, n)

        def run(eng, step):
            step(-1, 1, inv=False, state=False)
            step(0, 0, state=False)
            with eng.Fori(0, (NIT - 3) // 2) as m:
                step(2 * m + 1, 1)
                step(2 * m + 2, 0)
            step(NIT - 2, 1)
            step(NIT - 1, 0, front=False)
            step(NIT, 1, front=False, inv=False)

        @block.tensor
        def _(pe):
            def hidden(i, p):
                wait(pe, s_hid, i)
                wait(pe, s_RG, i - 2)
                z = Z2[:, bass.ds(256 * i, 256)]
                pe.matmul(pH[:, 0:256], w["Awa"][:, :], z, start=True, stop=True)
                pe.matmul(pH[:, 256:512], w["Ag"][:, :], z, start=True, stop=True).then_inc(s_hp, 1)

            def lora(i, p):
                pe.wait_ge(s_gs, i + 1)
                wait(pe, s_wa, i)
                wait(pe, s_g, i)
                wait(pe, s_QN, i - 1)
                for t in range(2):
                    pe.matmul(pW[:, t, 0:128], hid[:, t * 128:t * 128 + 128], w["Bwa"][:, :], start=True, stop=True)
                    m = pe.matmul(pW[:, t, 128:192], gh[:, t * 128:t * 128 + 128], w["Bg"][:, :], start=True, stop=True)
                m.then_inc(s_wp, 1)

            def cumulate(i, p):
                pe.wait_ge(s_lw, i + 1)
                wait(pe, s_exp, i)
                wait(pe, s_O, i - 2)
                for t in range(2):
                    for x in range(2):
                        pe.matmul(pC[:, t, x * D:x * D + D], c["tri"][:, x * 128:x * 128 + 128], lw[:, t, :], start=True, stop=True)
                    m = pe.matmul(pD[:, 2 * t:2 * t + 2], lw[:, t, :], c["ind"][:, :], start=True, stop=True)
                m.then_inc(s_cum, 1)

            def turn(i, p):
                pe.wait_ge(s_el, i + 1)
                wait(pe, s_mask, i)
                for x, src in enumerate(RBK[:, x] for x in range(4)):
                    m = pe.transpose(pT[0][:, x * 128:x * 128 + 128], src, c["eye"][:, :])
                m.then_inc(s_T, 1)

            def products(i, p):
                pe.wait_ge(s_FT, i + 1)
                wait(pe, s_xl, i)
                wait(pe, s_Ys, 5 * i)
                for t in range(2):
                    F = lambda x, n=1: FT[:, p, t, x * 128:(x + n) * 128]
                    pe.matmul(pT[t][:, 0:256], F(2), F(0, 2), start=True, stop=True)
                    pe.matmul(pT[t][:, 256:512], F(3), F(0, 2), start=True, stop=True)
                    m = pe.matmul(pL[:, t, :], F(0), F(2), start=True, stop=True)
                m.then_inc(s_prod, 1)

            def inner(i, p, l):
                if l == 1:
                    pe.wait_ge(s_ML, i + 1)
                pe.wait_ge(s_X, 6 * i + l)
                for t in range(2):
                    m = pe.matmul(pY[:, t, :], ML[:, l - 1, t, :], XX[:, t, 0, :], start=True, stop=True)
                m.then_inc(s_Y, 1)

            def merge(i, p, l):
                pe.wait_ge(s_Ys, 5 * i + l)
                for t in range(2):
                    if l < LEVELS:
                        pe.matmul(pX[:, t, 0, :], XX[:, t, 1, :], Ys[:, t, :], start=True, stop=True)
                    m = pe.matmul(pX[:, t, 1, :], Ys[:, t, :], XX[:, t, 1, :], start=True, stop=True)
                m.then_inc(s_pX, 1)

            def nv(i, p, fronts):
                pe.wait_ge(s_X, 6 * i + 6)
                pe.wait_ge(s_g, fronts)
                pe.wait_ge(s_wa, fronts)
                for t in range(2):
                    m = pe.matmul(pN[:, t, :], PM[:, p, t, 256:384], V[:, p, t, :], start=True, stop=True)
                m.then_inc(s_pN, 1)

            def wu(i, p):
                pe.wait_ge(s_QN, i + 1)
                pe.wait_ge(s_qn, i + 1)
                wait(pe, s_Z, 4 * i + 1)
                for t in range(2):
                    m = pe.matmul(pWU[:, t, :], XT[:, p, t, :], QN[:, p, t, :], start=True, stop=True)
                m.then_inc(s_pWU, 1)

            def rg(i, p, fronts):
                pe.wait_ge(s_WU, i + 1)
                pe.wait_ge(s_hid, fronts)
                for t in range(2):
                    pe.matmul(pR[:, t * 128:t * 128 + 128], WU[:, t, 0:D], PM[:, p, t, 128:256], start=True, stop=True)
                for t in range(2):
                    m = pe.matmul(pG[:, 2 * t:2 * t + 2, :], WU[:, t, 0:D], Bh[:, p, t], start=True, stop=True)
                m.then_inc(s_pRG, 1)

            def out_tile(i, p, t, fronts):
                if t == 0:
                    pe.wait_ge(s_RG, i + 1)
                    pe.wait_ge(s_exp, fronts)
                    wait(pe, s_O, i)
                pe.matmul(pO[:, t, :], PM[:, p, t, 384:512], V[:, p, t, :], start=True, stop=False, skip_group_check=True)
                pe.matmul(pO[:, t, :], PM[:, p, t, 128:256], WU[:, t, D:128], start=False, stop=False, skip_group_check=True)
                for n in (2 * t, 2 * t + 1):
                    r = slice((n % 2) * CS, (n % 2) * CS + CS)
                    pe.wait_ge(s_Z, 4 * i + n + 1)
                    pe.matmul(pZ[:, n, :], Kh[:, p, t, n % 2, :], V[:, p, t, :], start=True, stop=False)
                    pe.matmul(pZ[:, n, :], Bh[:, p, t, n % 2, :], WU[:, t, D:128], start=False, stop=False)
                    pe.matmul(pZ[:, n, :], GT[:, n, :], Z[:, (n - 1) % 4, :], start=False, stop=True).then_inc(s_pZ, 1)
                    m = pe.matmul(pO[r, t, :], RpT[:, n * CS:n * CS + CS], Z[:, (n - 1) % 4, :], start=False, stop=True,
                                  skip_group_check=True)
                    if n == 0:
                        m.then_inc(s_pO0, 1)
                if t == 1:
                    m.then_inc(s_pO, 1)

            def step(i, p, front=True, inv=True, state=True):
                f, s = (i + 1, 1 - p), (i - 1, 1 - p)
                fronts = i + 2 if front else NIT
                if front: hidden(*f)
                if inv: turn(i, p)
                if state: nv(*s, min(i + 1, NIT) if isinstance(i, int) else i + 1)
                if inv: products(i, p)
                if front: lora(*f)
                if state: wu(*s)
                if inv: inner(i, p, 1)
                if state: rg(*s, fronts)
                if inv: merge(i, p, 1)
                if front: cumulate(*f)
                if inv: inner(i, p, 2)
                if inv: merge(i, p, 2)
                if state: out_tile(*s, 0, fronts)
                if inv: inner(i, p, 3)
                if inv: merge(i, p, 3)
                if state: out_tile(*s, 1, fronts)
                if inv:
                    inner(i, p, 4)
                    merge(i, p, 4)
                    inner(i, p, 5)
                    merge(i, p, 5)

            run(pe, step)

        @block.scalar
        def _(act):
            act.preload_act_table(ACT.Exp)

            def hidden(i, p):
                act.wait_ge(s_hp, i + 1)
                wait(act, s_wp, i)
                act.activation(hid[0:D, :], pH[0:D, 0:256], ACT.Tanh)
                act.activation(hid[D:128, :], pH[D:128, 0:256], ACT.Copy)
                act.activation(gh[:, :], pH[:, 256:512], ACT.Tanh, scale=0.5).then_inc(s_hid, 1)

            def values(i, p):
                wait(act, s_O, i - 1)
                act.activation(V[:, p], rkv[:, bass.ds(2 * i, 2), 2 * D:3 * D], ACT.Copy).then_inc(s_V, 1)

            def tanh(i, p):
                act.wait_ge(s_wa, i + 1)
                wait(act, s_lw, i)
                act.activation(wa[:, :, :], wa[:, :, :], ACT.Tanh, scale=0.5).then_inc(s_th, 1)

            def exps(i, p):
                act.wait_ge(s_ex, i + 1)
                wait(act, s_el, i)
                wait(act, s_qn, i)
                wait(act, s_RG, i - 1)
                act.activation(eP[:, :, :], pC[:, :, 0:D], ACT.Exp)
                act.activation(eN[:, :, :], pC[:, :, 0:D], ACT.Exp, scale=-1.0)
                act.activation(eS[:, :, :], pC[:, :, D:128], ACT.Exp)
                act.activation(eX[:, :, :], ex[:, :, :], ACT.Exp)
                act.activation(DC[:, p, :], pD, ACT.Exp).then_inc(s_exp, 1)

            def turned(i, p):
                act.wait_ge(s_T, i + 1)
                wait(act, s_RG, i - 1)
                for t in range(2):
                    m = act.activation(FT[:, p, t, :], pT[0][t * D:t * D + D, :], ACT.Copy)
                m.then_inc(s_FT, 1)

            def inner(i, p, l):
                act.wait_ge(s_Y, 5 * i + l)
                act.activation(Ys[:, :, :], pY[:, :, :], ACT.Copy).then_inc(s_Ys, 1)

            def nv(i, p):
                act.wait_ge(s_pN, i + 1)
                act.activation(QN[:, p, :, D:128], pN[:, :, :], ACT.Copy).then_inc(s_QN, 1)

            def wu(i, p):
                act.wait_ge(s_pWU, i + 1)
                wait(act, s_O, i)
                act.activation(WU[:, :, :], pWU[:, :, :], ACT.Copy, scale=-1.0).then_inc(s_WU, 1)

            def store(i, p):
                act.wait_ge(s_pO, i + 1)
                act.activation(rkv[:, bass.ds(2 * i, 2), 0:D], pO[:, :, :], ACT.Copy).then_inc(s_O, 1)

            def step(i, p, front=True, inv=True, state=True):
                f, s = (i + 1, 1 - p), (i - 1, 1 - p)
                if front: hidden(*f)
                if inv: turned(i, p)
                if state: nv(*s)
                if state: wu(*s)
                if front: tanh(*f)
                if inv: inner(i, p, 1)
                if front: exps(*f)
                if inv: inner(i, p, 2)
                if inv: inner(i, p, 3)
                if state: store(*s)
                if front: values(*f)
                if inv: inner(i, p, 4)
                if inv: inner(i, p, 5)

            run(act, step)

        @block.gpsimd
        def _(pool):
            def step(i, p, front=True, inv=True, state=True):
                if inv:
                    pool.wait_ge(s_mask, i + 1)
                    wait(pool, s_X, 6 * i)
                    for l in range(LEVELS):
                        m = pool.tensor_tensor(ML[:, l], PM[:, p, :, 0:128], rep(c["lev"][:, l * 128:l * 128 + 128], 2), ALU.mult)
                    m.then_inc(s_ML, 1)
                if front:
                    f, q = i + 1, 1 - p
                    pool.wait_ge(s_exp, f + 1)
                    wait(pool, s_pWU, f - 1)
                    pool.tensor_tensor(QN[:, q, :, 0:D], kn[:, :, :], eX[:, :, :], ALU.mult).then_inc(s_qn, 1)
            run(pool, step)

        @block.vector
        def _(dve):
            dve.memset(Z[:, 3, :], 0.0).then_inc(s_Z, 1)
            for n in range(2):
                r = slice(CS - n * CS, 2 * CS - n * CS)
                dve.memset(Bh[r, :, :, n, :], 0.0)
                dve.memset(Kh[r, :, :, n, :], 0.0)
            TL = 8

            def gate(i, p):
                dve.wait_ge(s_hid, i + 1)
                dve.tensor_scalar(gh[:, :], gh[:, :], 0.5, 0.5, ALU.mult, ALU.add).then_inc(s_gs, 1)

            def lora(i, p):
                dve.wait_ge(s_wp, i + 1)
                dve.tensor_tensor(wa[:, :, :], pW[:, :, 0:128], rep(w["bwa"][:, :], 2), ALU.add).then_inc(s_wa, 1)

                dve.tensor_copy(gate_[:, bass.ds(2 * i, 2), :], pW[:, :, 128:192]).then_inc(s_g, 1)

            def bonus(i, p):
                dve.wait_ge(s_V, i + 1)
                dve.tensor_tensor(rkv[:, bass.ds(2 * i, 2), D:2 * D], V[:, p], bc(rs[:, :], D), ALU.mult)

            def decay(i, p):
                dve.wait_ge(s_th, i + 1)
                dve.tensor_scalar(lw[:, :, :], wa[:, :, 0:D], 0.5 * DECAY, 0.5 * DECAY, ALU.mult, ALU.add)
                dve.tensor_scalar(a_[:, :, :], wa[:, :, D:128], 0.5, 0.5, ALU.mult, ALU.add).then_inc(s_lw, 1)

            def tokens(i, p):
                link = linker(dve, s_dve, i * TL)
                r, k = rkv[:, bass.ds(2 * i, 2), 0:D], rkv[:, bass.ds(2 * i, 2), D:2 * D]
                wait(dve, s_qn, i)
                dve.wait_ge(s_lw, i + 1)
                link(dve.tensor_tensor(kn[:, :, :], k, rep(w["k_k"][:, :], 2), ALU.mult))
                link(dve.tensor_tensor(kn[:, :, :], kn[:, :, :], bc(rn[:, bass.ds(2 * i, 2)], D), ALU.mult))
                link(dve.tensor_tensor(bt[:, :, :], kn[:, :, :], a_[:, :, :], ALU.mult))
                link(dve.scalar_tensor_tensor(out=kp[:, :, :], in0=a_[:, :, :], scalar=-1.0, in1=rep(w["k_a"][:, :], 2),
                                              op0=ALU.add, op1=ALU.mult))
                link(dve.scalar_tensor_tensor(out=kp[:, :, :], in0=kp[:, :, :], scalar=1.0, in1=k, op0=ALU.add, op1=ALU.mult))
                link(dve.tensor_tensor(rk[:, :, :], r, rep(w["r_k"][:, :], 2), ALU.mult))
                link(dve.tensor_tensor(rk[:, :, :], rk[:, :, :], kp[:, :, :], ALU.mult))
                link(dve.tensor_reduce(rs[:, :], rk[:, :, :], AX.X, ALU.add))
                dve.wait_ge(s_cum, i + 1)
                dve.tensor_tensor(ex[:, :, :], pC[:, :, 0:D], lw[:, :, :], ALU.subtract).then_inc(s_ex, 1)
                assert link.count[0] == TL

            def scale(i, p):
                dve.wait_ge(s_exp, i + 1)
                wait(dve, s_O, i - 1)
                wait(dve, s_T, i)
                dve.tensor_tensor(RBK[:, 0], kn[:, :, :], eX[:, :, :], ALU.mult)
                dve.tensor_tensor(RBK[:, 1], rkv[:, bass.ds(2 * i, 2), 0:D], eP[:, :, :], ALU.mult)
                dve.tensor_tensor(RBK[:, 2], bt[:, :, :], eN[:, :, :], ALU.mult)
                dve.tensor_tensor(RBK[:, 3], kp[:, :, :], eN[:, :, :], ALU.mult)
                for n in range(2):
                    r = slice(n * CS, n * CS + CS)
                    dve.tensor_tensor(Bh[r, p, :, n, :], bt[r, :, :], eS[r, :, :], ALU.mult)
                    m = dve.tensor_tensor(Kh[r, p, :, n, :], kp[r, :, :], eS[r, :, :], ALU.mult)
                m.then_inc(s_el, 1)

            def mask(i, p):
                dve.wait_ge(s_prod, i + 1)
                wait(dve, s_O, i - 1)
                for t in range(2):
                    m = dve.tensor_tensor(PM[:, p, t, :], pT[t][:, :], c["mask"][:, :], ALU.mult)
                m.then_inc(s_mask, 1)
                dve.tensor_tensor(XX[:, :, 0, :], pL[:, :, :], rep(c["neg0"][:, 0:128], 2), ALU.mult).then_inc(s_xl, 1)
                dve.wait_ge(s_mask, i + 1)
                dve.tensor_tensor(XX[:, :, 1, :], PM[:, p, :, 0:128], rep(c["neg0"][:, 128:256], 2), ALU.mult).then_inc(s_xw, 1)
                dve.wait_ge(s_xw, i + 1)
                eye4 = c["eye"][:, :].rearrange("p (a b c) -> p a b c", a=1, b=1).broadcast_to([128, 2, 2, 128])
                dve.tensor_tensor(XX[:, :, :, :], XX[:, :, :, :], eye4, ALU.add).then_inc(s_X, 1)

            def merged(i, p, l):
                dve.wait_ge(s_pX, 5 * i + l)
                if l < LEVELS:
                    dve.tensor_tensor(XX[:, :, :, :], XX[:, :, :, :], pX[:, :, :, :], ALU.subtract).then_inc(s_X, 1)
                else:
                    dve.tensor_tensor(XT[:, p], XX[:, :, 1, :], pX[:, :, 1, :], ALU.subtract).then_inc(s_X, 1)

            def rg(i, p):
                dve.wait_ge(s_exp, i + 1)
                wait(dve, s_pO, i)
                dve.tensor_tensor(GT[:, :, :], rep(c["eye"][0:D, 0:D], 4), bc(DC[:, p, :], D), ALU.mult).then_inc(s_dI, 1)
                dve.wait_ge(s_pRG, i + 1)
                dve.tensor_tensor(RpT[:, :].rearrange("p (t n) -> p t n", t=2), pR.rearrange("p (t n) -> p t n", t=2),
                                  FT[:, p, :, 128:256], ALU.add)
                dve.wait_ge(s_dI, i + 1)
                dve.tensor_tensor(GT[:, :, :], pG, GT[:, :, :], ALU.add).then_inc(s_RG, 1)

            def new_state(i, p, n):
                dve.wait_ge(s_pZ, 4 * i + n + 1)
                if n == 3:
                    dve.wait_ge(s_pO0, i + 1)
                dve.tensor_scalar(Z[:, n, :], pZ[:, n, :], c["keep"][:, bass.ds(4 * i + n, 1)], None, ALU.mult).then_inc(s_Z, 1)

            def step(i, p, front=True, inv=True, state=True):
                f, s = (i + 1, 1 - p), (i - 1, 1 - p)
                if front: gate(*f)
                if inv: mask(i, p)
                if front: lora(*f)
                if state: rg(*s)
                if front: decay(*f)
                if inv: merged(i, p, 1)
                if front: tokens(*f)
                if inv: merged(i, p, 2)
                if state:
                    new_state(*s, 0)
                    new_state(*s, 1)
                if inv: merged(i, p, 3)
                if state:
                    new_state(*s, 2)
                    new_state(*s, 3)
                if inv: merged(i, p, 4)
                if front:
                    bonus(*f)
                    scale(*f)
                if inv: merged(i, p, 5)

            run(dve, step)


def outputs(nc, w, h, hout, rkv, gate_, eye):
    with ExitStack() as ctx:
        sb = lambda name, shape, dt=F32: ctx.enter_context(nc.sbuf_tensor(name, shape, dt))
        sem = lambda name: ctx.enter_context(semaphore(nc, name))
        hin = sb("O_hin", [128, 2, GRP, D])
        xc = sb("O_xc", [128, 2, GRP, D])
        sq = sb("O_sq", [128, GRP, D])
        st = sb("O_st", [128, 4, GRP])
        oT = sb("O_oT", [D, 2, QB])
        ho = sb("O_ho", [128, 2, GRP, D])
        pT = ctx.enter_context(nc.psum_tensor("O_pT", [128, 2, 512], F32))
        pO = ctx.enter_context(nc.psum_tensor("O_pO", [128, 2, 512], F32))
        s_in = [sem(f"O_h_in{k}") for k in range(2)]
        s_st = [sem(f"O_stored{k}") for k in range(2)]
        s_link, s_var, s_sqrt, s_x, s_T, s_ev, s_p, s_out = (sem("O_" + x) for x in (
            "step", "var", "root", "gated", "turned", "turned_copied", "projected", "summed"))
        hv = h.rearrange("(g j p) c -> g p j c", p=128, j=GRP)
        ov = hout.rearrange("(g j p) c -> g p j c", p=128, j=GRP)
        block = ctx.enter_context(nc.Block())

        @block.sync
        def _(sp):
            for k in range(2):
                sp.dma_start(hin[:, k], hv[k]).then_inc(s_in[k], 16)
            with sp.Fori(0, NG // 2 - 1) as gg:
                for k in range(2):
                    sp.wait_ge(s_out, 2 * gg + k + 1)
                    sp.dma_start(hin[:, k], hv[2 * gg + 2 + k]).then_inc(s_in[k], 16)
                    sp.dma_start(ov[2 * gg + k], ho[:, k]).then_inc(s_st[k], 16)
            for k in range(2):
                sp.wait_ge(s_out, NG - 2 + k + 1)
                sp.dma_start(ov[NG - 2 + k], ho[:, k]).then_inc(s_st[k], 16)
            for k in range(2):
                sp.wait_ge(s_st[k], 16 * (NG // 2) + 16)

        LINKS = 10

        @block.vector
        def _(dve):
            for k in range(2):
                dve.sem_inc(s_st[k], 16)

            def finish(g, gg, k):
                dve.wait_ge(s_p, g + 1)
                dve.wait_ge(s_in[k], 16 * gg + 16)
                dve.wait_ge(s_st[k], 16 * gg + 16)
                dve.tensor_tensor(ho[:, k], hin[:, k], pO[:, k, 0:GRP * D].rearrange("p (j c) -> p j c", c=D),
                                  ALU.add).then_inc(s_out, 1)

            with dve.Fori(0, NG // 2) as gg:
                for k in range(2):
                    g = 2 * gg + k
                    js = bass.ds(g * GRP, GRP)
                    link = linker(dve, s_link, g * LINKS)
                    S = lambda i: st[:, i, :]
                    dve.wait_ge(s_T, g + 1)
                    link(dve.tensor_reduce(S(0), rkv[:, js, 0:D], AX.X, ALU.add))
                    link(dve.tensor_scalar(S(1), S(0), 1.0 / D, None, ALU.mult))
                    link(dve.tensor_tensor(xc[:, k], rkv[:, js, 0:D], bc(S(1), D), ALU.subtract))
                    link(dve.tensor_tensor(sq[:, :, :], xc[:, k], xc[:, k], ALU.mult))
                    link(dve.tensor_reduce(S(2), sq[:, :, :], AX.X, ALU.add))
                    link(dve.tensor_scalar(S(2), S(2), 1.0 / D, GN_EPS, ALU.mult, ALU.add))
                    dve.reciprocal(S(3), S(2)).then_inc(s_var, 1)
                    dve.wait_ge(s_sqrt, g + 1)
                    link(dve.tensor_tensor(xc[:, k], xc[:, k], bc(S(3), D), ALU.mult))
                    link(dve.tensor_tensor(xc[:, k], xc[:, k], rep(w["gn_w"][:, :], GRP), ALU.mult))
                    link(dve.tensor_tensor(xc[:, k], xc[:, k], rep(w["gn_b"][:, :], GRP), ALU.add))
                    link(dve.tensor_tensor(xc[:, k], xc[:, k], rkv[:, js, D:2 * D], ALU.add))
                    dve.tensor_tensor(xc[:, k], xc[:, k], gate_[:, js, :], ALU.mult).then_inc(s_x, 1)
                    assert link.count[0] == LINKS
                    finish(g, gg, k)

        @block.scalar
        def _(act):
            act.preload_act_table(ACT.Sqrt)
            with act.Fori(0, NG // 2) as gg:
                for k in range(2):
                    g = 2 * gg + k
                    act.wait_ge(s_var, g + 1)
                    act.activation(st[:, 3, :], st[:, 3, :], ACT.Sqrt).then_inc(s_sqrt, 1)
                    act.wait_ge(s_T, g + 3)
                    pairs = lambda x: oT[:, k, 0:768].rearrange("p (j x n) -> p x j n", x=2, n=128)[:, x]
                    act.activation(pairs(0), pT[0:D, k, 0:384].rearrange("p (j n) -> p j n", n=128), ACT.Copy)
                    act.activation(pairs(1), pT[D:128, k, 0:384].rearrange("p (j n) -> p j n", n=128), ACT.Copy)
                    act.activation(oT[:, k, 768:896], pT[0:D, k, 384:512], ACT.Copy).then_inc(s_ev, 1)

        @block.tensor
        def _(pe):
            pe.sem_inc(s_T, 2)
            with pe.Fori(0, NG // 2) as gg:
                for k in range(2):
                    g = 2 * gg + k
                    pe.wait_ge(s_x, g + 1)
                    for j in range(GRP // 2):
                        pe.transpose(pT[:, k, j * 128:j * 128 + 128], xc[:, k, 2 * j:2 * j + 2, :], eye[:, :])
                    m = pe.transpose(pT[0:D, k, 384:512], xc[:, k, GRP - 1, :], eye[:, :])
                    m.then_inc(s_T, 1)
                    pe.wait_ge(s_ev, g + 1)
                    for j in range(GRP):
                        m = pe.matmul(pO[:, k, j * D:j * D + D], oT[:, k, j * 128:j * 128 + 128], w["Wo"][:, :], start=True, stop=True)
                    m.then_inc(s_p, 1)


def weights(nc, ctx, ins, cst):
    sb = lambda name, shape, dt=F32: ctx.enter_context(nc.sbuf_tensor(name, shape, dt))
    w = {"rkv": sb("W_rkv", [128, 192]), "Awa": sb("W_Awa", [128, 128]), "Ag": sb("W_Ag", [128, 128]),
         "Bwa": sb("W_Bwa", [128, 128]), "Bg": sb("W_Bg", [128, D]), "bwa": sb("W_bwa", [128, 128]),
         "Wo": sb("W_Wo", [D, D])}
    for n in ("k_k", "k_a", "r_k", "gn_w", "gn_b"):
        w[n] = sb("W_" + n, [128, D])
    mix = sb("W_mix", [128, 6])
    shapes = {"tri": [128, 256], "ind": [128, 2], "mask": [128, 512], "neg0": [128, 256], "lev": [128, LEVELS * 128],
              "eye": [128, 128], "keep": [D, TOK // CS]}
    c = {k: sb("K_" + k, v) for k, v in shapes.items()}
    with semaphore(nc, "W_in") as s_in, semaphore(nc, "W_zero") as s_z, semaphore(nc, "W_mixed") as s_m, nc.Block() as block:
        n = [0]

        @block.gpsimd
        def _(pool):
            pool.memset(w["Bwa"][:, :], 0.0).then_inc(s_z, 1)

        @block.sync
        def _(sp):
            def load(dst, src, slow=False):
                n[0] += 16
                sp.dma_start(dst, src, allow_slow_non_contiguous=slow).then_inc(s_in, 16)
            for k in c:
                load(c[k][:, :], cst[k])
            row = lambda a: a.rearrange("(a c) -> a c", a=1).broadcast_to([128, D])
            for p in (0, D):
                load(mix[p:p + D, :], ins["x_mix"].rearrange("i d -> d i"), True)
                for j, k in enumerate(("W_r", "W_k", "W_v")):
                    load(w["rkv"][p:p + D, j * D:j * D + D], ins[k])
                load(w["Awa"][p:p + D, 0:D], ins["A_w"])
                load(w["Awa"][p:p + D, D:128], ins["A_a"])
                load(w["Ag"][p:p + D, :], ins["A_g"])
            load(w["bwa"][:, 0:D], row(ins["b_w"]))
            load(w["bwa"][:, D:128], row(ins["b_a"]))
            load(w["Bg"][:, :], ins["B_g"])
            load(w["Wo"][:, :], ins["W_o"])
            for k in ("k_k", "k_a", "r_k", "gn_w", "gn_b"):
                load(w[k][:, :], row(ins[k]))
            sp.wait_ge(s_z, 1)
            load(w["Bwa"][0:D, 0:D], ins["B_w"])
            load(w["Bwa"][D:128, D:128], ins["B_a"])
            sp.wait_ge(s_in, n[0])

        @block.vector
        def _(dve):
            dve.wait_ge(s_in, n[0])
            dve.tensor_scalar(mix[0:D, :], mix[0:D, :], -1.0, 1.0, ALU.mult, ALU.add).then_inc(s_m, 1)
            dve.wait_ge(s_m, 1)
            for t, col, m in (("rkv", 0, 0), ("rkv", D, 2), ("rkv", 2 * D, 3), ("Awa", 0, 1), ("Awa", D, 4), ("Ag", 0, 5)):
                v = w[t][:, col:col + (128 if t == "Ag" else D)]
                dve.tensor_scalar(v, v, mix[:, m:m + 1], None, ALU.mult)
    return w, c


def tokenizer(nc, x, W1p, b1, W2p, b2p, W3p, b3, hA):
    with ExitStack() as ctx:
        sb = lambda name, shape, dt=F32: ctx.enter_context(nc.sbuf_tensor(name, shape, dt))
        ps = lambda name, shape, dt=F32: ctx.enter_context(nc.psum_tensor(name, shape, dt))
        sem = lambda name: ctx.enter_context(semaphore(nc, name))
        IMGSZ = PAD * PAD
        xa = sb("A_xa", [128, 2, IMGSZ])
        xb = sb("A_xb", [128, 2, IMGSZ])
        w1 = sb("A_w1", [128, NCH, CH])
        w2 = sb("A_w2", [CH, NCH * 128])
        w3 = sb("A_w3", [128, NCH, CH])
        b1s = sb("A_b1", [CH, 1])
        b2s = sb("A_b2", [128, NCH])
        b3s = sb("A_b3", [SUB, CH])
        h1 = sb("A_h1", [CH, TILE])
        sg = sb("A_sg", [128, NCH, TILE])
        u = sb("A_u", [128, NCH, TILE])
        hst = sb("A_hst", [SUB, 4, CH])
        pc = ps("A_pc", [CH, 512])
        pS = [ps(f"A_pS{q}", [128, 512]) for q in range(NCH)]
        po = ps("A_po", [128, 512])
        s_w = sem("A_weights_in")
        s_zero = sem("A_borders_zero")
        s_x = [sem(f"A_image_in{k}") for k in range(2)]
        s_conv = sem("A_conv")
        s_relu = sem("A_relu")
        s_gate = sem("A_gate_logits")
        s_sig = sem("A_gates")
        s_u = sem("A_gated")
        s_out = sem("A_out")
        s_ev = sem("A_out_copied")
        s_st = sem("A_stored")
        hA_v = hA.rearrange("(t g p) c -> p t g c", g=4, p=SUB)
        block = ctx.enter_context(nc.Block())

        def view(buf, half, K, t, tap):
            v = buf[0:K, half, :].rearrange("p (r c) -> p r c", c=PAD)
            return v[:, bass.ds(tap[0] + t * ROWS, ROWS), tap[1]:tap[1] + IMG]

        def taps(half, t, whole=False):
            for q in range(NCH):
                tap = TAPS[2 * q]
                K = 128 if q < NCH - 1 or whole else CH
                yield q, K, view(xa if q < 3 else xb, half, K, t, tap)

        @block.sync
        def _(sp):
            sp.dma_start(w1[:, :, :], W1p.rearrange("(q p) c -> p q c", p=128)).then_inc(s_w, 16)
            sp.dma_start(b1s[:, :], b1.rearrange("(c a) -> c a", a=1)).then_inc(s_w, 16)
            sp.dma_start(w2[:, :], W2p).then_inc(s_w, 16)
            sp.dma_start(b2s[:, :], b2p.rearrange("(q p) -> p q", p=128), allow_slow_non_contiguous=True).then_inc(s_w, 16)
            sp.dma_start(w3[:, :, :], W3p.rearrange("(q p) c -> p q c", p=128)).then_inc(s_w, 16)
            sp.dma_start(b3s[:, :], b3.rearrange("(a c) -> a c", a=1).broadcast_to([SUB, CH])).then_inc(s_w, 16)
            sp.wait_ge(s_zero, 2)
            def load_image(b):
                for buf, shift in ((xa, 0), (xb, 0), (xa, 1), (xb, PAD)):
                    p0 = 0 if shift == 0 else CH
                    o = PAD + 1 - shift
                    v = buf[p0:p0 + CH, b % 2, o:o + IMG * PAD].rearrange("p (r c) -> p r c", c=PAD)
                    sp.dma_start(v[:, :, 0:IMG], x[b]).then_inc(s_x[b % 2], 16)

            load_image(0)
            load_image(1)
            for b in range(BATCH):
                with sp.Fori(b * NT, b * NT + NT) as n:
                    sp.wait_ge(s_ev, n + 2)
                    sp.dma_start(hA_v[:, n], hst[:, :, :]).then_inc(s_st, 16)
                if b + 2 < BATCH:
                    load_image(b + 2)
            sp.wait_ge(s_st, 16 * BATCH * NT + 16)

        @block.gpsimd
        def _(pool):
            pool.memset(xa[:, :, :], 0.0).then_inc(s_zero, 1)
            pool.memset(xb[:, :, :], 0.0).then_inc(s_zero, 1)

        @block.tensor
        def _(pe):
            pe.wait_ge(s_w, 96)
            pe.sem_inc(s_ev, 1)
            pe.wait_ge(s_zero, 2)

            def conv(half, t):
                for q, K, v in taps(half, t, whole=True):
                    m = pe.matmul(pc[:, 0:TILE], w1[0:K, q, :], v, start=(q == 0), stop=(q == NCH - 1))
                m.then_inc(s_conv, 1)

            def gates(n):
                pe.wait_ge(s_relu, n + 1)
                for q in range(NCH):
                    M = 128 if q < NCH - 1 else CH
                    pe.matmul(pS[q][0:M, 0:TILE], w2[:, q * 128:q * 128 + M], h1[:, :],
                              start=True, stop=True).then_inc(s_gate, 1)

            def out(n):
                pe.wait_ge(s_ev, n + 1)
                pe.wait_ge(s_u, NCH * n + NCH)
                for g in range(4):
                    for q in range(NCH):
                        K = 128 if q < NCH - 1 else CH
                        m = pe.matmul(po[0:SUB, g * CH:(g + 1) * CH], u[0:K, q, g * SUB:(g + 1) * SUB],
                                      w3[0:K, q, :], start=(q == 0), stop=(q == NCH - 1))
                m.then_inc(s_out, 1)

            for b in range(BATCH):
                pe.wait_ge(s_x[b % 2], 64 * (b // 2 + 1))
                conv(b % 2, 0)
                with pe.Fori(0, NT - 1) as t:
                    gates(t + b * NT)
                    conv(b % 2, t + 1)
                    out(t + b * NT)
                gates(b * NT + NT - 1)
                out(b * NT + NT - 1)

        @block.scalar
        def _(act):
            act.wait_ge(s_w, 96)
            act.preload_act_table(ACT.Sigmoid)
            with act.Fori(0, BATCH * NT) as n:
                act.wait_ge(s_conv, n + 1)
                act.activation(h1[:, :], pc[:, 0:TILE], ACT.Relu, bias=b1s[:, 0:1]).then_inc(s_relu, 1)
                for q in range(NCH):
                    M = 128 if q < NCH - 1 else CH
                    act.wait_ge(s_gate, n * NCH + q + 1)
                    act.activation(sg[0:M, q, :], pS[q][0:M, 0:TILE], ACT.Sigmoid,
                                   bias=b2s[0:M, q:q + 1]).then_inc(s_sig, 1)

        @block.vector
        def _(dve):
            dve.wait_ge(s_w, 96)
            dve.sem_inc(s_st, 16)
            for b in range(BATCH):
                dve.wait_ge(s_x[b % 2], 64 * (b // 2 + 1))
                with dve.Fori(0, NT) as t:
                    n = t + b * NT
                    for q, K, v in taps(b % 2, t):
                        dve.wait_ge(s_sig, (t + b * NT) * NCH + q + 1)
                        dve.tensor_tensor(u[0:K, q, :].rearrange("p (r c) -> p r c", c=IMG),
                                          sg[0:K, q, :].rearrange("p (r c) -> p r c", c=IMG),
                                          v, ALU.mult).then_inc(s_u, 1)
                    dve.wait_ge(s_out, n + 1)
                    dve.wait_ge(s_st, n * 16 + 16)
                    dve.tensor_tensor(hst[:, :, :], po[0:SUB, 0:4 * CH].rearrange("p (g c) -> p g c", c=CH),
                                      b3s[:, :].rearrange("p (a c) -> p a c", a=1).broadcast_to([SUB, 4, CH]), ALU.add).then_inc(s_ev, 1)


def moe_constants():
    e = np.arange(EX)
    tok = np.arange(NTT)[None] * 128 + np.arange(128)[:, None]
    s, t = np.meshgrid(np.arange(128), np.arange(128), indexing="ij")
    c = {"less": np.tile((e[None] < e[:, None]).reshape(1, -1), (128, 1)),
         "base": np.tile(e[None] * CAP, (128, 1)),
         "dump": EX * CAP + tok,
         "upto": np.concatenate([s <= t, np.ones((128, 128))], 1)}
    return {k: np.ascontiguousarray(v.astype(np.float32)) for k, v in c.items()}


def layer_norm(nc, pre, h, XT, eye, rows=None):
    with ExitStack() as ctx:
        sb = lambda name, shape, dt=F32: ctx.enter_context(nc.sbuf_tensor(pre + name, shape, dt))
        sem = lambda name: ctx.enter_context(semaphore(nc, pre + name))
        hin = sb("hin", [128, 2, GRP, D])
        xc = sb("xc", [128, 2, GRP, D])
        sq = sb("sq", [128, GRP, D])
        st = sb("st", [128, 2, 4, GRP])
        pT = ctx.enter_context(nc.psum_tensor(pre + "pT", [128, 2, 512], F32))
        s_in = [sem(f"h_in{k}") for k in range(2)]
        s_free, s_link, s_var, s_sqrt, s_x, s_T, s_ev = (sem(x) for x in (
            "h_used", "step", "var", "root", "normed", "transposed", "features"))
        hv = h.rearrange("(g j p) c -> g p j c", p=128, j=GRP)
        block = ctx.enter_context(nc.Block())

        @block.sync
        def _(sp):
            for k in range(2):
                sp.dma_start(hin[:, k], hv[k]).then_inc(s_in[k], 16)
            with sp.Fori(0, NG // 2 - 1) as g:
                for k in range(2):
                    sp.wait_ge(s_free, 2 * g + k + 1)
                    sp.dma_start(hin[:, k], hv[2 * g + 2 + k]).then_inc(s_in[k], 16)

        LINKS = 6

        @block.vector
        def _(dve):
            with dve.Fori(0, NG // 2) as gg:
                for k in range(2):
                    g = 2 * gg + k
                    link = linker(dve, s_link, g * LINKS)
                    S = lambda i: st[:, k, i, :]
                    dve.wait_ge(s_in[k], 16 * gg + 16)
                    dve.wait_ge(s_T, g + 1)
                    link(dve.tensor_reduce(S(0), hin[:, k], AX.X, ALU.add))
                    link(dve.tensor_scalar(S(1), S(0), 1.0 / D, None, ALU.mult))
                    link(dve.tensor_tensor(xc[:, k], hin[:, k], bc(S(1), D), ALU.subtract))
                    dve.sem_inc(s_free, 1)
                    link(dve.tensor_tensor(sq[:, :, :], xc[:, k], xc[:, k], ALU.mult))
                    link(dve.tensor_reduce(S(2), sq[:, :, :], AX.X, ALU.add))
                    link(dve.tensor_scalar(S(2), S(2), 1.0 / D, LN_EPS, ALU.mult, ALU.add))
                    dve.reciprocal(S(3), S(2)).then_inc(s_var, 1)
                    dve.wait_ge(s_sqrt, g + 1)
                    if rows is not None:
                        dve.tensor_tensor(rows[:, bass.ds(g * GRP, GRP), :], xc[:, k], bc(S(3), D), ALU.mult)
                    dve.tensor_tensor(xc[:, k], xc[:, k], bc(S(3), D), ALU.mult).then_inc(s_x, 1)
                    assert link.count[0] == LINKS

        @block.tensor
        def _(pe):
            pe.sem_inc(s_T, 2)
            with pe.Fori(0, NG // 2) as gg:
                for k in range(2):
                    g = 2 * gg + k
                    pe.wait_ge(s_x, g + 1)
                    pe.wait_ge(s_ev, g + 1)
                    for j in range(GRP // 2):
                        pe.transpose(pT[:, k, j * 128:j * 128 + 128], xc[:, k, 2 * j:2 * j + 2, :], eye[:, :])
                    pe.transpose(pT[0:D, k, 384:512], xc[:, k, GRP - 1, :], eye[:, :]).then_inc(s_T, 1)

        @block.scalar
        def _(act):
            act.preload_act_table(ACT.Sqrt)
            act.sem_inc(s_ev, 2)
            with act.Fori(0, NG // 2) as gg:
                for k in range(2):
                    g = 2 * gg + k
                    act.wait_ge(s_var, g + 1)
                    act.activation(st[:, k, 3, :], st[:, k, 3, :], ACT.Sqrt).then_inc(s_sqrt, 1)
                    act.wait_ge(s_T, g + 3)
                    z = XT[0:D, bass.ds(g * QB, QB)]
                    pairs = lambda x: z[:, 0:768].rearrange("p (j x n) -> p x j n", x=2, n=128)[:, x]
                    act.activation(pairs(0), pT[0:D, k, 0:384].rearrange("p (j n) -> p j n", n=128), ACT.Copy)
                    act.activation(pairs(1), pT[D:128, k, 0:384].rearrange("p (j n) -> p j n", n=128), ACT.Copy)
                    act.activation(z[:, 768:896], pT[0:D, k, 384:512], ACT.Copy).then_inc(s_ev, 1)


def gating(nc, pre, XT, wg, gb, less, top, cw, chosen=None):
    with ExitStack() as ctx:
        sb = lambda name, shape, dt=F32: ctx.enter_context(nc.sbuf_tensor(pre + name, shape, dt))
        sem = lambda name: ctx.enter_context(semaphore(nc, pre + name))
        xs = sb("xs", [D, 2, QB])
        lg = sb("lg", [128, 2, GRP, EX])
        st = sb("st", [128, 3, GRP])
        gt = sb("gt", [128, GRP, EX, EX])
        eq = sb("eq", [128, GRP, EX, EX])
        sel = sb("sel", [128, GRP, EX])
        pL = ctx.enter_context(nc.psum_tensor(pre + "pL", [128, 2, 512], F32))
        s_xs, s_p, s_lg, s_e, s_link = (sem(x) for x in ("moved", "logits", "shifted", "exp", "step"))
        block = ctx.enter_context(nc.Block())

        @block.scalar
        def _(act):
            act.preload_act_table(ACT.Exp)
            with act.Fori(0, NG // 2) as gg:
                for k in range(2):
                    g = 2 * gg + k
                    act.wait_ge(s_p, g + 1)
                    act.activation(xs[:, k, :], XT[0:D, bass.ds(g * QB, QB)], ACT.Copy).then_inc(s_xs, 1)
                    act.wait_ge(s_lg, g + 1)
                    act.activation(lg[:, k], lg[:, k], ACT.Exp).then_inc(s_e, 1)

        @block.tensor
        def _(pe):
            pe.sem_inc(s_p, 2)
            with pe.Fori(0, NG // 2) as gg:
                for k in range(2):
                    g = 2 * gg + k
                    pe.wait_ge(s_xs, g + 1)
                    for j in range(GRP):
                        m = pe.matmul(pL[:, k, j * EX:j * EX + EX], xs[:, k, j * 128:j * 128 + 128], wg, start=True, stop=True)
                    m.then_inc(s_p, 1)

        LINKS = 12

        @block.vector
        def _(dve):
            with dve.Fori(0, NG // 2) as gg:
                for k in range(2):
                    g = 2 * gg + k
                    link = linker(dve, s_link, g * LINKS)
                    js = bass.ds(g * GRP, GRP)
                    P = lg[:, k]
                    dve.wait_ge(s_p, g + 3)
                    link(dve.tensor_tensor(P, pL[:, k, 0:GRP * EX].rearrange("p (j e) -> p j e", e=EX), rep(gb, GRP), ALU.add))
                    link(dve.tensor_reduce(st[:, 0, :], P, AX.X, ALU.max))
                    dve.tensor_tensor(P, P, bc(st[:, 0, :], EX), ALU.subtract).then_inc(s_lg, 1)
                    dve.wait_ge(s_e, g + 1)
                    link(dve.tensor_reduce(st[:, 1, :], P, AX.X, ALU.add))
                    link(dve.reciprocal(st[:, 2, :], st[:, 1, :]))
                    link(dve.tensor_tensor(P, P, bc(st[:, 2, :], EX), ALU.mult))
                    own = P.rearrange("p j (e a) -> p j e a", a=1).broadcast_to([128, GRP, EX, EX])
                    other = P.rearrange("p j (a e) -> p j a e", a=1).broadcast_to([128, GRP, EX, EX])
                    lower = less.rearrange("p (a e f) -> p a e f", a=1, e=EX).broadcast_to([128, GRP, EX, EX])
                    link(dve.tensor_tensor(gt[:, :, :, :], other, own, ALU.is_gt))
                    link(dve.tensor_tensor(eq[:, :, :, :], other, own, ALU.is_equal))
                    link(dve.tensor_tensor(eq[:, :, :, :], eq[:, :, :, :], lower, ALU.mult))
                    link(dve.tensor_tensor(gt[:, :, :, :], gt[:, :, :, :], eq[:, :, :, :], ALU.add))
                    link(dve.tensor_reduce(sel[:, :, :], gt[:, :, :, :], AX.X, ALU.add))
                    link(dve.tensor_scalar(sel[:, :, :], sel[:, :, :], float(top), None, ALU.is_lt))
                    if chosen is not None:
                        dve.tensor_copy(chosen[:, js, :], sel[:, :, :])
                    link(dve.tensor_tensor(cw[:, js, :], P, sel[:, :, :], ALU.mult))
                    assert link.count[0] == LINKS


def experts_dense(nc, h, hout, XT, cw, w, eye):
    with ExitStack() as ctx:
        sb = lambda name, shape, dt=F32: ctx.enter_context(nc.sbuf_tensor("C_" + name, shape, dt))
        ps = lambda name, shape, dt=F32: ctx.enter_context(nc.psum_tensor("C_" + name, shape, dt))
        sem = lambda name: ctx.enter_context(semaphore(nc, "C_" + name))
        G = sb("G", [128, 2, EX, QB])
        cs = sb("cs", [128, 2, GRP, EX])
        cT = sb("cT", [GRP * EX, 2, 128])
        pr = sb("pr", [128, 2, EX, D])
        acc = sb("acc", [128, GRP, D])
        hin = sb("hin", [128, 2, GRP, D])
        ho = sb("ho", [128, 2, GRP, D])
        pH = ps("pH", [128, 4, 512])
        pY = ps("pY", [128, 2, 512])
        pB = ps("pB", [128, 512])
        pC = ps("pC", [GRP * EX, 512])
        s_in = [sem(f"h_in{k}") for k in range(2)]
        s_st = [sem(f"stored{k}") for k in range(2)]
        s_h, s_G, s_y, s_pr, s_red, s_cs, s_cT, s_cTs, s_b, s_acc, s_out = (sem(x) for x in (
            "hidden", "gelu", "products", "weighted", "summed", "weights_moved", "weights_turned", "weights_copied",
            "bias", "accumulated", "out"))
        hv = h.rearrange("(g j p) c -> g p j c", p=128, j=GRP)
        ov = hout.rearrange("(g j p) c -> g p j c", p=128, j=GRP)
        block = ctx.enter_context(nc.Block())

        @block.sync
        def _(sp):
            for k in range(2):
                sp.dma_start(hin[:, k], hv[k]).then_inc(s_in[k], 16)
            with sp.Fori(0, NG // 2 - 1) as gg:
                for k in range(2):
                    sp.wait_ge(s_out, 2 * gg + k + 1)
                    sp.dma_start(hin[:, k], hv[2 * gg + 2 + k]).then_inc(s_in[k], 16)
                    sp.dma_start(ov[2 * gg + k], ho[:, k]).then_inc(s_st[k], 16)
            for k in range(2):
                sp.wait_ge(s_out, NG - 2 + k + 1)
                sp.dma_start(ov[NG - 2 + k], ho[:, k]).then_inc(s_st[k], 16)
            for k in range(2):
                sp.wait_ge(s_st[k], 16 * (NG // 2) + 16)

        @block.tensor
        def _(pe):
            pe.sem_inc(s_G, 4)
            pe.sem_inc(s_pr, 2)

            def hidden(g, k, e):
                for half in range(2):
                    u = g * (2 * EX) + 2 * e + half
                    pe.wait_ge(s_G, u + 1)
                    pe.matmul(pH[:, (2 * e + half) % 4, 0:QH], w["W1"][:, e, :], XT[:, bass.ds(g * QB + half * QH, QH)],
                              start=True, stop=True).then_inc(s_h, 1)

            def tile(g, k, j):
                if j == 0:
                    pe.wait_ge(s_G, g * (2 * EX) + 2 * EX + 4)
                pe.wait_ge(s_pr, g * GRP + j + 1)
                y = (k + j) % 2
                for e in range(EX):
                    m = pe.matmul(pY[:, y, e * D:e * D + D], G[:, k, e, j * 128:j * 128 + 128], w["W2"][:, e, :],
                                  start=True, stop=True)
                m.then_inc(s_y, 1)

            def turn_weights(g, k):
                pe.wait_ge(s_cs, g + 1)
                if not (isinstance(g, int) and g == 0):
                    pe.wait_ge(s_cTs, g)
                pe.matmul(pC[:, 0:128], cs[:, k].rearrange("p j e -> p (j e)"), eye[:, :], start=True, stop=True).then_inc(s_cT, 1)

            def bias(g, k):
                pe.wait_ge(s_cTs, g + 1)
                if not (isinstance(g, int) and g == 0):
                    pe.wait_ge(s_acc, g)
                pe.matmul(pB[:, 0:GRP * D], cT[:, k, :], w["b2"][:, :], start=True, stop=True).then_inc(s_b, 1)

            def step(g, k, ahead=True, out=True):
                for e in range(EX):
                    if ahead: hidden(g + 1, 1 - k, e)
                    if out and e < GRP: tile(g, k, e)
                    if out and e == GRP - 3: turn_weights(g, k)
                    if out and e == EX - 1: bias(g, k)

            step(-1, 1, out=False)
            with pe.Fori(0, (NG - 2) // 2) as m:
                step(2 * m, 0)
                step(2 * m + 1, 1)
            step(NG - 2, 0)
            step(NG - 1, 1, ahead=False)

        @block.scalar
        def _(act):
            act.preload_act_table(ACT.Gelu)

            def step(g, k, ahead=True, out=True):
                f, q = g + 1, 1 - k
                if ahead and not (isinstance(g, int) and g <= 0):
                    act.wait_ge(s_y, g * GRP)
                for e in range(EX):
                    for half in range(2):
                        if ahead:
                            act.wait_ge(s_h, f * (2 * EX) + 2 * e + half + 1)
                            act.activation(G[:, q, e, half * QH:half * QH + QH], pH[:, (2 * e + half) % 4, 0:QH],
                                           ACT.Gelu, bias=w["b1"][:, e:e + 1]).then_inc(s_G, 1)
                    if out and e == GRP - 1:
                        act.wait_ge(s_cT, g + 1)
                        act.activation(cT[:, k, :], pC[:, 0:128], ACT.Copy).then_inc(s_cTs, 1)

            step(-1, 1, out=False)
            with act.Fori(0, (NG - 2) // 2) as m:
                step(2 * m, 0)
                step(2 * m + 1, 1)
            step(NG - 2, 0)
            step(NG - 1, 1, ahead=False)

        @block.vector
        def _(dve):
            for k in range(2):
                dve.sem_inc(s_st[k], 16)
            with dve.Fori(0, NG // 2) as gg:
                for k in range(2):
                    g = 2 * gg + k
                    dve.wait_ge(s_st[k], 16 * gg + 16)
                    dve.tensor_copy(cs[:, k], cw[:, bass.ds(g * GRP, GRP), :]).then_inc(s_cs, 1)
                    dve.wait_ge(s_cs, g + 1)
                    for j in range(GRP):
                        y = (k + j) % 2
                        dve.wait_ge(s_y, g * GRP + j + 1)
                        cb = cs[:, k, j, :].rearrange("p (e a) -> p e a", a=1).broadcast_to([128, EX, D])
                        dve.tensor_tensor(pr[:, y], pY[:, y, :].rearrange("p (e c) -> p e c", e=EX), cb, ALU.mult).then_inc(s_pr, 1)
                        dve.wait_ge(s_pr, g * GRP + j + 3)
                        dve.tensor_reduce(acc[:, j, :], pr[:, y].rearrange("p e c -> p c e"), AX.X, ALU.add).then_inc(s_red, 1)
                    dve.wait_ge(s_red, g * GRP + GRP)
                    dve.wait_ge(s_b, g + 1)
                    dve.tensor_tensor(acc[:, :, :], acc[:, :, :], pB[:, 0:GRP * D].rearrange("p (j c) -> p j c", c=D),
                                      ALU.add).then_inc(s_acc, 1)
                    dve.wait_ge(s_acc, g + 1)
                    dve.wait_ge(s_in[k], 16 * gg + 16)
                    dve.tensor_tensor(ho[:, k], hin[:, k], acc[:, :, :], ALU.add).then_inc(s_out, 1)


def moe1_weights(nc, ctx, ins, cst):
    sb = lambda name, shape, dt=F32: ctx.enter_context(nc.sbuf_tensor("CW_" + name, shape, dt))
    w = {"gate": sb("gate", [D, EX]), "gb": sb("gb", [128, EX]), "W1": sb("W1", [128, EX, F1]), "b1": sb("b1", [F1, EX]),
         "W2": sb("W2", [F1, EX, D]), "b2": sb("b2", [GRP * EX, GRP * D]), "less": sb("less", [128, EX * EX])}
    n = [0]
    with semaphore(nc, "CW_in") as s_in, semaphore(nc, "CW_zero") as s_z, nc.Block() as block:
        @block.gpsimd
        def _(pool):
            pool.memset(w["W1"][D:128, :, :], 0.0)
            pool.memset(w["b2"][:, :], 0.0).then_inc(s_z, 1)

        @block.sync
        def _(sp):
            def load(dst, src, slow=False):
                n[0] += 16
                sp.dma_start(dst, src, allow_slow_non_contiguous=slow).then_inc(s_in, 16)
            load(w["less"][:, :], cst["less"])
            load(w["gate"][:, :], ins["gate_w"])
            load(w["gb"][:, :], ins["gate_b"].rearrange("(a c) -> a c", a=1).broadcast_to([128, EX]))
            load(w["W1"][0:D, :, :], ins["W1"].rearrange("e d f -> d e f"))
            load(w["b1"][:, :], ins["b1"].rearrange("e f -> f e"), True)
            load(w["W2"][:, :, :], ins["W2"].rearrange("e f d -> f e d"))
            sp.wait_ge(s_z, 1)
            for j in range(GRP):
                load(w["b2"][j * EX:j * EX + EX, j * D:j * D + D], ins["b2"])
            sp.wait_ge(s_in, n[0])
    return w


def slots(nc, c, chosen, cw, dest, src, wt):
    N = NTT * EX
    with ExitStack() as ctx:
        sb = lambda name, shape, dt=F32: ctx.enter_context(nc.sbuf_tensor("S_" + name, shape, dt))
        sem = lambda name: ctx.enter_context(semaphore(nc, "S_" + name))
        cnt = sb("cnt", [128, NTT, EX])
        tot = sb("tot", [128, NTT, EX])
        run_ = sb("run", [128, NTT, EX])
        one = sb("one", [128, NTT])
        T = sb("T", [128, NTT])
        B = sb("B", [128, NTT])
        kept = sb("kept", [128, NTT])
        df = sb("df", [128, NTT])
        sf = sb("sf", [128, NTT])
        pI = ctx.enter_context(nc.psum_tensor("S_pI", [128, 4, 512], F32))
        s_p, s_l = sem("counted"), sem("step")
        block = ctx.enter_context(nc.Block())
        flat = chosen[:, :, :].rearrange("p j e -> p (j e)")

        @block.tensor
        def _(pe):
            for x in range(2):
                for half in range(2):
                    m = pe.matmul(pI[:, 2 * x + half, 0:N // 2], c["upto"][:, x * 128:x * 128 + 128],
                                  flat[:, half * (N // 2):(half + 1) * (N // 2)], start=True, stop=True)
            m.then_inc(s_p, 1)

        @block.vector
        def _(dve):
            link = linker(dve, s_l)
            dve.wait_ge(s_p, 1)
            v = lambda t: t[:, :, :].rearrange("p (x j) e -> p x (j e)", x=2)
            link(dve.tensor_copy(v(cnt), pI[:, 0:2, 0:N // 2]))
            link(dve.tensor_copy(v(tot), pI[:, 2:4, 0:N // 2]))
            link(dve.memset(one[:, :], 1.0))
            for e in range(EX):
                m = dve.tensor_tensor_scan(run_[:, :, e], one[:, :], tot[:, :, e], 0.0, ALU.mult, ALU.add)
            link(m)
            link(dve.tensor_tensor(run_[:, :, :], run_[:, :, :], tot[:, :, :], ALU.subtract))
            link(dve.tensor_tensor(cnt[:, :, :], cnt[:, :, :], run_[:, :, :], ALU.add))
            link(dve.tensor_tensor(cnt[:, :, :], cnt[:, :, :], chosen[:, :, :], ALU.mult))
            link(dve.tensor_reduce(T[:, :], cnt[:, :, :], AX.X, ALU.add))
            link(dve.tensor_tensor(tot[:, :, :], chosen[:, :, :], rep(c["base"][:, :], NTT), ALU.mult))
            link(dve.tensor_reduce(B[:, :], tot[:, :, :], AX.X, ALU.add))
            link(dve.tensor_scalar(kept[:, :], T[:, :], CAP + 0.5, None, ALU.is_lt))
            link(dve.tensor_reduce(wt[:, :], cw[:, :, :], AX.X, ALU.add))
            link(dve.tensor_tensor(wt[:, :], wt[:, :], kept[:, :], ALU.mult))
            link(dve.scalar_tensor_tensor(out=df[:, :], in0=T[:, :], scalar=-1.0, in1=B[:, :], op0=ALU.add, op1=ALU.add))
            link(dve.tensor_tensor(df[:, :], df[:, :], c["dump"][:, :], ALU.subtract))
            link(dve.tensor_tensor(df[:, :], df[:, :], kept[:, :], ALU.mult))
            link(dve.tensor_tensor(df[:, :], df[:, :], c["dump"][:, :], ALU.add))
            link(dve.tensor_scalar(sf[:, :], T[:, :], -1.0, float(CAP - 1), ALU.add, ALU.min))
            link(dve.tensor_tensor(sf[:, :], sf[:, :], B[:, :], ALU.add))
            link(dve.tensor_copy(dest[:, :], df[:, :]))
            link(dve.tensor_copy(src[:, :], sf[:, :]))


def dispatch(nc, rows, dest, buf):
    with ExitStack() as ctx:
        z = ctx.enter_context(nc.sbuf_tensor("X_zero", [SR, CAP // SR * D], F32))
        s_z, s_zero, s_sent = (ctx.enter_context(semaphore(nc, "X_" + x)) for x in ("zeros", "cleared", "sent"))
        block = ctx.enter_context(nc.Block())

        @block.vector
        def _(dve):
            dve.memset(z[:, :], 0.0).then_inc(s_z, 1)

        @block.sync
        def _(sp):
            sp.wait_ge(s_z, 1)
            bv = buf[0:EX * CAP, :].rearrange("(e p r) c -> e p (r c)", e=EX, p=SR)
            for e in range(EX):
                sp.dma_start(bv[e], z[:, :]).then_inc(s_zero, 16)
            sp.wait_ge(s_zero, 16 * EX)

        @block.gpsimd
        def _(pool):
            pool.wait_ge(s_zero, 16 * EX)
            for j in range(NTT):
                pool.indirect_dma_start(buf, bass.IndirectOffsetOnAxis(ap=dest[:, j:j + 1], axis=0), rows[:, j, :], None).then_inc(s_sent, 16)
            pool.wait_ge(s_sent, 16 * NTT)


def experts_sparse(nc, ins, buf, ybuf, eye):
    NU = EX * CU
    with ExitStack() as ctx:
        sb = lambda name, shape, dt=F32: ctx.enter_context(nc.sbuf_tensor("E_" + name, shape, dt))
        ps = lambda name, shape, dt=F32: ctx.enter_context(nc.psum_tensor("E_" + name, shape, dt))
        sem = lambda name: ctx.enter_context(semaphore(nc, "E_" + name))
        w1 = sb("w1", [D, 2, F2])
        w2 = sb("w2", [128, 2, 2, D])
        b1 = sb("b1", [128, 2, 2])
        b2 = sb("b2", [SR, 2, D])
        xin = sb("xin", [SR, 2, ST, D])
        xT = sb("xT", [D, 2, UT])
        hid = sb("hid", [128, 2, 2, UT])
        y = sb("y", [SR, 2, ST, D])
        pT = ps("pT", [128, 2, 512])
        pH = ps("pH", [128, 2, 2, 512])
        pY = ps("pY", [128, 2, 512])
        s_w = [sem(f"weights_in{k}") for k in range(2)]
        s_x = [sem(f"rows_in{k}") for k in range(2)]
        s_st = [sem(f"stored{k}") for k in range(2)]
        s_T, s_xT, s_h, s_ra, s_rd, s_y, s_out = (sem(x) for x in (
            "turned", "features", "hidden", "relu_act", "relu_dve", "products", "out"))
        bv = buf[0:EX * CAP, :].rearrange("(u s p) c -> u p s c", p=SR, s=ST)
        yv = ybuf.rearrange("(u s p) c -> u p s c", p=SR, s=ST)
        w1v = ins["w1"].rearrange("e d f -> e d f")
        w2v = ins["w2"].rearrange("e (x f) d -> e f x d", x=2)
        b1v = ins["b1"].rearrange("e (x f) -> e f x", x=2)
        block = ctx.enter_context(nc.Block())

        def wait(eng, s, n):
            if not (isinstance(n, int) and n <= 0):
                eng.wait_ge(s, n)

        def run(eng, step):
            step(-1, 7, mid=False, back=False)
            step(0, 0, back=False)
            for u in range(1, 8):
                step(u, u)
            with eng.Fori(1, EX // 2 - 1) as m:
                for q in range(8):
                    step(8 * m + q, q)
            for q in range(7):
                step(NU - 8 + q, q)
            step(NU - 1, 7, front=False)
            step(NU, 0, front=False, mid=False)

        @block.sync
        def _(sp):
            def load_w(e, k):
                sp.dma_start(w1[:, k, :], w1v[e]).then_inc(s_w[k], 16)
                sp.dma_start(w2[:, k], w2v[e]).then_inc(s_w[k], 16)
                sp.dma_start(b1[:, k, :], b1v[e], allow_slow_non_contiguous=True).then_inc(s_w[k], 16)
                sp.dma_start(b2[:, k, :], ins["b2"][e:e + 1, :].broadcast_to([SR, D]) if isinstance(e, int)
                             else ins["b2"][bass.ds(e, 1), :].broadcast_to([SR, D])).then_inc(s_w[k], 16)
            for k in range(2):
                load_w(k, k)
                sp.dma_start(xin[:, k], bv[k]).then_inc(s_x[k], 16)

            def unit(u, q, load=True):
                k = q % 2
                if load:
                    sp.wait_ge(s_T, u + 1)
                    sp.dma_start(xin[:, k], bv[u + 2]).then_inc(s_x[k], 16)
                sp.wait_ge(s_out, u + 1)
                sp.dma_start(yv[u], y[:, k]).then_inc(s_st[k], 16)

            def eight(m):
                for q in range(8):
                    k = q % 2
                    u = 8 * m + q
                    sp.wait_ge(s_T, u + 1)
                    sp.dma_start(xin[:, k], bv[u + 2]).then_inc(s_x[k], 16)
                    sp.wait_ge(s_out, u + 1)
                    sp.dma_start(yv[u], y[:, k]).then_inc(s_st[k], 16)
                    if q % 4 == 3:
                        load_w(2 * m + q // 4 + 2, q // 4)
            with sp.Fori(0, EX // 2 - 1) as m:
                eight(m)
            for q in range(8):
                unit(NU - 8 + q, q, load=q < 6)
            for k in range(2):
                sp.wait_ge(s_st[k], 16 * (NU // 2) + 16)

        @block.tensor
        def _(pe):
            def turn(u, q):
                k = q % 2
                wait(pe, s_xT, u - 1)
                if isinstance(u, int):
                    pe.wait_ge(s_x[k], 16 * (u // 2) + 16)
                else:
                    pe.wait_ge(s_x[k], (u - q) * 8 + 16 * (q // 2) + 16)
                for s in range(ST // 2):
                    pe.transpose(pT[:, k, s * SR:s * SR + SR], xin[:, k, 2 * s:2 * s + 2, :], eye[0:SR, 0:SR])
                pe.transpose(pT[0:D, k, 2 * SR:3 * SR], xin[:, k, ST - 1, :], eye[0:SR, 0:SR]).then_inc(s_T, 1)

            def hidden(u, q):
                k, kw = q % 2, q // 4
                pe.wait_ge(s_xT, u + 1)
                wait(pe, s_ra, u - 1)
                wait(pe, s_rd, u - 1)
                if q % 4 == 0:
                    pe.wait_ge(s_w[kw], 64 * (u // 8) + 64 if isinstance(u, int) else (u - q) * 8 + 64)
                for f in range(2):
                    pe.matmul(pH[:, k, f, 0:UT], w1[:, kw, f * 128:f * 128 + 128], xT[:, k, :], start=True, stop=True).then_inc(s_h, 1)

            def multiply(u, q):
                k, kw = q % 2, q // 4
                pe.wait_ge(s_ra, u + 1)
                pe.wait_ge(s_rd, u + 1)
                wait(pe, s_out, u - 1)
                for s in range(ST):
                    for f in range(2):
                        m = pe.matmul(pY[0:SR, k, s * D:s * D + D], hid[:, k, f, s * SR:s * SR + SR], w2[:, kw, f, :],
                                      start=(f == 0), stop=(f == 1))
                m.then_inc(s_y, 1)

            def step(u, q, front=True, mid=True, back=True):
                if front: turn(u + 1, (q + 1) % 8)
                if mid: hidden(u, q)
                if back: multiply(u - 1, (q - 1) % 8)
            run(pe, step)

        @block.scalar
        def _(act):
            act.preload_act_table(ACT.Exp)

            def step(u, q, front=True, mid=True, back=True):
                if front:
                    k = (q + 1) % 2
                    act.wait_ge(s_T, u + 2)
                    wait(act, s_h, 2 * u)
                    pairs = lambda x: xT[:, k, 0:4 * SR].rearrange("p (j x n) -> p x j n", x=2, n=SR)[:, x]
                    act.activation(pairs(0), pT[0:D, k, 0:2 * SR].rearrange("p (j n) -> p j n", n=SR), ACT.Copy)
                    act.activation(pairs(1), pT[D:128, k, 0:2 * SR].rearrange("p (j n) -> p j n", n=SR), ACT.Copy)
                    act.activation(xT[:, k, 4 * SR:UT], pT[0:D, k, 2 * SR:3 * SR], ACT.Copy).then_inc(s_xT, 1)
                if mid:
                    k = q % 2
                    act.wait_ge(s_h, 2 * u + 1)
                    wait(act, s_y, u - 1)
                    act.activation(hid[:, k, 0, :], pH[:, k, 0, 0:UT], ACT.Relu, bias=b1[:, q // 4, 0:1]).then_inc(s_ra, 1)
            run(act, step)

        @block.vector
        def _(dve):
            for k in range(2):
                dve.sem_inc(s_st[k], 16)

            def step(u, q, front=True, mid=True, back=True):
                if mid:
                    k = q % 2
                    dve.wait_ge(s_h, 2 * u + 2)
                    wait(dve, s_y, u - 1)
                    dve.tensor_scalar(hid[:, k, 1, :], pH[:, k, 1, 0:UT], b1[:, q // 4, 1:2], 0.0, ALU.add, ALU.max).then_inc(s_rd, 1)
                if back:
                    v, r = u - 1, (q - 1) % 8
                    k = r % 2
                    dve.wait_ge(s_y, v + 1)
                    dve.wait_ge(s_st[k], 16 * (v // 2) + 16 if isinstance(v, int) else (u - q) * 8 + (16 * ((q - 1) // 2) + 16))
                    dve.tensor_tensor(y[:, k], pY[0:SR, k, 0:ST * D].rearrange("p (s c) -> p s c", c=D),
                                      rep(b2[:, r // 4, :], ST), ALU.add).then_inc(s_out, 1)
            run(dve, step)


def combine(nc, h, hout, ybuf, src, wt):
    with ExitStack() as ctx:
        sb = lambda name, shape, dt=F32: ctx.enter_context(nc.sbuf_tensor("G_" + name, shape, dt))
        sem = lambda name: ctx.enter_context(semaphore(nc, "G_" + name))
        hin = sb("hin", [128, 2, GRP, D])
        ho = sb("ho", [128, 2, GRP, D])
        gy = sb("gy", [128, 2, GRP, D])
        yy = sb("yy", [128, GRP, D])
        ok = sb("ok", [128, GRP, D], U32)
        hi = sb("hi", [128, GRP, D], U32)
        lo = sb("lo", [128, GRP, D], U32)
        big = sb("big", [128, 2, GRP, D])
        tick = sb("tick", [128, 1])
        s_in = [sem(f"h_in{k}") for k in range(2)]
        s_st = [sem(f"stored{k}") for k in range(2)]
        s_g = [sem(f"gathered{k}") for k in range(2)]
        s_l, s_k, s_out, s_used = sem("step"), sem("constants"), sem("out"), sem("gather_used")
        hv = h.rearrange("(g j p) c -> g p j c", p=128, j=GRP)
        ov = hout.rearrange("(g j p) c -> g p j c", p=128, j=GRP)
        block = ctx.enter_context(nc.Block())

        @block.gpsimd
        def _(pool):
            for g in range(NG):
                if g >= 2:
                    pool.wait_ge(s_used, g - 1)
                for j in range(GRP):
                    pool.indirect_dma_start(gy[:, g % 2, j, :], None, ybuf,
                                            bass.IndirectOffsetOnAxis(ap=src[:, g * GRP + j:g * GRP + j + 1], axis=0)).then_inc(s_g[g % 2], 16)

        @block.sync
        def _(sp):
            for k in range(2):
                sp.dma_start(hin[:, k], hv[k]).then_inc(s_in[k], 16)
            with sp.Fori(0, NG // 2 - 1) as gg:
                for k in range(2):
                    sp.wait_ge(s_out, 2 * gg + k + 1)
                    sp.dma_start(hin[:, k], hv[2 * gg + 2 + k]).then_inc(s_in[k], 16)
                    sp.dma_start(ov[2 * gg + k], ho[:, k]).then_inc(s_st[k], 16)
            for k in range(2):
                sp.wait_ge(s_out, NG - 2 + k + 1)
                sp.dma_start(ov[NG - 2 + k], ho[:, k]).then_inc(s_st[k], 16)
            for k in range(2):
                sp.wait_ge(s_st[k], 16 * (NG // 2) + 16)

        LINKS = 9

        @block.vector
        def _(dve):
            for k in range(2):
                dve.sem_inc(s_st[k], 16)
            dve.memset(big[:, 0], 10000.0)
            dve.memset(big[:, 1], -10000.0).then_inc(s_k, 1)
            dve.wait_ge(s_k, 1)
            with dve.Fori(0, NG // 2) as gg:
                for k in range(2):
                    g = 2 * gg + k
                    link = linker(dve, s_l, g * LINKS)
                    dve.wait_ge(s_g[k], 16 * GRP * gg + 16 * GRP)
                    link(dve.tensor_tensor(gy[:, k], gy[:, k], bc(wt[:, bass.ds(g * GRP, GRP)], D), ALU.mult))
                    link(dve.tensor_tensor(ok[:, :, :], gy[:, k], gy[:, k], ALU.is_equal))
                    link(dve.tensor_scalar(hi[:, :, :], gy[:, k], FMAX, None, ALU.is_gt))
                    link(dve.tensor_scalar(lo[:, :, :], gy[:, k], -FMAX, None, ALU.is_lt))
                    link(dve.memset(yy[:, :, :], 0.0))
                    dve.memset(tick[:, :], 0.0)
                    link(dve.copy_predicated(yy[:, :, :], ok[:, :, :], gy[:, k]))
                    dve.sem_inc(s_used, 1)
                    dve.memset(tick[:, :], 0.0)
                    link(dve.copy_predicated(yy[:, :, :], hi[:, :, :], big[:, 0]))
                    dve.memset(tick[:, :], 0.0)
                    link(dve.copy_predicated(yy[:, :, :], lo[:, :, :], big[:, 1]))
                    dve.wait_ge(s_in[k], 16 * gg + 16)
                    dve.wait_ge(s_st[k], 16 * gg + 16)
                    link(dve.tensor_tensor(ho[:, k], hin[:, k], yy[:, :, :], ALU.add))
                    dve.sem_inc(s_out, 1)
                    assert link.count[0] == LINKS


def unit_vectors(nc, h, Fhl, ftok, ident):
    with ExitStack() as ctx:
        sb = lambda name, shape, dt=F32: ctx.enter_context(nc.sbuf_tensor(name, shape, dt))
        ps = lambda name, shape, dt=F32: ctx.enter_context(nc.psum_tensor(name, shape, dt))
        sem = lambda name: ctx.enter_context(semaphore(nc, name))
        hin = sb("D_hin", [128, 2, GRP, D])
        xc = sb("D_xc", [128, 2, GRP, D])
        sq = sb("D_sq", [128, 2, GRP, D])
        st = sb("D_st", [128, 2, 8, GRP])
        pT = ps("D_pT", [128, 2, GRP * 128 + 128], F16)
        s_in = [sem(f"D_h_in{k}") for k in range(2)]
        s_free = sem("D_h_used")
        s_link = sem("D_norm_step")
        s_var = sem("D_variance")
        s_sqrt = sem("D_root")
        s_part = sem("D_parts")
        s_T = sem("D_transposed")
        s_ev = sem("D_features")
        hv = h.rearrange("(g j p) c -> g p j c", p=128, j=GRP)
        block = ctx.enter_context(nc.Block())

        @block.sync
        def _(sp):
            sp.dma_start(hin[:, 0], hv[0]).then_inc(s_in[0], 16)
            sp.dma_start(hin[:, 1], hv[1]).then_inc(s_in[1], 16)
            with sp.Fori(0, NG // 2 - 1) as g:
                for k in range(2):
                    sp.wait_ge(s_free, 2 * g + k + 1)
                    sp.dma_start(hin[:, k], hv[2 * g + 2 + k]).then_inc(s_in[k], 16)

        LINKS = 11

        @block.vector
        def _(dve):
            with dve.Fori(0, NG // 2) as gg:
                for k in range(2):
                    g = 2 * gg + k
                    link = linker(dve, s_link, g * LINKS)
                    S = lambda i: st[:, k, i, :]
                    dve.wait_ge(s_in[k], 16 * gg + 16)
                    link(dve.tensor_reduce(S(0), hin[:, k], AX.X, ALU.add))
                    link(dve.tensor_scalar(S(1), S(0), 1.0 / D, None, ALU.mult))
                    link(dve.tensor_tensor(xc[:, k], hin[:, k], bc(S(1), D), ALU.subtract))
                    dve.sem_inc(s_free, 1)
                    link(dve.tensor_tensor(sq[:, k], xc[:, k], xc[:, k], ALU.mult))
                    link(dve.tensor_reduce(S(2), sq[:, k], AX.X, ALU.add))
                    link(dve.tensor_scalar(S(3), S(2), 1.0 / D, LN_EPS, ALU.mult, ALU.add))
                    dve.reciprocal(S(3), S(3)).then_inc(s_var, 1)
                    dve.wait_ge(s_sqrt, 2 * g + 1)
                    link(dve.tensor_tensor(S(4), S(2), S(3), ALU.mult))
                    dve.tensor_tensor(S(4), S(4), S(3), ALU.mult).then_inc(s_var, 1)
                    dve.wait_ge(s_sqrt, 2 * g + 2)
                    link(dve.tensor_scalar(S(4), S(4), N_EPS, None, ALU.max))
                    link(dve.reciprocal(S(5), S(4)))
                    link(dve.scalar_tensor_tensor(out=S(5), in0=S(5), scalar=FS, in1=S(3),
                                                  op0=ALU.mult, op1=ALU.mult))
                    link(dve.tensor_tensor(xc[:, k], xc[:, k], bc(S(5), D), ALU.mult))
                    assert link.count[0] == LINKS
                    js = bass.ds(g * GRP, GRP)
                    dve.tensor_copy(ftok[:, js, 0:D], xc[:, k]).then_inc(s_part, 1)
                    dve.wait_ge(s_part, 2 * g + 1)
                    dve.tensor_tensor(ftok[:, js, D:2 * D], xc[:, k], ftok[:, js, 0:D], ALU.subtract).then_inc(s_part, 1)

        @block.tensor
        def _(pe):
            with pe.Fori(0, NG // 2) as gg:
                for k in range(2):
                    g = 2 * gg + k
                    pe.wait_ge(s_part, 2 * g + 2)
                    pe.wait_ge(s_ev, g + 1)
                    for j in range(GRP):
                        m = pe.transpose(pT[:, k, j * 128:j * 128 + 128], ftok[:, g * GRP + j, :], ident[:, :])
                    m.then_inc(s_T, 1)

        @block.scalar
        def _(act):
            act.preload_act_table(ACT.Sqrt)
            act.sem_inc(s_ev, 2)
            with act.Fori(0, NG // 2) as gg:
                for k in range(2):
                    g = 2 * gg + k
                    for i in range(2):
                        act.wait_ge(s_var, 2 * g + i + 1)
                        act.activation(st[:, k, 3 + i, :], st[:, k, 3 + i, :], ACT.Sqrt).then_inc(s_sqrt, 1)
                    act.wait_ge(s_T, g + 1)
                    act.activation(Fhl[:, bass.ds(g * QB, QB)], pT[:, k, 0:QB], ACT.Copy).then_inc(s_ev, 1)


def attention(nc, Fhl, ftok, OT, den):
    U = 2 * NTT
    with ExitStack() as ctx:
        sb = lambda name, shape, dt=F32: ctx.enter_context(nc.sbuf_tensor(name, shape, dt))
        ps = lambda name, shape, dt=F32: ctx.enter_context(nc.psum_tensor(name, shape, dt))
        sem = lambda name: ctx.enter_context(semaphore(nc, name))
        qhi = sb("D_qhi", [128, 2, QB], F16)
        qlo = sb("D_qlo", [128, 2, QB], F16)
        E = sb("D_E", [128, 4, QH])
        Eh = sb("D_Eh", [128, 4, QH], F16)
        El = sb("D_El", [128, 4, QH], F16)
        pS = ps("D_pS", [128, 4, 512])
        pO = ps("D_pO", [128, 2, 2, 512])
        s_q = [sem(f"D_queries_in{k}") for k in range(2)]
        s_S = sem("D_scores")
        s_E = sem("D_exp")
        s_hD = sem("D_exp_high")
        s_lo = sem("D_exp_low")
        s_pv = sem("D_weighted")
        s_ev = sem("D_out_copied")
        block = ctx.enter_context(nc.Block())

        @block.sync
        def _(sp):
            def load(k, b):
                cols = bass.ds(b * QB, QB)
                for dst, p in ((qhi, 0), (qlo, D)):
                    for half in range(2):
                        sp.dma_start(dst[half * D:half * D + D, k, :], Fhl[p:p + D, cols]).then_inc(s_q[k], 16)
            load(0, 0)
            load(1, 1)
            with sp.Fori(0, NG // 2 - 1) as bb:
                for k in range(2):
                    sp.wait_ge(s_pv, bb * (2 * U) + (k + 1) * U + 4)
                    load(k, 2 * bb + 2 + k)

        @block.tensor
        def _(pe):
            def scores(r, k, j, half):
                keys = Fhl[:, bass.ds(j * 128, 128)]
                cols = slice(half * QH, half * QH + QH)
                pe.matmul(pS[:, r, 0:QH], keys, qhi[:, k, cols], start=True, stop=False)
                pe.matmul(pS[:, r, 0:QH], keys, qlo[:, k, cols], start=False, stop=True).then_inc(s_S, 1)

            def weigh(r, k, j, half, first, last, u):
                pe.wait_ge(s_lo, u + 1)
                f = ftok[:, j, :]
                pe.matmul(pO[:, k, half, 0:QH], f, Eh[:, r, :], start=first, stop=False)
                pe.matmul(pO[:, k, half, 0:QH], f, El[:, r, :], start=False, stop=last).then_inc(s_pv, 1)

            def four(k, base, j, first=False, last=False, next_load=None, end=False):
                for r in range(4):
                    ahead = r + 3
                    if not (end and ahead >= 4):
                        pe.wait_ge(s_E, base + r + 1)
                        if last and ahead >= 4:
                            if r == 1:
                                pe.wait_ge(s_q[1 - k], next_load)
                            scores(ahead % 4, 1 - k, (ahead - 4) // 2, ahead % 2)
                        else:
                            scores(ahead % 4, k, j + ahead // 2, ahead % 2)
                    weigh(r, k, j + r // 2, r % 2, first and r < 2, last and r >= 2, base + r)

            def query_block(k, b, next_load, end=False):
                pe.wait_ge(s_ev, b + 1)
                four(k, b * U, 0, first=True)
                with pe.Fori(1, NTT // 2 - 1) as m:
                    four(k, b * U + 4 * m, 2 * m)
                four(k, b * U + U - 4, NTT - 2, last=True, next_load=next_load, end=end)

            pe.wait_ge(s_q[0], 64)
            for r in range(3):
                scores(r, 0, r // 2, r % 2)
            with pe.Fori(0, NG // 2 - 1) as bb:
                query_block(0, 2 * bb, 64 * bb + 64)
                query_block(1, 2 * bb + 1, 64 * bb + 128)
            query_block(0, NG - 2, 64 * (NG // 2))
            query_block(1, NG - 1, None, end=True)

        @block.scalar
        def _(act):
            act.preload_act_table(ACT.Exp)
            act.sem_inc(s_E, 1)
            act.sem_inc(s_pv, 4)
            with act.Fori(0, NG * NTT // 2) as m:
                for r in range(4):
                    act.wait_ge(s_S, 4 * m + r + 1)
                    act.wait_ge(s_pv, 4 * m + r + 1)
                    if r % 2 == 0:
                        act.activation(Eh[:, r, :], pS[:, r, 0:QH], ACT.Exp, scale=1.0 / (FS * FS))
                    act.activation(E[:, r, :], pS[:, r, 0:QH], ACT.Exp, scale=1.0 / (FS * FS),
                                   accum_out=den[:, bass.ds(4 * m + r, 1)]).then_inc(s_E, 1)

        @block.vector
        def _(dve):
            dve.sem_inc(s_ev, 2)

            def four(m):
                for r in range(4):
                    dve.wait_ge(s_E, 4 * m + r + 2)
                    if r % 2 == 1:
                        dve.tensor_copy(Eh[:, r, :], E[:, r, :]).then_inc(s_hD, 1)
                        dve.wait_ge(s_hD, 2 * m + r // 2 + 1)
                    dve.tensor_tensor(El[:, r, :], E[:, r, :], Eh[:, r, :], ALU.subtract).then_inc(s_lo, 1)

            def copy_out(b, k):
                dve.wait_ge(s_pv, b * U + U + 4)
                dve.tensor_copy(OT[:, bass.ds(b * QB, QB)].rearrange("p (a n) -> p a n", a=2),
                                pO[:, k, :, 0:QH]).then_inc(s_ev, 1)

            M = NTT // 2
            with dve.Fori(0, M) as m:
                four(m)
            with dve.Fori(0, NG // 2 - 1) as bb:
                for k in range(2):
                    four((2 * bb + k + 1) * M)
                    copy_out(2 * bb + k, k)
                    with dve.Fori(1, M) as m:
                        four((2 * bb + k + 1) * M + m)
            four((NG - 1) * M)
            copy_out(NG - 2, 0)
            with dve.Fori(1, M) as m:
                four((NG - 1) * M + m)
            copy_out(NG - 1, 1)


def blend(nc, h, hout, ftok, OT, den, fold):
    with ExitStack() as ctx:
        sb = lambda name, shape, dt=F32: ctx.enter_context(nc.sbuf_tensor(name, shape, dt))
        ps = lambda name, shape, dt=F32: ctx.enter_context(nc.psum_tensor(name, shape, dt))
        sem = lambda name: ctx.enter_context(semaphore(nc, name))
        hin = sb("F_hin", [128, 2, GRP, D])
        f8 = sb("F_f8", [128, GRP, D])
        fc = sb("F_fc", [128, GRP, D])
        sq = sb("F_sq", [128, GRP, D])
        ho = sb("F_ho", [128, 2, GRP, D])
        rden = sb("F_rden", [128, NTT])
        st = sb("F_st", [128, 2, GRP])
        pt = ps("F_pt", [128, 2, 512])
        ot = sb("F_ot", [128, 2, QB])
        s_in = [sem(f"F_h_in{k}") for k in range(2)]
        s_link = sem("F_step")
        s_den = sem("F_sum_step")
        s_n2 = sem("F_squares")
        s_root = sem("F_root")
        s_ot = sem("F_sums_moved")
        s_T = sem("F_token_rows")
        s_used = sem("F_rows_used")
        s_out = sem("F_out")
        s_st = [sem(f"F_stored{k}") for k in range(2)]
        hv = h.rearrange("(g j p) c -> g p j c", p=128, j=GRP)
        ov = hout.rearrange("(g j p) c -> g p j c", p=128, j=GRP)
        block = ctx.enter_context(nc.Block())

        @block.sync
        def _(sp):
            sp.dma_start(hin[:, 0], hv[0]).then_inc(s_in[0], 16)
            sp.dma_start(hin[:, 1], hv[1]).then_inc(s_in[1], 16)
            with sp.Fori(0, NG // 2 - 1) as gg:
                for k in range(2):
                    sp.wait_ge(s_out, 2 * gg + k + 1)
                    sp.dma_start(hin[:, k], hv[2 * gg + 2 + k]).then_inc(s_in[k], 16)
                    sp.dma_start(ov[2 * gg + k], ho[:, k]).then_inc(s_st[k], 16)
            for k in range(2):
                sp.wait_ge(s_out, NG - 2 + k + 1)
                sp.dma_start(ov[NG - 2 + k], ho[:, k]).then_inc(s_st[k], 16)
            for k in range(2):
                sp.wait_ge(s_st[k], 16 * (NG // 2) + 16)

        @block.tensor
        def _(pe):
            with pe.Fori(0, NG // 2) as gg:
                for k in range(2):
                    pe.wait_ge(s_used, 2 * gg + k + 1)
                    pe.wait_ge(s_ot, 2 * gg + k + 1)
                    for j in range(GRP):
                        m = pe.matmul(pt[:, k, j * D:j * D + D], ot[:, k, j * 128:j * 128 + 128], fold[:, :], start=True, stop=True)
                    m.then_inc(s_T, 1)

        @block.scalar
        def _(act):
            act.preload_act_table(ACT.Sqrt)
            act.sem_inc(s_T, 2)
            with act.Fori(0, NG // 2) as gg:
                for k in range(2):
                    g = 2 * gg + k
                    act.wait_ge(s_T, g + 1)
                    act.activation(ot[:, k, :], OT[:, bass.ds(g * QB, QB)], ACT.Copy).then_inc(s_ot, 1)
                    act.wait_ge(s_n2, g + 1)
                    act.activation(st[:, 0, :], st[:, 0, :], ACT.Sqrt).then_inc(s_root, 1)

        LINKS = 8

        @block.vector
        def _(dve):
            dve.sem_inc(s_used, 2)
            for k in range(2):
                dve.sem_inc(s_st[k], 16)
            link = linker(dve, s_den)
            link(dve.tensor_reduce(rden[:, :], den[:, :].rearrange("p (b j a) -> p j b a", j=NTT, a=2), AX.XY, ALU.add))
            link(dve.reciprocal(rden[:, :], rden[:, :]))
            link(dve.tensor_scalar(rden[:, :], rden[:, :], (1.0 - BLEND) / FS, None, ALU.mult))
            with dve.Fori(0, NG // 2) as gg:
                for k in range(2):
                    g = 2 * gg + k
                    js = bass.ds(g * GRP, GRP)
                    link = linker(dve, s_link, g * LINKS)
                    link(dve.tensor_tensor(f8[:, :, :], ftok[:, js, 0:D], ftok[:, js, D:2 * D], ALU.add))
                    dve.wait_ge(s_T, g + 3)
                    link(dve.tensor_tensor(fc[:, :, :], pt[:, k, 0:GRP * D].rearrange("p (j c) -> p j c", c=D),
                                           bc(rden[:, js], D), ALU.mult))
                    dve.sem_inc(s_used, 1)
                    link(dve.scalar_tensor_tensor(out=fc[:, :, :], in0=f8[:, :, :], scalar=BLEND / FS, in1=fc[:, :, :],
                                                  op0=ALU.mult, op1=ALU.add))
                    link(dve.tensor_tensor(sq[:, :, :], fc[:, :, :], fc[:, :, :], ALU.mult))
                    dve.tensor_reduce(st[:, 0, :], sq[:, :, :], AX.X, ALU.add).then_inc(s_n2, 1)
                    dve.wait_ge(s_root, g + 1)
                    link(dve.tensor_scalar(st[:, 0, :], st[:, 0, :], N_EPS, None, ALU.max))
                    link(dve.reciprocal(st[:, 1, :], st[:, 0, :]))
                    link(dve.tensor_tensor(fc[:, :, :], fc[:, :, :], bc(st[:, 1, :], D), ALU.mult))
                    dve.wait_ge(s_in[k], 16 * gg + 16)
                    dve.wait_ge(s_st[k], 16 * gg + 16)
                    link(dve.tensor_tensor(ho[:, k], hin[:, k], fc[:, :, :], ALU.add))
                    dve.sem_inc(s_out, 1)
                    assert link.count[0] == LINKS


RWKV_INS = ("x_mix", "W_r", "W_k", "W_v", "W_o", "A_w", "B_w", "b_w", "A_a", "B_a", "b_a", "A_g", "B_g",
            "k_k", "k_a", "r_k", "gn_w", "gn_b")


def network(nc, ins, cst, out):
    dram = lambda name, shape: nc.dram_tensor(name, shape, F32, kind="Internal").ap()
    hA, hB, hC, hD = (dram(f"h_{x}", [TOK, D]) for x in ("tokens", "rwkv", "experts1", "attention"))
    buf = dram("expert_rows", [EX * CAP + TOK, D])
    ybuf = dram("expert_outputs", [EX * CAP, D])
    part = lambda pre: {k[len(pre):]: v for k, v in ins.items() if k.startswith(pre)}

    tk = part("L0_tok_")
    tokenizer(nc, ins["x"], tk["W1"], tk["b1"], tk["W2"], tk["b2"], tk["W3"], tk["b3"], hA)

    with ExitStack() as ctx:
        sb = lambda name, shape, dt=F32: ctx.enter_context(nc.sbuf_tensor(name, shape, dt))
        w, c = weights(nc, ctx, part("L0_attn_"), cst)
        rkv = sb("rkv", [128, NTT, 3 * D])
        rn = sb("rn", [128, NTT])
        ga = sb("ga", [128, NTT, D])
        with nc.sbuf_tensor("Z2", [128, TOK], F32) as Z2:
            norm_features(nc, hA, Z2, c["eye"])
            project(nc, w, Z2, rkv, rn)
            recurrence(nc, w, c, Z2, rkv, ga, rn)
        outputs(nc, w, hA, hB, rkv, ga, c["eye"])

    with ExitStack() as ctx:
        sb = lambda name, shape, dt=F32: ctx.enter_context(nc.sbuf_tensor(name, shape, dt))
        eye = sb("eye", [128, 128])
        XT = sb("XT1", [128, TOK])
        cw = sb("cw1", [128, NTT, EX])
        load_all(nc, "C", [(eye[:, :], cst["eye"])], zero=[XT[D:128, :]])
        w = moe1_weights(nc, ctx, part("L0_ffn_"), cst)
        layer_norm(nc, "C0_", hB, XT, eye)
        gating(nc, "C1_", XT, w["gate"][:, :], w["gb"][:, :], w["less"][:, :], 2, cw)
        experts_dense(nc, hB, hC, XT, cw, w, eye)

    with ExitStack() as ctx:
        sb = lambda name, shape, dt=F32: ctx.enter_context(nc.sbuf_tensor(name, shape, dt))
        Fhl = sb("Fhl", [128, TOK], F16)
        ftok = sb("ftok", [128, NTT, 128], F16)
        OT = sb("OT", [128, TOK])
        den = sb("den", [128, NG * NTT * 2])
        eye16 = sb("eye16", [128, 128], F16)
        fold = sb("fold", [128, D])
        load_all(nc, "D", [(eye16[:, :], cst["eye16"]), (fold[:, :], cst["fold"])])
        unit_vectors(nc, hC, Fhl, ftok, eye16)
        attention(nc, Fhl, ftok, OT, den)
        blend(nc, hC, hD, ftok, OT, den, fold)

    with ExitStack() as ctx:
        sb = lambda name, shape, dt=F32: ctx.enter_context(nc.sbuf_tensor(name, shape, dt))
        p = part("L1_ffn_")
        eye = sb("eye2", [128, 128])
        cw = sb("cw2", [128, NTT, EX])
        chosen = sb("chosen", [128, NTT, EX])
        rows = sb("rows", [128, NTT, D])
        dest = sb("dest", [128, NTT], U32)
        src = sb("src", [128, NTT], U32)
        wt = sb("wt", [128, NTT])
        gw = sb("gate_w2", [D, EX])
        gb = sb("gate_b2", [128, EX])
        c = {k: sb(f"c_{k}", list(v.shape)) for k, v in cst.items() if k in MOE_CONSTANTS}
        load_all(nc, "E", [(eye[:, :], cst["eye"]), (gw[:, :], p["gate_w"]),
                           (gb[:, :], p["gate_b"].rearrange("(a c) -> a c", a=1).broadcast_to([128, EX]))]
                 + [(c[k][:, :], cst[k]) for k in MOE_CONSTANTS])
        with nc.sbuf_tensor("XT2", [D, TOK], F32) as XT:
            layer_norm(nc, "E0_", hD, XT, eye, rows)
            gating(nc, "E1_", XT, gw[:, :], gb[:, :], c["less"][:, :], 1, cw, chosen)
        slots(nc, c, chosen, cw, dest, src, wt)
        dispatch(nc, rows, dest, buf)
        experts_sparse(nc, p, buf, ybuf, eye)
        combine(nc, hD, out, ybuf, src, wt)


MOE_CONSTANTS = ("less", "base", "dump", "upto")


def load_all(nc, name, pairs, zero=()):
    with semaphore(nc, name + "_loaded") as s, semaphore(nc, name + "_zeroed") as z, nc.Block() as block:
        @block.sync
        def _(sp):
            for dst, src in pairs:
                sp.dma_start(dst, src).then_inc(s, 16)
            sp.wait_ge(s, 16 * len(pairs))

        @block.vector
        def _(dve):
            for dst in zero:
                dve.memset(dst, 0.0).then_inc(z, 1)


def all_constants():
    c = dict(constants())
    c.update(moe_constants())
    c["eye16"] = np.eye(128).astype(np.float16)
    c["fold"] = np.tile(np.eye(D), (2, 1)).astype(np.float32)
    return c


def tap_rows(W):
    W = W.reshape(CH, 9, -1).transpose(1, 0, 2)[[3 * i + j for i, j in TAPS]].reshape(9 * CH, -1)
    return np.concatenate([W, np.zeros((NCH * 128 - 9 * CH, W.shape[1]), W.dtype)])


def kernel(**inputs):
    import concourse.bacc as _bacc
    from concourse.bass_utils import run_bass_kernel_spmd as _run

    data = {k: np.asarray(v) for k, v in inputs.items()}
    data["x"] = data["x"].reshape(BATCH, CH, IMG, IMG)
    data["L0_tok_W1"] = tap_rows(data["L0_tok_W1"])
    data["L0_tok_W2"] = tap_rows(data["L0_tok_W2"].T).T
    data["L0_tok_b2"] = tap_rows(data["L0_tok_b2"][:, None])[:, 0]
    data["L0_tok_W3"] = tap_rows(data["L0_tok_W3"])

    nc = _bacc.Bacc("TRN2", target_bir_lowering=False, num_devices=1)
    arrays = {}

    def place(name, a):
        arrays[name] = np.ascontiguousarray(a)
        return nc.dram_tensor(name, a.shape, mybir.dt.from_np(a.dtype), kind="ExternalInput").ap()
    ins = {k: place("in_" + k, v) for k, v in data.items()}
    cst = {k: place("const_" + k, v) for k, v in all_constants().items()}
    out = nc.dram_tensor("out", (TOK, D), F32, kind="ExternalOutput").ap()
    network(nc, ins, cst, out)
    r = _run(nc, [arrays], core_ids=[0])
    return r.results[0]["out"].reshape(BATCH, SEQ, D)
```

```python
from contextlib import ExitStack, contextmanager
import numpy as np
from concourse import bass, mybir
F32 = mybir.dt.float32
F16 = mybir.dt.float16
U32 = mybir.dt.uint32
ALU = mybir.AluOpType
ACT = mybir.ActivationFunctionType
AX = mybir.AxisListType

BATCH, CH, IMG = 4, 64, 56
D = CH
SEQ = IMG * IMG
TOK = BATCH * SEQ
NTT = TOK // 128
GRP = 7
NG = NTT // GRP
QB = GRP * 128
QH = QB // 2
LN_EPS = 1e-5
N_EPS = 1e-12
FMAX = 3.4028234663852886e38

PAD = IMG + 2
ROWS = 8
TILE = ROWS * IMG
NT = IMG // ROWS
SUB = TILE // 4
TAPS = [(0, 0), (0, 1), (1, 0), (1, 1), (2, 0), (2, 1), (0, 2), (1, 2), (2, 2)]
NCH = 5

GN_EPS = D * 1e-5
DECAY = -0.6065306597126334
CS = 64
NIT = NTT // 2
LEVELS = 5

EX = 8
F1 = 128
F2 = 256
CAP = -(-5 * TOK // (4 * EX))
CU = 4
UT = CAP // CU
ST = 5
SR = UT // ST

FS = 64.0
BLEND = 0.8


@contextmanager
def semaphore(nc, name):
    s = nc.alloc_semaphore(name=name)
    yield s
    nc.gpsimd.sem_clear(s)
    nc.release_semaphore(s)


def pairs(eng, sem, base):
    n = [0]

    def both(op, before=None):
        for k in range(2):
            if n[0]:
                eng.wait_ge(sem, base + done(n[0] - 1, k))
            if before is not None:
                before(k)
            op(k).then_inc(sem, 1)
        n[0] += 1
    both.count = n
    return both


def done(n, k):
    return 2 * n + k + 1


def constants():
    s, t = np.meshgrid(np.arange(128), np.arange(128), indexing="ij")
    same = s // CS == t // CS
    up, upi = same & (s < t), same & (s <= t)
    c = {"tri": np.concatenate([upi, same & (s > t)], 1),
         "ind": np.stack([np.arange(128) // CS == k for k in range(2)], 1),
         "mask": np.concatenate([up, upi, up, upi], 1),
         "neg0": -np.concatenate([(s % 2 == 1) & (t == s - 1), (t % 2 == 1) & (s == t - 1)], 1).astype(np.float32),
         "lev": np.concatenate([(s >> (l + 1) == t >> (l + 1)) & ((t >> l) & 1 == 1) & ((s >> l) & 1 == 0)
                                for l in range(1, LEVELS + 1)], 1),
         "eye": s == t,
         "keep": np.tile((np.arange(1, NTT + 1) % (SEQ // CS) != 0)[None], (D, 1))}
    return {k: np.ascontiguousarray(v.astype(np.float32)) for k, v in c.items()}


def linker(eng, sem, base=0):
    n = [0]

    def link(ins):
        n[0] += 1
        ins.then_inc(sem, 1)
        eng.wait_ge(sem, base + n[0])
    link.count = n
    return link


def bc(ap, n):
    p, g = ap.shape
    return ap.rearrange("p (g a) -> p g a", a=1).broadcast_to([p, g, n])


def rep(ap, n):
    p, c = ap.shape
    return ap.rearrange("p (a c) -> p a c", a=1).broadcast_to([p, n, c])


def norm_features(nc, h, Z2, eye):
    with ExitStack() as ctx:
        sb = lambda name, shape, dt=F32: ctx.enter_context(nc.sbuf_tensor(name, shape, dt))
        sem = lambda name: ctx.enter_context(semaphore(nc, name))
        hin = sb("B0_hin", [128, 2, GRP, D])
        xc = sb("B0_xc", [128, 2, GRP, D])
        sq = sb("B0_sq", [128, 2, GRP, D])
        st = sb("B0_st", [128, 2, 4, GRP])
        pT = ctx.enter_context(nc.psum_tensor("B0_pT", [128, 2, 512], F32))
        s_in = [sem(f"B0_h_in{k}") for k in range(2)]
        s_link, s_sqrt = sem("B0_step"), sem("B0_root")
        s_T, s_ev, s_z, s_sh = sem("B0_transposed"), sem("B0_features"), sem("B0_starts"), sem("B0_shifted")
        hv = h.rearrange("(g j p) c -> g p j c", p=128, j=GRP)
        block = ctx.enter_context(nc.Block())

        LINKS = 8
        CENTERED, VAR, NORMED = 2, 6, LINKS - 1

        @block.sync
        def _(sp):
            for k in range(2):
                sp.dma_start(hin[:, k], hv[k]).then_inc(s_in[k], 16)
            with sp.Fori(0, NG // 2 - 1) as g:
                for k in range(2):
                    sp.wait_ge(s_link, g * (2 * LINKS) + done(CENTERED, k))
                    sp.dma_start(hin[:, k], hv[2 * g + 2 + k]).then_inc(s_in[k], 16)
            for b in range(BATCH):
                sp.wait_ge(s_ev, 2 + min(NG, -(-(b + 1) * SEQ // QB)))
                sp.dma_start(Z2[D:2 * D, b * SEQ + 1:(b + 1) * SEQ], Z2[0:D, b * SEQ:(b + 1) * SEQ - 1]).then_inc(s_sh, 16)
            sp.wait_ge(s_sh, 16 * BATCH)

        @block.gpsimd
        def _(pool):
            for b in range(BATCH):
                m = pool.memset(Z2[D:2 * D, b * SEQ:b * SEQ + 1], 0.0)
            m.then_inc(s_z, 1)

        @block.vector
        def _(dve):
            with dve.Fori(0, NG // 2) as gg:
                both = pairs(dve, s_link, gg * (2 * LINKS))
                S = lambda k, i: st[:, k, i, :]
                both(lambda k: dve.tensor_reduce(S(k, 0), hin[:, k], AX.X, ALU.add),
                     lambda k: dve.wait_ge(s_in[k], 16 * gg + 16))
                both(lambda k: dve.tensor_scalar(S(k, 1), S(k, 0), 1.0 / D, None, ALU.mult))
                both(lambda k: dve.tensor_tensor(xc[:, k], hin[:, k], bc(S(k, 1), D), ALU.subtract),
                     lambda k: dve.wait_ge(s_T, 2 * gg + k + 1))
                both(lambda k: dve.tensor_tensor(sq[:, k], xc[:, k], xc[:, k], ALU.mult))
                both(lambda k: dve.tensor_reduce(S(k, 2), sq[:, k], AX.X, ALU.add))
                both(lambda k: dve.tensor_scalar(S(k, 2), S(k, 2), 1.0 / D, LN_EPS, ALU.mult, ALU.add))
                both(lambda k: dve.reciprocal(S(k, 3), S(k, 2)))
                both(lambda k: dve.tensor_tensor(xc[:, k], xc[:, k], bc(S(k, 3), D), ALU.mult),
                     lambda k: dve.wait_ge(s_sqrt, 2 * gg + k + 1))
                assert both.count[0] == LINKS

        @block.tensor
        def _(pe):
            pe.sem_inc(s_T, 2)
            with pe.Fori(0, NG // 2) as gg:
                for k in range(2):
                    g = 2 * gg + k
                    pe.wait_ge(s_link, gg * (2 * LINKS) + done(NORMED, k))
                    pe.wait_ge(s_ev, g + 1)
                    for j in range(GRP // 2):
                        pe.transpose(pT[:, k, j * 128:j * 128 + 128], xc[:, k, 2 * j:2 * j + 2, :], eye[:, :])
                    m = pe.transpose(pT[0:D, k, 384:512], xc[:, k, GRP - 1, :], eye[:, :])
                    m.then_inc(s_T, 1)

        @block.scalar
        def _(act):
            act.preload_act_table(ACT.Sqrt)
            act.sem_inc(s_ev, 2)
            with act.Fori(0, NG // 2) as gg:
                for k in range(2):
                    g = 2 * gg + k
                    act.wait_ge(s_link, gg * (2 * LINKS) + done(VAR, k))
                    act.activation(st[:, k, 3, :], st[:, k, 3, :], ACT.Sqrt).then_inc(s_sqrt, 1)
                for k in range(2):
                    g = 2 * gg + k
                    act.wait_ge(s_T, g + 3)
                    z = Z2[0:D, bass.ds(g * QB, QB)]
                    pair = lambda x: z[:, 0:768].rearrange("p (j x n) -> p x j n", x=2, n=128)[:, x]
                    act.activation(pair(0), pT[0:D, k, 0:384].rearrange("p (j n) -> p j n", n=128), ACT.Copy)
                    act.activation(pair(1), pT[D:128, k, 0:384].rearrange("p (j n) -> p j n", n=128), ACT.Copy)
                    act.activation(z[:, 768:896], pT[0:D, k, 384:512], ACT.Copy).then_inc(s_ev, 1)


def project(nc, w, Z2, rkv, rn):
    with ExitStack() as ctx:
        sb = lambda name, shape, dt=F32: ctx.enter_context(nc.sbuf_tensor(name, shape, dt))
        sem = lambda name: ctx.enter_context(semaphore(nc, name))
        zs = sb("P_zs", [128, 2, QB])
        kk = sb("P_kk", [128, GRP, D])
        pR = ctx.enter_context(nc.psum_tensor("P_pR", [128, 2, 4, 512], F32))
        s_zs, s_p, s_rkv, s_kk, s_n, s_end, s_root = (sem("P_" + x) for x in (
            "tile_moved", "projected", "rows_copied", "keys_scaled", "norms", "norms_done", "root"))
        block = ctx.enter_context(nc.Block())

        @block.scalar
        def _(act):
            act.preload_act_table(ACT.Sqrt)
            with act.Fori(0, NG // 2) as gg:
                for k in range(2):
                    g = 2 * gg + k
                    act.wait_ge(s_p, g + 1)
                    act.activation(zs[:, k, :], Z2[:, bass.ds(g * QB, QB)], ACT.Copy).then_inc(s_zs, 1)
            act.wait_ge(s_end, 1)
            act.activation(rn[:, :], rn[:, :], ACT.Sqrt).then_inc(s_root, 1)

        @block.tensor
        def _(pe):
            pe.sem_inc(s_p, 2)
            with pe.Fori(0, NG // 2) as gg:
                for k in range(2):
                    g = 2 * gg + k
                    pe.wait_ge(s_zs, g + 1)
                    pe.wait_ge(s_rkv, g + 1)
                    for j in range(GRP):
                        m = pe.matmul(pR[:, k, j // 2, (j % 2) * 192:(j % 2) * 192 + 192],
                                      zs[:, k, j * 128:j * 128 + 128], w["rkv"][:, :], start=True, stop=True)
                    m.then_inc(s_p, 1)

        @block.vector
        def _(dve):
            dve.sem_inc(s_rkv, 2)
            with dve.Fori(0, NG // 2) as gg:
                for k in range(2):
                    g = 2 * gg + k
                    dve.wait_ge(s_p, g + 3)
                    dve.tensor_copy(rkv[:, bass.ds(g * GRP, 6), :].rearrange("p (b j) c -> p b j c", j=2),
                                    pR[:, k, 0:3, 0:384].rearrange("p b (j c) -> p b j c", j=2))
                    dve.tensor_copy(rkv[:, bass.ds(g * GRP + 6, 1), :].rearrange("p a c -> p (a c)"),
                                    pR[:, k, 3, 0:192]).then_inc(s_rkv, 1)
                    dve.wait_ge(s_rkv, g + 3)
                    dve.tensor_tensor(kk[:, :, :], rkv[:, bass.ds(g * GRP, GRP), D:2 * D], rep(w["k_k"][:, :], GRP),
                                      ALU.mult).then_inc(s_kk, 1)
                    dve.wait_ge(s_kk, 2 * g + 1)
                    dve.tensor_tensor(kk[:, :, :], kk[:, :, :], kk[:, :, :], ALU.mult).then_inc(s_kk, 1)
                    dve.wait_ge(s_kk, 2 * g + 2)
                    dve.tensor_reduce(rn[:, bass.ds(g * GRP, GRP)], kk[:, :, :], AX.X, ALU.add).then_inc(s_n, 1)
                    dve.wait_ge(s_n, g + 1)
            dve.sem_inc(s_end, 1)
            dve.wait_ge(s_root, 1)
            dve.tensor_scalar(rn[:, :], rn[:, :], N_EPS, None, ALU.max).then_inc(s_end, 1)
            dve.wait_ge(s_end, 2)
            dve.reciprocal(rn[:, :], rn[:, :]).then_inc(s_end, 1)


def recurrence(nc, w, c, Z2, rkv, gate_, rn):
    with ExitStack() as ctx:
        sb = lambda name, shape, dt=F32: ctx.enter_context(nc.sbuf_tensor(name, shape, dt))
        sem = lambda name: ctx.enter_context(semaphore(nc, "R_" + name))
        hid = sb("R_hid", [128, 256])
        gh = sb("R_gh", [128, 256])
        wa = sb("R_wa", [128, 2, 128])
        lw = sb("R_lw", [128, 2, D])
        a_ = sb("R_a", [128, 2, D])
        ex = sb("R_ex", [128, 2, D])
        eP = sb("R_eP", [128, 2, D])
        eN = sb("R_eN", [128, 2, D])
        eS = sb("R_eS", [128, 2, D])
        eX = sb("R_eX", [128, 2, D])
        kn = sb("R_kn", [128, 2, D])
        kp = sb("R_kp", [128, 2, D])
        bt = sb("R_bt", [128, 2, D])
        rk = sb("R_rk", [128, 2, D])
        rs = sb("R_rs", [128, 2])
        V = sb("R_V", [128, 2, 2, D])
        DC = sb("R_DC", [D, 2, 4])
        QN = sb("R_QN", [128, 2, 2, 128])
        RBK = sb("R_QRBK", [128, 4, 2, D])
        Bh = sb("R_Bh", [128, 2, 2, 2, D])
        Kh = sb("R_Kh", [128, 2, 2, 2, D])
        FT = sb("R_FT", [D, 2, 2, 512])
        PM = sb("R_PM", [128, 2, 2, 512])
        ML = sb("R_ML", [128, LEVELS, 2, 128])
        XX = sb("R_XX", [128, 2, 2, 128])
        XT = sb("R_XT", [128, 2, 2, 128])
        Ys = sb("R_Ys", [128, 2, 128])
        WU = sb("R_WU", [128, 2, 128])
        RpT = sb("R_RpT", [D, 256])
        GT = sb("R_GT", [D, 4, D])
        Z = sb("R_Z", [D, 2, 2, D])
        bank = [ctx.enter_context(nc.psum_tensor(f"R_b{i}", [128, 512], F32)) for i in range(8)]
        pH = bank[0]
        pW = bank[1][:, 0:384].rearrange("p (t c) -> p t c", t=2)
        pN = bank[1][:, 384:512].rearrange("p (t c) -> p t c", t=2)
        pC = bank[2][:, 0:256].rearrange("p (t c) -> p t c", t=2)
        pD = bank[2][0:D, 256:260]
        pO = bank[2][:, 264:392].rearrange("p (t c) -> p t c", t=2)
        pT = bank[3:5]
        pL = [bank[b][:, 0:128] for b in (5, 7)]
        pY = [bank[b][:, 128:256] for b in (5, 7)]
        pX = [bank[b][:, 256:512].rearrange("p (x c) -> p x c", x=2) for b in (5, 7)]
        pZ = bank[6][0:D, 0:256].rearrange("p (n t c) -> p n t c", n=2, t=2)
        pWU = bank[6][:, 256:512].rearrange("p (t c) -> p t c", t=2)
        pR = bank[0][0:D, 0:256]
        pG = bank[0][0:D, 256:512].rearrange("p (n c) -> p n c", n=4)
        (s_hp, s_hid, s_gs, s_wp, s_wa, s_th, s_V, s_g, s_lw, s_cum, s_ex, s_exp, s_el, s_T, s_FT, s_prod, s_mask,
         s_ML, s_X, s_Y, s_Ys, s_pX, s_pN, s_QN, s_pWU, s_WU, s_pRG, s_RG, s_pZ, s_Z, s_pO, s_O, s_dve, s_xl, s_X0, s_dI, s_qn, s_bk) = (
            sem(x) for x in ("hidden", "hidden_copied", "gate_hidden", "lora", "lora_biased", "lora_tanh", "v_copied",
                             "gate_stored", "log_decay", "cumulated", "exclusive", "exponentials", "scaled", "turned",
                             "turned_copied", "products", "masked", "level_masks", "inverse", "inner", "inner_copied",
                             "merge", "nv", "nv_copied", "wu", "wu_copied", "rg", "rg_copied", "state_sum", "state",
                             "out", "out_stored", "token_step", "first_blocks", "first_inverse", "decay_diagonal", "q_copied", "state_factors"))
        block = ctx.enter_context(nc.Block())

        halves = lambda x: x.rearrange("p (s j) c -> p s j c", s=2)
        rkv_, gates_, rn_ = halves(rkv[:, :, :]), halves(gate_[:, :, :]), rn[:, :].rearrange("p (s j) -> p s j", s=2)
        Z2_ = Z2[:, :].rearrange("p (s n) -> p s n", s=2)

        TL = 8

        def wait(eng, s, n):
            if not (isinstance(n, int) and n <= 0):
                eng.wait_ge(s, n)

        def run(eng, step):
            step(-1, 1, inv=False, state=False)
            step(0, 0, state=False)
            step(1, 1)
            step(2, 0)
            with eng.Fori(1, (NIT - 3) // 2) as m:
                step(2 * m + 1, 1)
                step(2 * m + 2, 0)
            step(NIT - 2, 1)
            step(NIT - 1, 0, front=False)
            step(NIT, 1, front=False, inv=False)

        @block.tensor
        def _(pe):
            def hidden(i, p):
                wait(pe, s_hid, i)
                wait(pe, s_RG, i - 2)
                z = Z2_[:, :, bass.ds(128 * i, 128)]
                two = lambda x: x.rearrange("p (s n) -> p s n", s=2)
                pe.matmul(two(pH[:, 0:256]), w["Awa"][:, :], z, start=True, stop=True)
                pe.matmul(two(pH[:, 256:512]), w["Ag"][:, :], z, start=True, stop=True).then_inc(s_hp, 1)

            def lora(i, p):
                pe.wait_ge(s_gs, i + 1)
                wait(pe, s_wa, i)
                wait(pe, s_g, i)
                wait(pe, s_QN, i - 1)
                for t in range(2):
                    pe.matmul(pW[:, t, 0:128], hid[:, t * 128:t * 128 + 128], w["Bwa"][:, :], start=True, stop=True)
                    m = pe.matmul(pW[:, t, 128:192], gh[:, t * 128:t * 128 + 128], w["Bg"][:, :], start=True, stop=True)
                m.then_inc(s_wp, 1)

            def cumulate(i, p):
                pe.wait_ge(s_lw, i + 1)
                wait(pe, s_exp, i)
                wait(pe, s_O, i - 2)
                for t in range(2):
                    for x in range(2):
                        pe.matmul(pC[:, t, x * D:x * D + D], c["tri"][:, x * 128:x * 128 + 128], lw[:, t, :], start=True, stop=True)
                    m = pe.matmul(pD[:, 2 * t:2 * t + 2], lw[:, t, :], c["ind"][:, :], start=True, stop=True)
                m.then_inc(s_cum, 1)

            def turn(i, p):
                pe.wait_ge(s_el, i + 1)
                wait(pe, s_mask, 2 * i)
                for x in range(4):
                    m = pe.transpose(pT[0][:, x * 128:x * 128 + 128], RBK[:, x], c["eye"][:, :])
                m.then_inc(s_T, 1)

            def products(i, p):
                pe.wait_ge(s_FT, 2 * i + 2)
                wait(pe, s_X, 11 * i)
                for t in range(2):
                    F = lambda x, n=1: FT[:, p, t, x * 128:(x + n) * 128]
                    pe.matmul(pT[t][:, 0:256], F(2), F(0, 2), start=True, stop=True)
                    pe.matmul(pT[t][:, 256:512], F(3), F(0, 2), start=True, stop=True)
                    pe.matmul(pL[t], F(0), F(2), start=True, stop=True).then_inc(s_prod, 1)

            def inner(i, p, l):
                pe.wait_ge(s_ML, 5 * i + l)
                if l == 1:
                    pe.wait_ge(s_X0, i + 1)
                for t in range(2):
                    if l > 1:
                        pe.wait_ge(s_X, 11 * i + 1 + 2 * (l - 2) + t + 1)
                    pe.matmul(pY[t], ML[:, l - 1, t, :], XX[:, t, 0, :], start=True, stop=True).then_inc(s_Y, 1)

            def merge(i, p, l):
                if l == 1:
                    pe.wait_ge(s_X, 11 * i + 1)
                for t in range(2):
                    pe.wait_ge(s_Ys, 10 * i + 2 * (l - 1) + t + 1)
                    if l < LEVELS:
                        pe.matmul(pX[t][:, 0, :], XX[:, t, 1, :], Ys[:, t, :], start=True, stop=True)
                    pe.matmul(pX[t][:, 1, :], Ys[:, t, :], XX[:, t, 1, :], start=True, stop=True).then_inc(s_pX, 1)

            def nv(i, p, fronts):
                pe.wait_ge(s_X, 11 * i + 11)
                pe.wait_ge(s_g, fronts)
                pe.wait_ge(s_wa, fronts)
                for t in range(2):
                    m = pe.matmul(pN[:, t, :], PM[:, p, t, 256:384], V[:, p, t, :], start=True, stop=True)
                m.then_inc(s_pN, 1)

            def wu(i, p):
                pe.wait_ge(s_QN, i + 1)
                pe.wait_ge(s_qn, i + 1)
                wait(pe, s_Z, 2 * i + 1)
                for t in range(2):
                    m = pe.matmul(pWU[:, t, :], XT[:, p, t, :], QN[:, p, t, :], start=True, stop=True)
                m.then_inc(s_pWU, 1)

            def rg(i, p, fronts):
                pe.wait_ge(s_WU, i + 1)
                pe.wait_ge(s_hid, fronts)
                pe.wait_ge(s_bk, i + 1)
                for t in range(2):
                    pe.matmul(pR[:, t * 128:t * 128 + 128], WU[:, t, 0:D], PM[:, p, t, 128:256], start=True, stop=True)
                for t in range(2):
                    m = pe.matmul(pG[:, 2 * t:2 * t + 2, :], WU[:, t, 0:D], Bh[:, p, t], start=True, stop=True)
                m.then_inc(s_pRG, 1)

            def out_chunk(i, p, n, fronts):
                if n == 0:
                    pe.wait_ge(s_RG, i + 1)
                    pe.wait_ge(s_exp, fronts)
                    wait(pe, s_O, i)
                pe.wait_ge(s_Z, 2 * i + n + 1)
                for t in range(2):
                    pe.matmul(pZ[:, n, t, :], Kh[:, p, t, n, :], V[:, p, t, :], start=True, stop=False)
                    pe.matmul(pZ[:, n, t, :], Bh[:, p, t, n, :], WU[:, t, D:128], start=False, stop=False)
                    m = pe.matmul(pZ[:, n, t, :], GT[:, 2 * t + n, :], Z[:, 1 - n, t, :], start=False, stop=True)
                m.then_inc(s_pZ, 1)
                for t in range(2):
                    o, r = pO[n * CS:n * CS + CS, t, :], slice(n * CS, n * CS + CS)
                    pe.matmul(o, PM[:, p, t, 384 + n * CS:384 + n * CS + CS], V[:, p, t, :], start=True, stop=False)
                    pe.matmul(o, PM[:, p, t, 128 + n * CS:128 + n * CS + CS], WU[:, t, D:128], start=False, stop=False)
                    m = pe.matmul(o, RpT[:, t * 128 + n * CS:t * 128 + n * CS + CS], Z[:, 1 - n, t, :], start=False, stop=True)
                if n == 1:
                    m.then_inc(s_pO, 1)

            def step(i, p, front=True, inv=True, state=True):
                f, s = (i + 1, 1 - p), (i - 1, 1 - p)
                fronts = i + 2 if front else NIT
                if state: nv(*s, min(i + 1, NIT) if isinstance(i, int) else i + 1)
                if inv: products(i, p)
                if front: hidden(*f)
                if state: wu(*s)
                if inv: inner(i, p, 1)
                if front: lora(*f)
                if inv: merge(i, p, 1)
                if state: rg(*s, fronts)
                if inv: inner(i, p, 2)
                if front: cumulate(*f)
                if inv:
                    merge(i, p, 2)
                    inner(i, p, 3)
                    merge(i, p, 3)
                    inner(i, p, 4)
                if inv: merge(i, p, 4)
                if state: out_chunk(*s, 0, fronts)
                if inv: inner(i, p, 5)
                if front: turn(*f)
                if inv: merge(i, p, 5)
                if state: out_chunk(*s, 1, fronts)

            run(pe, step)

        @block.scalar
        def _(act):
            act.preload_act_table(ACT.Exp)

            def hidden(i, p):
                act.wait_ge(s_hp, i + 1)
                wait(act, s_wp, i)
                act.activation(hid[0:D, :], pH[0:D, 0:256], ACT.Tanh)
                act.activation(hid[D:128, :], pH[D:128, 0:256], ACT.Copy)
                act.activation(gh[:, :], pH[:, 256:512], ACT.Tanh, scale=0.5).then_inc(s_hid, 1)

            def values(i, p):
                wait(act, s_O, i - 1)
                act.activation(V[:, p], rkv_[:, :, i, 2 * D:3 * D], ACT.Copy).then_inc(s_V, 1)

            def tanh(i, p):
                act.wait_ge(s_wa, i + 1)
                wait(act, s_lw, i)
                act.activation(wa[:, :, :], wa[:, :, :], ACT.Tanh, scale=0.5).then_inc(s_th, 1)

            def exps(i, p):
                act.wait_ge(s_ex, i + 1)
                wait(act, s_el, i)
                wait(act, s_bk, i)
                wait(act, s_qn, i)
                wait(act, s_RG, i - 1)
                act.activation(eP[:, :, :], pC[:, :, 0:D], ACT.Exp)
                act.activation(eN[:, :, :], pC[:, :, 0:D], ACT.Exp, scale=-1.0)
                act.activation(eS[:, :, :], pC[:, :, D:128], ACT.Exp)
                act.activation(eX[:, :, :], ex[:, :, :], ACT.Exp)
                act.activation(DC[:, p, :], pD, ACT.Exp).then_inc(s_exp, 1)

            def turned(i, p):
                act.wait_ge(s_T, i + 1)
                wait(act, s_RG, i - 1)
                act.activation(FT[:, p, 0, :], pT[0][0:D, :], ACT.Copy).then_inc(s_FT, 1)

            def inner(i, p, l):
                for t in range(2):
                    act.wait_ge(s_Y, 10 * i + 2 * (l - 1) + t + 1)
                    act.activation(Ys[:, t, :], pY[t], ACT.Copy).then_inc(s_Ys, 1)

            def gates(i, p):
                act.wait_ge(s_wp, i + 1)
                act.activation(gates_[:, :, i, :], pW[:, :, 128:192], ACT.Copy).then_inc(s_g, 1)

            def nv(i, p):
                act.wait_ge(s_pN, i + 1)
                act.activation(QN[:, p, :, D:128], pN[:, :, :], ACT.Copy).then_inc(s_QN, 1)

            def wu(i, p):
                act.wait_ge(s_pWU, i + 1)
                wait(act, s_O, i)
                act.activation(WU[:, :, :], pWU[:, :, :], ACT.Copy, scale=-1.0).then_inc(s_WU, 1)

            def store(i, p):
                act.wait_ge(s_pO, i + 1)
                act.activation(rkv_[:, :, i, 0:D], pO[:, :, :], ACT.Copy).then_inc(s_O, 1)

            def step(i, p, front=True, inv=True, state=True):
                f, s = (i + 1, 1 - p), (i - 1, 1 - p)
                if state: nv(*s)
                if front: hidden(*f)
                if state: wu(*s)
                if inv: inner(i, p, 1)
                if front:
                    tanh(*f)
                    gates(*f)
                if inv:
                    inner(i, p, 2)
                    inner(i, p, 3)
                if front:
                    exps(*f)
                if inv:
                    inner(i, p, 4)
                    inner(i, p, 5)
                if front: turned(*f)
                if state: store(*s)
                if front: values(*f)

            run(act, step)

        @block.gpsimd
        def _(pool):
            def step(i, p, front=True, inv=True, state=True):
                if inv:
                    pool.wait_ge(s_mask, 2 * i + 2)
                    wait(pool, s_X, 11 * i)
                    for l in range(LEVELS):
                        pool.tensor_tensor(ML[:, l], PM[:, p, :, 0:128], rep(c["lev"][:, l * 128:l * 128 + 128], 2), ALU.mult).then_inc(s_ML, 1)
                if front:
                    f, q = i + 1, 1 - p
                    pool.wait_ge(s_exp, f + 1)
                    pool.wait_ge(s_dve, TL * f + 2)
                    wait(pool, s_pWU, f - 1)
                    pool.tensor_tensor(QN[:, q, :, 0:D], kn[:, :, :], eX[:, :, :], ALU.mult).then_inc(s_qn, 1)
            run(pool, step)

        @block.vector
        def _(dve):
            dve.memset(Z[:, 1, :, :], 0.0).then_inc(s_Z, 1)
            for n in range(2):
                r = slice(CS - n * CS, 2 * CS - n * CS)
                dve.memset(Bh[r, :, :, n, :], 0.0)
                dve.memset(Kh[r, :, :, n, :], 0.0)

            def gate(i, p):
                dve.wait_ge(s_hid, i + 1)
                dve.tensor_scalar(gh[:, :], gh[:, :], 0.5, 0.5, ALU.mult, ALU.add).then_inc(s_gs, 1)

            def lora(i, p):
                dve.wait_ge(s_wp, i + 1)
                dve.tensor_tensor(wa[:, :, :], pW[:, :, 0:128], rep(w["bwa"][:, :], 2), ALU.add).then_inc(s_wa, 1)

            def bonus(i, p):
                dve.wait_ge(s_V, i + 1)
                dve.tensor_tensor(rkv_[:, :, i, D:2 * D], V[:, p], bc(rs[:, :], D), ALU.mult)

            def decay(i, p):
                dve.wait_ge(s_th, i + 1)
                dve.tensor_scalar(lw[:, :, :], wa[:, :, 0:D], 0.5 * DECAY, 0.5 * DECAY, ALU.mult, ALU.add)
                dve.tensor_scalar(a_[:, :, :], wa[:, :, D:128], 0.5, 0.5, ALU.mult, ALU.add).then_inc(s_lw, 1)

            def tokens(i, p):
                link = linker(dve, s_dve, i * TL)
                k = rkv_[:, :, i, D:2 * D]
                wait(dve, s_qn, i)
                dve.wait_ge(s_lw, i + 1)
                link(dve.tensor_tensor(kn[:, :, :], k, rep(w["k_k"][:, :], 2), ALU.mult))
                link(dve.tensor_tensor(kn[:, :, :], kn[:, :, :], bc(rn_[:, :, i], D), ALU.mult))
                link(dve.tensor_tensor(bt[:, :, :], kn[:, :, :], a_[:, :, :], ALU.mult))
                link(dve.scalar_tensor_tensor(out=kp[:, :, :], in0=a_[:, :, :], scalar=-1.0, in1=rep(w["k_a"][:, :], 2),
                                              op0=ALU.add, op1=ALU.mult))
                link(dve.scalar_tensor_tensor(out=kp[:, :, :], in0=kp[:, :, :], scalar=1.0, in1=k, op0=ALU.add, op1=ALU.mult))
                assert link.count[0] == 5

            def bonus_sum(i, p):
                link = linker(dve, s_dve, i * TL + 5)
                r = rkv_[:, :, i, 0:D]
                link(dve.tensor_tensor(rk[:, :, :], r, rep(w["r_k"][:, :], 2), ALU.mult))
                link(dve.tensor_tensor(rk[:, :, :], rk[:, :, :], kp[:, :, :], ALU.mult))
                link(dve.tensor_reduce(rs[:, :], rk[:, :, :], AX.X, ALU.add))
                assert link.count[0] == TL - 5

            def exclusive(i, p):
                dve.wait_ge(s_cum, i + 1)
                dve.tensor_tensor(ex[:, :, :], pC[:, :, 0:D], lw[:, :, :], ALU.subtract).then_inc(s_ex, 1)

            def scale(i, p):
                dve.wait_ge(s_exp, i + 1)
                wait(dve, s_T, i)
                dve.tensor_tensor(RBK[:, 0], kn[:, :, :], eX[:, :, :], ALU.mult)
                dve.tensor_tensor(RBK[:, 1], rkv_[:, :, i, 0:D], eP[:, :, :], ALU.mult)
                dve.tensor_tensor(RBK[:, 2], bt[:, :, :], eN[:, :, :], ALU.mult)
                dve.tensor_tensor(RBK[:, 3], kp[:, :, :], eN[:, :, :], ALU.mult).then_inc(s_el, 1)

            def factors(i, p):
                wait(dve, s_O, i - 1)
                for n in range(2):
                    r = slice(n * CS, n * CS + CS)
                    dve.tensor_tensor(Bh[r, p, :, n, :], bt[r, :, :], eS[r, :, :], ALU.mult)
                    m = dve.tensor_tensor(Kh[r, p, :, n, :], kp[r, :, :], eS[r, :, :], ALU.mult)
                m.then_inc(s_bk, 1)

            def turned(i, p):
                dve.wait_ge(s_T, i + 1)
                dve.tensor_copy(FT[:, p, 1, :], pT[0][D:2 * D, :]).then_inc(s_FT, 1)

            def mask(i, p):
                wait(dve, s_O, i - 1)
                for t in range(2):
                    dve.wait_ge(s_prod, 2 * i + t + 1)
                    dve.tensor_tensor(PM[:, p, t, :], pT[t][:, :], c["mask"][:, :], ALU.mult).then_inc(s_mask, 1)
                for t in range(2):
                    m = dve.tensor_tensor(XX[:, t, 0, :], pL[t], c["neg0"][:, 0:128], ALU.mult)
                m.then_inc(s_xl, 1)
                dve.wait_ge(s_mask, 2 * i + 2)
                dve.tensor_tensor(XX[:, :, 1, :], PM[:, p, :, 0:128], rep(c["neg0"][:, 128:256], 2), ALU.mult).then_inc(s_xl, 1)
                dve.wait_ge(s_xl, 2 * i + 1)
                dve.tensor_tensor(XX[:, :, 0, :], XX[:, :, 0, :], rep(c["eye"][:, :], 2), ALU.add).then_inc(s_X0, 1)
                dve.wait_ge(s_xl, 2 * i + 2)
                dve.tensor_tensor(XX[:, :, 1, :], XX[:, :, 1, :], rep(c["eye"][:, :], 2), ALU.add).then_inc(s_X, 1)

            def merged(i, p, l):
                for t in range(2):
                    dve.wait_ge(s_pX, 10 * i + 2 * (l - 1) + t + 1)
                    if l < LEVELS:
                        dve.tensor_tensor(XX[:, t], XX[:, t], pX[t], ALU.subtract).then_inc(s_X, 1)
                    else:
                        dve.tensor_tensor(XT[:, p, t], XX[:, t, 1, :], pX[t][:, 1, :], ALU.subtract).then_inc(s_X, 1)

            def rg(i, p):
                dve.wait_ge(s_exp, i + 1)
                wait(dve, s_pO, i)
                dve.tensor_tensor(GT[:, :, :], rep(c["eye"][0:D, 0:D], 4), bc(DC[:, p, :], D), ALU.mult).then_inc(s_dI, 1)
                dve.wait_ge(s_pRG, i + 1)
                dve.tensor_tensor(RpT[:, :].rearrange("p (t n) -> p t n", t=2), pR.rearrange("p (t n) -> p t n", t=2),
                                  FT[:, p, :, 128:256], ALU.add)
                dve.wait_ge(s_dI, i + 1)
                dve.tensor_tensor(GT[:, :, :], pG, GT[:, :, :], ALU.add).then_inc(s_RG, 1)

            def new_state(i, p, n):
                dve.wait_ge(s_pZ, 2 * i + n + 1)
                dve.tensor_scalar(Z[:, n], pZ[:, n], c["keep"][:, bass.ds(2 * i + n, 1)], None, ALU.mult).then_inc(s_Z, 1)

            def step(i, p, front=True, inv=True, state=True):
                f, s = (i + 1, 1 - p), (i - 1, 1 - p)
                if inv:
                    factors(i, p)
                    bonus(i, p)
                    mask(i, p)
                if front:
                    gate(*f)
                    lora(*f)
                if inv: merged(i, p, 1)
                if front: decay(*f)
                if state: rg(*s)
                if inv: merged(i, p, 2)
                if front:
                    exclusive(*f)
                    tokens(*f)
                if inv: merged(i, p, 3)
                if front: bonus_sum(*f)
                if inv: merged(i, p, 4)
                if front: scale(*f)
                if state: new_state(*s, 0)
                if inv: merged(i, p, 5)
                if front: turned(*f)
                if state: new_state(*s, 1)

            run(dve, step)


def outputs(nc, w, h, hout, rkv, gate_, eye):
    with ExitStack() as ctx:
        sb = lambda name, shape, dt=F32: ctx.enter_context(nc.sbuf_tensor(name, shape, dt))
        sem = lambda name: ctx.enter_context(semaphore(nc, name))
        hin = sb("O_hin", [128, 2, GRP, D])
        xc = sb("O_xc", [128, 2, GRP, D])
        sq = sb("O_sq", [128, 2, GRP, D])
        st = sb("O_st", [128, 2, 4, GRP])
        oT = sb("O_oT", [D, 2, QB])
        ho = sb("O_ho", [128, 2, GRP, D])
        pT = ctx.enter_context(nc.psum_tensor("O_pT", [128, 2, 512], F32))
        pO = ctx.enter_context(nc.psum_tensor("O_pO", [128, 2, 512], F32))
        s_in = [sem(f"O_h_in{k}") for k in range(2)]
        s_st = [sem(f"O_stored{k}") for k in range(2)]
        s_link, s_sqrt, s_T, s_ev, s_p, s_out = (sem("O_" + x) for x in (
            "step", "root", "turned", "turned_copied", "projected", "summed"))
        hv = h.rearrange("(g j p) c -> g p j c", p=128, j=GRP)
        ov = hout.rearrange("(g j p) c -> g p j c", p=128, j=GRP)
        block = ctx.enter_context(nc.Block())

        LINKS = 12
        VAR, GATED = 6, LINKS - 1

        @block.sync
        def _(sp):
            for k in range(2):
                sp.dma_start(hin[:, k], hv[k]).then_inc(s_in[k], 16)
            with sp.Fori(0, NG // 2 - 1) as gg:
                for k in range(2):
                    sp.wait_ge(s_out, 2 * gg + k + 3)
                    sp.dma_start(hin[:, k], hv[2 * gg + 2 + k]).then_inc(s_in[k], 16)
                    sp.dma_start(ov[2 * gg + k], ho[:, k]).then_inc(s_st[k], 16)
            for k in range(2):
                sp.wait_ge(s_out, NG - 2 + k + 3)
                sp.dma_start(ov[NG - 2 + k], ho[:, k]).then_inc(s_st[k], 16)
            for k in range(2):
                sp.wait_ge(s_st[k], 16 * (NG // 2) + 16)

        @block.vector
        def _(dve):
            for k in range(2):
                dve.sem_inc(s_st[k], 16)
            dve.sem_inc(s_out, 2)

            def finish(gg):
                for k in range(2):
                    dve.wait_ge(s_p, 2 * gg + k + 1)
                    dve.wait_ge(s_in[k], 16 * gg + 16)
                    dve.wait_ge(s_st[k], 16 * gg + 16)
                    dve.tensor_tensor(ho[:, k], hin[:, k], pO[:, k, 0:GRP * D].rearrange("p (j c) -> p j c", c=D),
                                      ALU.add).then_inc(s_out, 1)

            def normalize(gg):
                both = pairs(dve, s_link, gg * (2 * LINKS))
                js = lambda k: bass.ds((2 * gg + k) * GRP, GRP)
                S = lambda k, i: st[:, k, i, :]
                both(lambda k: dve.tensor_reduce(S(k, 0), rkv[:, js(k), 0:D], AX.X, ALU.add))
                both(lambda k: dve.tensor_scalar(S(k, 1), S(k, 0), 1.0 / D, None, ALU.mult))
                both(lambda k: dve.tensor_tensor(xc[:, k], rkv[:, js(k), 0:D], bc(S(k, 1), D), ALU.subtract),
                     lambda k: dve.wait_ge(s_T, 2 * gg + k + 1))
                both(lambda k: dve.tensor_tensor(sq[:, k], xc[:, k], xc[:, k], ALU.mult))
                both(lambda k: dve.tensor_reduce(S(k, 2), sq[:, k], AX.X, ALU.add))
                both(lambda k: dve.tensor_scalar(S(k, 2), S(k, 2), 1.0 / D, GN_EPS, ALU.mult, ALU.add))
                both(lambda k: dve.reciprocal(S(k, 3), S(k, 2)))
                both(lambda k: dve.tensor_tensor(xc[:, k], xc[:, k], bc(S(k, 3), D), ALU.mult),
                     lambda k: dve.wait_ge(s_sqrt, 2 * gg + k + 1))
                both(lambda k: dve.tensor_tensor(xc[:, k], xc[:, k], rep(w["gn_w"][:, :], GRP), ALU.mult))
                both(lambda k: dve.tensor_tensor(xc[:, k], xc[:, k], rep(w["gn_b"][:, :], GRP), ALU.add))
                both(lambda k: dve.tensor_tensor(xc[:, k], xc[:, k], rkv[:, js(k), D:2 * D], ALU.add))
                both(lambda k: dve.tensor_tensor(xc[:, k], xc[:, k], gate_[:, js(k), :], ALU.mult))
                assert both.count[0] == LINKS

            normalize(0)
            with dve.Fori(1, NG // 2) as gg:
                normalize(gg)
                finish(gg - 1)
            finish(NG // 2 - 1)

        @block.scalar
        def _(act):
            act.preload_act_table(ACT.Sqrt)
            with act.Fori(0, NG // 2) as gg:
                for k in range(2):
                    g = 2 * gg + k
                    act.wait_ge(s_link, gg * (2 * LINKS) + done(VAR, k))
                    act.activation(st[:, k, 3, :], st[:, k, 3, :], ACT.Sqrt).then_inc(s_sqrt, 1)
                for k in range(2):
                    g = 2 * gg + k
                    act.wait_ge(s_T, g + 3)
                    pair = lambda x: oT[:, k, 0:768].rearrange("p (j x n) -> p x j n", x=2, n=128)[:, x]
                    act.activation(pair(0), pT[0:D, k, 0:384].rearrange("p (j n) -> p j n", n=128), ACT.Copy)
                    act.activation(pair(1), pT[D:128, k, 0:384].rearrange("p (j n) -> p j n", n=128), ACT.Copy)
                    act.activation(oT[:, k, 768:896], pT[0:D, k, 384:512], ACT.Copy).then_inc(s_ev, 1)

        @block.tensor
        def _(pe):
            pe.sem_inc(s_T, 2)
            with pe.Fori(0, NG // 2) as gg:
                for k in range(2):
                    g = 2 * gg + k
                    pe.wait_ge(s_link, gg * (2 * LINKS) + done(GATED, k))
                    for j in range(GRP // 2):
                        pe.transpose(pT[:, k, j * 128:j * 128 + 128], xc[:, k, 2 * j:2 * j + 2, :], eye[:, :])
                    m = pe.transpose(pT[0:D, k, 384:512], xc[:, k, GRP - 1, :], eye[:, :])
                    m.then_inc(s_T, 1)
                    pe.wait_ge(s_ev, g + 1)
                    pe.wait_ge(s_out, g + 1)
                    for j in range(GRP):
                        m = pe.matmul(pO[:, k, j * D:j * D + D], oT[:, k, j * 128:j * 128 + 128], w["Wo"][:, :], start=True, stop=True)
                    m.then_inc(s_p, 1)


def weights(nc, ctx, ins, cst):
    sb = lambda name, shape, dt=F32: ctx.enter_context(nc.sbuf_tensor(name, shape, dt))
    w = {"rkv": sb("W_rkv", [128, 192]), "Awa": sb("W_Awa", [128, 128]), "Ag": sb("W_Ag", [128, 128]),
         "Bwa": sb("W_Bwa", [128, 128]), "Bg": sb("W_Bg", [128, D]), "bwa": sb("W_bwa", [128, 128]),
         "Wo": sb("W_Wo", [D, D])}
    for n in ("k_k", "k_a", "r_k", "gn_w", "gn_b"):
        w[n] = sb("W_" + n, [128, D])
    mix = sb("W_mix", [128, 6])
    shapes = {"tri": [128, 256], "ind": [128, 2], "mask": [128, 512], "neg0": [128, 256], "lev": [128, LEVELS * 128],
              "eye": [128, 128], "keep": [D, NTT]}
    c = {k: sb("K_" + k, v) for k, v in shapes.items()}
    with semaphore(nc, "W_in") as s_in, semaphore(nc, "W_zero") as s_z, semaphore(nc, "W_mixed") as s_m, nc.Block() as block:
        n = [0]

        @block.gpsimd
        def _(pool):
            pool.memset(w["Bwa"][:, :], 0.0).then_inc(s_z, 1)

        @block.sync
        def _(sp):
            def load(dst, src, slow=False):
                n[0] += 16
                sp.dma_start(dst, src, allow_slow_non_contiguous=slow).then_inc(s_in, 16)
            for k in c:
                load(c[k][:, :], cst[k])
            row = lambda a: a.rearrange("(a c) -> a c", a=1).broadcast_to([128, D])
            for p in (0, D):
                load(mix[p:p + D, :], ins["x_mix"].rearrange("i d -> d i"), True)
                for j, k in enumerate(("W_r", "W_k", "W_v")):
                    load(w["rkv"][p:p + D, j * D:j * D + D], ins[k])
                load(w["Awa"][p:p + D, 0:D], ins["A_w"])
                load(w["Awa"][p:p + D, D:128], ins["A_a"])
                load(w["Ag"][p:p + D, :], ins["A_g"])
            load(w["bwa"][:, 0:D], row(ins["b_w"]))
            load(w["bwa"][:, D:128], row(ins["b_a"]))
            load(w["Bg"][:, :], ins["B_g"])
            load(w["Wo"][:, :], ins["W_o"])
            for k in ("k_k", "k_a", "r_k", "gn_w", "gn_b"):
                load(w[k][:, :], row(ins[k]))
            sp.wait_ge(s_z, 1)
            load(w["Bwa"][0:D, 0:D], ins["B_w"])
            load(w["Bwa"][D:128, D:128], ins["B_a"])
            sp.wait_ge(s_in, n[0])

        @block.vector
        def _(dve):
            dve.wait_ge(s_in, n[0])
            dve.tensor_scalar(mix[0:D, :], mix[0:D, :], -1.0, 1.0, ALU.mult, ALU.add).then_inc(s_m, 1)
            dve.wait_ge(s_m, 1)
            for t, col, m in (("rkv", 0, 0), ("rkv", D, 2), ("rkv", 2 * D, 3), ("Awa", 0, 1), ("Awa", D, 4), ("Ag", 0, 5)):
                v = w[t][:, col:col + (128 if t == "Ag" else D)]
                dve.tensor_scalar(v, v, mix[:, m:m + 1], None, ALU.mult)
    return w, c


def tokenizer(nc, x, W1p, b1, W2p, b2p, W3p, b3, hA):
    with ExitStack() as ctx:
        sb = lambda name, shape, dt=F32: ctx.enter_context(nc.sbuf_tensor(name, shape, dt))
        ps = lambda name, shape, dt=F32: ctx.enter_context(nc.psum_tensor(name, shape, dt))
        sem = lambda name: ctx.enter_context(semaphore(nc, name))
        IMGSZ = PAD * PAD
        xa = sb("A_xa", [128, 2, IMGSZ])
        xb = sb("A_xb", [128, 2, IMGSZ])
        w1 = sb("A_w1", [128, NCH, CH])
        w2 = sb("A_w2", [128, NCH * 128])
        w3 = sb("A_w3", [128, NCH, CH])
        b1s = sb("A_b1", [CH, 1])
        b2s = sb("A_b2", [128, NCH])
        b3s = sb("A_b3", [SUB, CH])
        h1 = sb("A_h1", [128, TILE])
        sg = sb("A_sg", [128, NCH, TILE])
        u = sb("A_u", [128, NCH, TILE])
        hst = sb("A_hst", [SUB, 4, CH])
        pc = ps("A_pc", [CH, 512])
        pS = [ps(f"A_pS{q}", [128, 512]) for q in range(NCH)]
        po = ps("A_po", [128, 512])
        s_w = sem("A_weights_in")
        s_zero = sem("A_borders_zero")
        s_zero_a = sem("A_borders_zero_a")
        s_x = [sem(f"A_image_in{k}") for k in range(2)]
        s_conv = sem("A_conv")
        s_relu = sem("A_relu")
        s_gate = sem("A_gate_logits")
        s_sig = sem("A_gates")
        s_u = sem("A_gated")
        s_out = sem("A_out")
        s_ev = sem("A_out_copied")
        s_st = sem("A_stored")
        hA_v = hA.rearrange("(t g p) c -> p t g c", g=4, p=SUB)
        block = ctx.enter_context(nc.Block())

        def view(buf, half, K, t, tap):
            v = buf[0:K, half, :].rearrange("p (r c) -> p r c", c=PAD)
            return v[:, bass.ds(tap[0] + t * ROWS, ROWS), tap[1]:tap[1] + IMG]

        def taps(half, t, whole=False):
            for q in range(NCH):
                tap = TAPS[2 * q]
                K = 128 if q < NCH - 1 or whole else CH
                yield q, K, view(xa if q < 3 else xb, half, K, t, tap)

        @block.sync
        def _(sp):
            sp.dma_start(w1[:, :, :], W1p.rearrange("(q p) c -> p q c", p=128)).then_inc(s_w, 16)
            sp.dma_start(b1s[:, :], b1.rearrange("(c a) -> c a", a=1)).then_inc(s_w, 16)
            sp.dma_start(w2[0:CH, :], W2p).then_inc(s_w, 16)
            sp.dma_start(b2s[:, :], b2p.rearrange("(q p) -> p q", p=128), allow_slow_non_contiguous=True).then_inc(s_w, 16)
            sp.dma_start(w3[:, :, :], W3p.rearrange("(q p) c -> p q c", p=128)).then_inc(s_w, 16)
            sp.dma_start(b3s[:, :], b3.rearrange("(a c) -> a c", a=1).broadcast_to([SUB, CH])).then_inc(s_w, 16)
            def load_image(b):
                for buf, shift in ((xa, 0), (xb, 0), (xa, 1), (xb, PAD)):
                    p0 = 0 if shift == 0 else CH
                    o = PAD + 1 - shift
                    v = buf[p0:p0 + CH, b % 2, o:o + IMG * PAD].rearrange("p (r c) -> p r c", c=PAD)
                    sp.dma_start(v[:, :, 0:IMG], x[b]).then_inc(s_x[b % 2], 16)

            for k in range(2):
                sp.wait_ge(s_zero, k + 1)
                sp.wait_ge(s_zero_a, k + 1)
                load_image(k)
            for b in range(BATCH):
                with sp.Fori(b * NT, b * NT + NT) as n:
                    sp.wait_ge(s_ev, n + 2)
                    sp.dma_start(hA_v[:, n], hst[:, :, :]).then_inc(s_st, 16)
                if b + 2 < BATCH:
                    load_image(b + 2)
            sp.wait_ge(s_st, 16 * BATCH * NT + 16)

        @block.gpsimd
        def _(pool):
            for k in range(2):
                pool.memset(xb[:, k, :], 0.0).then_inc(s_zero, 1)

        @block.tensor
        def _(pe):
            pe.wait_ge(s_w, 96)
            pe.sem_inc(s_ev, 1)
            pe.wait_ge(s_zero_a, 3)

            def conv(half, t):
                for q, K, v in taps(half, t, whole=True):
                    m = pe.matmul(pc[:, 0:TILE], w1[0:K, q, :], v, start=(q == 0), stop=(q == NCH - 1))
                m.then_inc(s_conv, 1)

            def gates(n):
                pe.wait_ge(s_relu, n + 1)
                for q in range(NCH):
                    M = 128 if q < NCH - 1 else CH
                    pe.matmul(pS[q][0:M, 0:TILE], w2[:, q * 128:q * 128 + M], h1[:, :],
                              start=True, stop=True).then_inc(s_gate, 1)

            def out(n):
                pe.wait_ge(s_ev, n + 1)
                pe.wait_ge(s_u, NCH * n + NCH)
                for g in range(4):
                    for q in range(NCH):
                        K = 128 if q < NCH - 1 else CH
                        m = pe.matmul(po[0:SUB, g * CH:(g + 1) * CH], u[0:K, q, g * SUB:(g + 1) * SUB],
                                      w3[0:K, q, :], start=(q == 0), stop=(q == NCH - 1))
                m.then_inc(s_out, 1)

            for b in range(BATCH):
                pe.wait_ge(s_x[b % 2], 64 * (b // 2 + 1))
                conv(b % 2, 0)
                with pe.Fori(0, NT - 1) as t:
                    gates(t + b * NT)
                    conv(b % 2, t + 1)
                    out(t + b * NT)
                gates(b * NT + NT - 1)
                out(b * NT + NT - 1)

        @block.scalar
        def _(act):
            act.wait_ge(s_w, 96)
            act.preload_act_table(ACT.Sigmoid)
            with act.Fori(0, BATCH * NT) as n:
                act.wait_ge(s_conv, n + 1)
                act.activation(h1[0:CH, :], pc[:, 0:TILE], ACT.Relu, bias=b1s[:, 0:1]).then_inc(s_relu, 1)
                for q in range(NCH):
                    M = 128 if q < NCH - 1 else CH
                    act.wait_ge(s_gate, n * NCH + q + 1)
                    act.activation(sg[0:M, q, :], pS[q][0:M, 0:TILE], ACT.Sigmoid,
                                   bias=b2s[0:M, q:q + 1]).then_inc(s_sig, 1)

        @block.vector
        def _(dve):
            for k in range(2):
                dve.memset(xa[:, k, :], 0.0).then_inc(s_zero_a, 1)
            dve.memset(w2[CH:128, :], 0.0)
            dve.memset(h1[CH:128, :], 0.0).then_inc(s_zero_a, 1)
            dve.wait_ge(s_w, 96)
            dve.sem_inc(s_st, 16)
            for b in range(BATCH):
                dve.wait_ge(s_x[b % 2], 64 * (b // 2 + 1))
                with dve.Fori(0, NT) as t:
                    n = t + b * NT
                    for q, K, v in taps(b % 2, t):
                        dve.wait_ge(s_sig, (t + b * NT) * NCH + q + 1)
                        dve.tensor_tensor(u[0:K, q, :].rearrange("p (r c) -> p r c", c=IMG),
                                          sg[0:K, q, :].rearrange("p (r c) -> p r c", c=IMG),
                                          v, ALU.mult).then_inc(s_u, 1)
                    dve.wait_ge(s_out, n + 1)
                    dve.wait_ge(s_st, n * 16 + 16)
                    dve.tensor_tensor(hst[:, :, :], po[0:SUB, 0:4 * CH].rearrange("p (g c) -> p g c", c=CH),
                                      b3s[:, :].rearrange("p (a c) -> p a c", a=1).broadcast_to([SUB, 4, CH]), ALU.add).then_inc(s_ev, 1)


def moe_constants():
    e = np.arange(EX)
    tok = np.arange(NTT)[None] * 128 + np.arange(128)[:, None]
    s, t = np.meshgrid(np.arange(128), np.arange(128), indexing="ij")
    c = {"less": np.tile((e[None] < e[:, None]).reshape(1, -1), (128, 1)),
         "base": np.tile(e[None] * CAP, (128, 1)),
         "dump": EX * CAP + tok,
         "upto": np.concatenate([s <= t, np.ones((128, 128))], 1)}
    return {k: np.ascontiguousarray(v.astype(np.float32)) for k, v in c.items()}


def layer_norm(nc, pre, h, XT, eye, rows=None):
    with ExitStack() as ctx:
        sb = lambda name, shape, dt=F32: ctx.enter_context(nc.sbuf_tensor(pre + name, shape, dt))
        sem = lambda name: ctx.enter_context(semaphore(nc, pre + name))
        hin = sb("hin", [128, 2, GRP, D])
        xc = sb("xc", [128, 2, GRP, D])
        sq = sb("sq", [128, 2, GRP, D])
        st = sb("st", [128, 2, 4, GRP])
        pT = ctx.enter_context(nc.psum_tensor(pre + "pT", [128, 2, 512], F32))
        s_in = [sem(f"h_in{k}") for k in range(2)]
        s_link, s_sqrt, s_T, s_ev = (sem(x) for x in (
            "step", "root", "transposed", "features"))
        hv = h.rearrange("(g p j) c -> g p j c" if rows is None else "(g j p) c -> g p j c", p=128, j=GRP)
        block = ctx.enter_context(nc.Block())

        LINKS = 8 if rows is None else 9
        CENTERED, VAR, NORMED = 2, 6, LINKS - 1

        @block.sync
        def _(sp):
            for k in range(2):
                sp.dma_start(hin[:, k], hv[k]).then_inc(s_in[k], 16)
            with sp.Fori(0, NG // 2 - 1) as g:
                for k in range(2):
                    sp.wait_ge(s_link, g * (2 * LINKS) + done(CENTERED, k))
                    sp.dma_start(hin[:, k], hv[2 * g + 2 + k]).then_inc(s_in[k], 16)

        @block.vector
        def _(dve):
            with dve.Fori(0, NG // 2) as gg:
                both = pairs(dve, s_link, gg * (2 * LINKS))
                S = lambda k, i: st[:, k, i, :]
                both(lambda k: dve.tensor_reduce(S(k, 0), hin[:, k], AX.X, ALU.add),
                     lambda k: dve.wait_ge(s_in[k], 16 * gg + 16))
                both(lambda k: dve.tensor_scalar(S(k, 1), S(k, 0), 1.0 / D, None, ALU.mult))
                both(lambda k: dve.tensor_tensor(xc[:, k], hin[:, k], bc(S(k, 1), D), ALU.subtract),
                     lambda k: dve.wait_ge(s_T, 2 * gg + k + 1))
                both(lambda k: dve.tensor_tensor(sq[:, k], xc[:, k], xc[:, k], ALU.mult))
                both(lambda k: dve.tensor_reduce(S(k, 2), sq[:, k], AX.X, ALU.add))
                both(lambda k: dve.tensor_scalar(S(k, 2), S(k, 2), 1.0 / D, LN_EPS, ALU.mult, ALU.add))
                both(lambda k: dve.reciprocal(S(k, 3), S(k, 2)))
                if rows is not None:
                    both(lambda k: dve.tensor_tensor(rows[:, bass.ds((2 * gg + k) * GRP, GRP), :], xc[:, k], bc(S(k, 3), D), ALU.mult),
                         lambda k: dve.wait_ge(s_sqrt, 2 * gg + k + 1))
                both(lambda k: dve.tensor_tensor(xc[:, k], xc[:, k], bc(S(k, 3), D), ALU.mult),
                     lambda k: dve.wait_ge(s_sqrt, 2 * gg + k + 1))
                assert both.count[0] == LINKS

        @block.tensor
        def _(pe):
            pe.sem_inc(s_T, 2)
            with pe.Fori(0, NG // 2) as gg:
                for k in range(2):
                    g = 2 * gg + k
                    pe.wait_ge(s_link, gg * (2 * LINKS) + done(NORMED, k))
                    pe.wait_ge(s_ev, g + 1)
                    for j in range(GRP // 2):
                        pe.transpose(pT[:, k, j * 128:j * 128 + 128], xc[:, k, 2 * j:2 * j + 2, :], eye[:, :])
                    pe.transpose(pT[0:D, k, 384:512], xc[:, k, GRP - 1, :], eye[:, :]).then_inc(s_T, 1)

        @block.scalar
        def _(act):
            act.preload_act_table(ACT.Sqrt)
            act.sem_inc(s_ev, 2)
            with act.Fori(0, NG // 2) as gg:
                for k in range(2):
                    g = 2 * gg + k
                    act.wait_ge(s_link, gg * (2 * LINKS) + done(VAR, k))
                    act.activation(st[:, k, 3, :], st[:, k, 3, :], ACT.Sqrt).then_inc(s_sqrt, 1)
                for k in range(2):
                    g = 2 * gg + k
                    act.wait_ge(s_T, g + 3)
                    z = XT[0:D, bass.ds(g * QB, QB)]
                    pair = lambda x: z[:, 0:768].rearrange("p (j x n) -> p x j n", x=2, n=128)[:, x]
                    act.activation(pair(0), pT[0:D, k, 0:384].rearrange("p (j n) -> p j n", n=128), ACT.Copy)
                    act.activation(pair(1), pT[D:128, k, 0:384].rearrange("p (j n) -> p j n", n=128), ACT.Copy)
                    act.activation(z[:, 768:896], pT[0:D, k, 384:512], ACT.Copy).then_inc(s_ev, 1)


def gating(nc, pre, XT, wg, gb, less, top, cw, chosen=None):
    with ExitStack() as ctx:
        sb = lambda name, shape, dt=F32: ctx.enter_context(nc.sbuf_tensor(pre + name, shape, dt))
        sem = lambda name: ctx.enter_context(semaphore(nc, pre + name))
        xs = sb("xs", [D, 2, QB])
        lg = sb("lg", [128, 2, GRP, EX])
        st = sb("st", [128, 2, 3, GRP])
        gt = sb("gt", [128, 2, GRP, EX, EX])
        eq = sb("eq", [128, 2, GRP, EX, EX])
        sel = sb("sel", [128, 2, GRP, EX])
        pL = ctx.enter_context(nc.psum_tensor(pre + "pL", [128, 2, 512], F32))
        s_xs, s_p, s_e, s_link = (sem(x) for x in ("moved", "logits", "exp", "step"))
        block = ctx.enter_context(nc.Block())

        LINKS = 13 if chosen is None else 14
        SHIFTED = 2

        @block.scalar
        def _(act):
            act.preload_act_table(ACT.Exp)
            with act.Fori(0, NG // 2) as gg:
                for k in range(2):
                    g = 2 * gg + k
                    act.wait_ge(s_p, g + 1)
                    act.activation(xs[:, k, :], XT[0:D, bass.ds(g * QB, QB)], ACT.Copy).then_inc(s_xs, 1)
                for k in range(2):
                    act.wait_ge(s_link, gg * (2 * LINKS) + done(SHIFTED, k))
                    act.activation(lg[:, k], lg[:, k], ACT.Exp).then_inc(s_e, 1)

        @block.tensor
        def _(pe):
            pe.sem_inc(s_p, 2)
            with pe.Fori(0, NG // 2) as gg:
                for k in range(2):
                    g = 2 * gg + k
                    pe.wait_ge(s_xs, g + 1)
                    for j in range(GRP):
                        m = pe.matmul(pL[:, k, j * EX:j * EX + EX], xs[:, k, j * 128:j * 128 + 128], wg, start=True, stop=True)
                    m.then_inc(s_p, 1)

        @block.vector
        def _(dve):
            with dve.Fori(0, NG // 2) as gg:
                both = pairs(dve, s_link, gg * (2 * LINKS))
                js = lambda k: bass.ds((2 * gg + k) * GRP, GRP)
                own = lambda k: lg[:, k].rearrange("p j (e a) -> p j e a", a=1).broadcast_to([128, GRP, EX, EX])
                other = lambda k: lg[:, k].rearrange("p j (a e) -> p j a e", a=1).broadcast_to([128, GRP, EX, EX])
                lower = less.rearrange("p (a e f) -> p a e f", a=1, e=EX).broadcast_to([128, GRP, EX, EX])
                both(lambda k: dve.tensor_tensor(lg[:, k], pL[:, k, 0:GRP * EX].rearrange("p (j e) -> p j e", e=EX), rep(gb, GRP), ALU.add),
                     lambda k: dve.wait_ge(s_p, 2 * gg + k + 3))
                both(lambda k: dve.tensor_reduce(st[:, k, 0, :], lg[:, k], AX.X, ALU.max))
                both(lambda k: dve.tensor_tensor(lg[:, k], lg[:, k], bc(st[:, k, 0, :], EX), ALU.subtract))
                both(lambda k: dve.tensor_reduce(st[:, k, 1, :], lg[:, k], AX.X, ALU.add),
                     lambda k: dve.wait_ge(s_e, 2 * gg + k + 1))
                both(lambda k: dve.reciprocal(st[:, k, 2, :], st[:, k, 1, :]))
                both(lambda k: dve.tensor_tensor(lg[:, k], lg[:, k], bc(st[:, k, 2, :], EX), ALU.mult))
                both(lambda k: dve.tensor_tensor(gt[:, k], other(k), own(k), ALU.is_gt))
                both(lambda k: dve.tensor_tensor(eq[:, k], other(k), own(k), ALU.is_equal))
                both(lambda k: dve.tensor_tensor(eq[:, k], eq[:, k], lower, ALU.mult))
                both(lambda k: dve.tensor_tensor(gt[:, k], gt[:, k], eq[:, k], ALU.add))
                both(lambda k: dve.tensor_reduce(sel[:, k], gt[:, k], AX.X, ALU.add))
                both(lambda k: dve.tensor_scalar(sel[:, k], sel[:, k], float(top), None, ALU.is_lt))
                if chosen is not None:
                    both(lambda k: dve.tensor_copy(chosen[:, js(k), :], sel[:, k]))
                both(lambda k: dve.tensor_tensor(cw[:, js(k), :], lg[:, k], sel[:, k], ALU.mult))
                assert both.count[0] == LINKS
                dve.wait_ge(s_link, gg * (2 * LINKS) + done(LINKS - 1, 1))


def experts_dense(nc, h, hout, XT, cw, w, eye):
    with ExitStack() as ctx:
        sb = lambda name, shape, dt=F32: ctx.enter_context(nc.sbuf_tensor("C_" + name, shape, dt))
        ps = lambda name, shape, dt=F32: ctx.enter_context(nc.psum_tensor("C_" + name, shape, dt))
        sem = lambda name: ctx.enter_context(semaphore(nc, "C_" + name))
        G = sb("G", [128, 2, EX, QB])
        cs = sb("cs", [128, 2, GRP, EX])
        cT = sb("cT", [GRP * EX, 2, 128])
        pr = sb("pr", [128, 2, EX, D])
        acc = sb("acc", [128, GRP, D])
        hin = sb("hin", [128, 2, GRP, D])
        ho = sb("ho", [128, 2, GRP, D])
        pH = ps("pH", [128, 4, 512])
        pY = ps("pY", [128, 2, 512])
        pB = ps("pB", [128, 512])
        pC = ps("pC", [GRP * EX, 512])
        s_in = [sem(f"h_in{k}") for k in range(2)]
        s_st = [sem(f"stored{k}") for k in range(2)]
        s_h, s_G, s_y, s_pr, s_red, s_cs, s_cT, s_cTs, s_b, s_acc, s_out = (sem(x) for x in (
            "hidden", "gelu", "products", "weighted", "summed", "weights_moved", "weights_turned", "weights_copied",
            "bias", "accumulated", "out"))
        hv = h.rearrange("(g p j) c -> g p j c", p=128, j=GRP)
        ov = hout.rearrange("(g p j) c -> g p j c", p=128, j=GRP)
        block = ctx.enter_context(nc.Block())

        @block.sync
        def _(sp):
            for k in range(2):
                sp.dma_start(hin[:, k], hv[k]).then_inc(s_in[k], 16)
            with sp.Fori(0, NG // 2 - 1) as gg:
                for k in range(2):
                    sp.wait_ge(s_out, 2 * gg + k + 1)
                    sp.dma_start(hin[:, k], hv[2 * gg + 2 + k]).then_inc(s_in[k], 16)
                    sp.dma_start(ov[2 * gg + k], ho[:, k]).then_inc(s_st[k], 16)
            for k in range(2):
                sp.wait_ge(s_out, NG - 2 + k + 1)
                sp.dma_start(ov[NG - 2 + k], ho[:, k]).then_inc(s_st[k], 16)
            for k in range(2):
                sp.wait_ge(s_st[k], 16 * (NG // 2) + 16)

        @block.tensor
        def _(pe):
            pe.sem_inc(s_G, 4)
            pe.sem_inc(s_pr, 2)

            def hidden(g, k, e):
                for half in range(2):
                    u = g * (2 * EX) + 2 * e + half
                    pe.wait_ge(s_G, u + 1)
                    pe.matmul(pH[:, (2 * e + half) % 4, 0:QH], w["W1"][:, e, :], XT[:, bass.ds(g * QB + half * QH, QH)],
                              start=True, stop=True).then_inc(s_h, 1)

            def tile(g, k, j):
                if j == 0:
                    pe.wait_ge(s_G, g * (2 * EX) + 2 * EX + 4)
                pe.wait_ge(s_pr, g * GRP + j + 1)
                y = (k + j) % 2
                for e in range(EX):
                    m = pe.matmul(pY[:, y, e * D:e * D + D], G[:, k, e, j * 128:j * 128 + 128], w["W2"][:, e, :],
                                  start=True, stop=True)
                m.then_inc(s_y, 1)

            def turn_weights(g, k):
                pe.wait_ge(s_cs, g + 1)
                if not (isinstance(g, int) and g == 0):
                    pe.wait_ge(s_cTs, g)
                pe.matmul(pC[:, 0:128], cs[:, k].rearrange("p j e -> p (j e)"), eye[:, :], start=True, stop=True).then_inc(s_cT, 1)

            def bias(g, k):
                pe.wait_ge(s_cTs, g + 1)
                if not (isinstance(g, int) and g == 0):
                    pe.wait_ge(s_acc, g)
                pe.matmul(pB[:, 0:GRP * D], cT[:, k, :], w["b2"][:, :], start=True, stop=True).then_inc(s_b, 1)

            def step(g, k, ahead=True, out=True):
                for e in range(EX):
                    if ahead: hidden(g + 1, 1 - k, e)
                    if out and e < GRP: tile(g, k, e)
                    if out and e == GRP - 3: turn_weights(g, k)
                    if out and e == EX - 1: bias(g, k)

            step(-1, 1, out=False)
            step(0, 0)
            step(1, 1)
            with pe.Fori(1, (NG - 2) // 2) as m:
                step(2 * m, 0)
                step(2 * m + 1, 1)
            step(NG - 2, 0)
            step(NG - 1, 1, ahead=False)

        @block.scalar
        def _(act):
            act.preload_act_table(ACT.Gelu)

            def step(g, k, ahead=True, out=True):
                f, q = g + 1, 1 - k
                if ahead and not (isinstance(g, int) and g <= 0):
                    act.wait_ge(s_y, g * GRP)
                for e in range(EX):
                    for half in range(2):
                        if ahead:
                            act.wait_ge(s_h, f * (2 * EX) + 2 * e + half + 1)
                            act.activation(G[:, q, e, half * QH:half * QH + QH], pH[:, (2 * e + half) % 4, 0:QH],
                                           ACT.Gelu, bias=w["b1"][:, e:e + 1]).then_inc(s_G, 1)
                    if out and e == GRP - 1:
                        act.wait_ge(s_cT, g + 1)
                        act.activation(cT[:, k, :], pC[:, 0:128], ACT.Copy).then_inc(s_cTs, 1)

            step(-1, 1, out=False)
            step(0, 0)
            step(1, 1)
            with act.Fori(1, (NG - 2) // 2) as m:
                step(2 * m, 0)
                step(2 * m + 1, 1)
            step(NG - 2, 0)
            step(NG - 1, 1, ahead=False)

        @block.vector
        def _(dve):
            for k in range(2):
                dve.sem_inc(s_st[k], 16)
            with dve.Fori(0, NG // 2) as gg:
                for k in range(2):
                    g = 2 * gg + k
                    dve.wait_ge(s_st[k], 16 * gg + 16)
                    dve.tensor_copy(cs[:, k], cw[:, bass.ds(g * GRP, GRP), :]).then_inc(s_cs, 1)
                    dve.wait_ge(s_cs, g + 1)
                    for j in range(GRP):
                        y = (k + j) % 2
                        dve.wait_ge(s_y, g * GRP + j + 1)
                        cb = cs[:, k, j, :].rearrange("p (e a) -> p e a", a=1).broadcast_to([128, EX, D])
                        dve.tensor_tensor(pr[:, y], pY[:, y, :].rearrange("p (e c) -> p e c", e=EX), cb, ALU.mult).then_inc(s_pr, 1)
                        dve.wait_ge(s_pr, g * GRP + j + 3)
                        dve.tensor_reduce(acc[:, j, :], pr[:, y].rearrange("p e c -> p c e"), AX.X, ALU.add).then_inc(s_red, 1)
                    dve.wait_ge(s_red, g * GRP + GRP)
                    dve.wait_ge(s_b, g + 1)
                    dve.tensor_tensor(acc[:, :, :], acc[:, :, :], pB[:, 0:GRP * D].rearrange("p (j c) -> p j c", c=D),
                                      ALU.add).then_inc(s_acc, 1)
                    dve.wait_ge(s_acc, g + 1)
                    dve.wait_ge(s_in[k], 16 * gg + 16)
                    dve.tensor_tensor(ho[:, k], hin[:, k], acc[:, :, :], ALU.add).then_inc(s_out, 1)


def moe1_weights(nc, ctx, ins, cst):
    sb = lambda name, shape, dt=F32: ctx.enter_context(nc.sbuf_tensor("CW_" + name, shape, dt))
    w = {"gate": sb("gate", [D, EX]), "gb": sb("gb", [128, EX]), "W1": sb("W1", [128, EX, F1]), "b1": sb("b1", [F1, EX]),
         "W2": sb("W2", [F1, EX, D]), "b2": sb("b2", [GRP * EX, GRP * D]), "less": sb("less", [128, EX * EX])}
    n = [0]
    with semaphore(nc, "CW_in") as s_in, semaphore(nc, "CW_zero") as s_z, nc.Block() as block:
        @block.gpsimd
        def _(pool):
            pool.memset(w["W1"][D:128, :, :], 0.0)
            pool.memset(w["b2"][:, :], 0.0).then_inc(s_z, 1)

        @block.sync
        def _(sp):
            def load(dst, src, slow=False):
                n[0] += 16
                sp.dma_start(dst, src, allow_slow_non_contiguous=slow).then_inc(s_in, 16)
            load(w["less"][:, :], cst["less"])
            load(w["gate"][:, :], ins["gate_w"])
            load(w["gb"][:, :], ins["gate_b"].rearrange("(a c) -> a c", a=1).broadcast_to([128, EX]))
            load(w["W1"][0:D, :, :], ins["W1"].rearrange("e d f -> d e f"))
            load(w["b1"][:, :], ins["b1"].rearrange("e f -> f e"), True)
            load(w["W2"][:, :, :], ins["W2"].rearrange("e f d -> f e d"))
            sp.wait_ge(s_z, 1)
            for j in range(GRP):
                load(w["b2"][j * EX:j * EX + EX, j * D:j * D + D], ins["b2"])
            sp.wait_ge(s_in, n[0])
    return w


def slots(nc, c, chosen, cw, dest, src, wt):
    N = NTT * EX
    with ExitStack() as ctx:
        sb = lambda name, shape, dt=F32: ctx.enter_context(nc.sbuf_tensor("S_" + name, shape, dt))
        sem = lambda name: ctx.enter_context(semaphore(nc, "S_" + name))
        cnt = sb("cnt", [128, NTT, EX])
        tot = sb("tot", [128, NTT, EX])
        run_ = sb("run", [128, NTT, EX])
        one = sb("one", [128, NTT])
        T = sb("T", [128, NTT])
        B = sb("B", [128, NTT])
        kept = sb("kept", [128, NTT])
        df = sb("df", [128, NTT])
        sf = sb("sf", [128, NTT])
        pI = ctx.enter_context(nc.psum_tensor("S_pI", [128, 4, 512], F32))
        s_p, s_l = sem("counted"), sem("step")
        block = ctx.enter_context(nc.Block())
        flat = chosen[:, :, :].rearrange("p j e -> p (j e)")

        @block.tensor
        def _(pe):
            for x in range(2):
                for half in range(2):
                    m = pe.matmul(pI[:, 2 * x + half, 0:N // 2], c["upto"][:, x * 128:x * 128 + 128],
                                  flat[:, half * (N // 2):(half + 1) * (N // 2)], start=True, stop=True)
            m.then_inc(s_p, 1)

        @block.vector
        def _(dve):
            link = linker(dve, s_l)
            dve.wait_ge(s_p, 1)
            v = lambda t: t[:, :, :].rearrange("p (x j) e -> p x (j e)", x=2)
            link(dve.tensor_copy(v(cnt), pI[:, 0:2, 0:N // 2]))
            link(dve.tensor_copy(v(tot), pI[:, 2:4, 0:N // 2]))
            link(dve.memset(one[:, :], 1.0))
            for e in range(EX):
                m = dve.tensor_tensor_scan(run_[:, :, e], one[:, :], tot[:, :, e], 0.0, ALU.mult, ALU.add)
            link(m)
            link(dve.tensor_tensor(run_[:, :, :], run_[:, :, :], tot[:, :, :], ALU.subtract))
            link(dve.tensor_tensor(cnt[:, :, :], cnt[:, :, :], run_[:, :, :], ALU.add))
            link(dve.tensor_tensor(cnt[:, :, :], cnt[:, :, :], chosen[:, :, :], ALU.mult))
            link(dve.tensor_reduce(T[:, :], cnt[:, :, :], AX.X, ALU.add))
            link(dve.tensor_tensor(tot[:, :, :], chosen[:, :, :], rep(c["base"][:, :], NTT), ALU.mult))
            link(dve.tensor_reduce(B[:, :], tot[:, :, :], AX.X, ALU.add))
            link(dve.tensor_scalar(kept[:, :], T[:, :], CAP + 0.5, None, ALU.is_lt))
            link(dve.tensor_reduce(wt[:, :], cw[:, :, :], AX.X, ALU.add))
            link(dve.tensor_tensor(wt[:, :], wt[:, :], kept[:, :], ALU.mult))
            link(dve.scalar_tensor_tensor(out=df[:, :], in0=T[:, :], scalar=-1.0, in1=B[:, :], op0=ALU.add, op1=ALU.add))
            link(dve.tensor_tensor(df[:, :], df[:, :], c["dump"][:, :], ALU.subtract))
            link(dve.tensor_tensor(df[:, :], df[:, :], kept[:, :], ALU.mult))
            link(dve.tensor_tensor(df[:, :], df[:, :], c["dump"][:, :], ALU.add))
            link(dve.tensor_scalar(sf[:, :], T[:, :], -1.0, float(CAP - 1), ALU.add, ALU.min))
            link(dve.tensor_tensor(sf[:, :], sf[:, :], B[:, :], ALU.add))
            link(dve.tensor_copy(dest[:, :], df[:, :]))
            link(dve.tensor_copy(src[:, :], sf[:, :]))


def dispatch(nc, rows, dest, buf):
    with ExitStack() as ctx:
        z = ctx.enter_context(nc.sbuf_tensor("X_zero", [SR, CAP // SR * D], F32))
        s_z, s_zero, s_sent = (ctx.enter_context(semaphore(nc, "X_" + x)) for x in ("zeros", "cleared", "sent"))
        block = ctx.enter_context(nc.Block())

        @block.vector
        def _(dve):
            dve.memset(z[:, :], 0.0).then_inc(s_z, 1)

        @block.sync
        def _(sp):
            sp.wait_ge(s_z, 1)
            bv = buf[0:EX * CAP, :].rearrange("(e p r) c -> e p (r c)", e=EX, p=SR)
            for e in range(EX):
                sp.dma_start(bv[e], z[:, :]).then_inc(s_zero, 16)
            sp.wait_ge(s_zero, 16 * EX)

        @block.gpsimd
        def _(pool):
            pool.wait_ge(s_zero, 16 * EX)
            for j in range(NTT):
                pool.indirect_dma_start(buf, bass.IndirectOffsetOnAxis(ap=dest[:, j:j + 1], axis=0), rows[:, j, :], None).then_inc(s_sent, 16)
            pool.wait_ge(s_sent, 16 * NTT)


def experts_sparse(nc, ins, buf, ybuf, eye):
    NU = EX * CU
    XB = 4
    with ExitStack() as ctx:
        sb = lambda name, shape, dt=F32: ctx.enter_context(nc.sbuf_tensor("E_" + name, shape, dt))
        ps = lambda name, shape, dt=F32: ctx.enter_context(nc.psum_tensor("E_" + name, shape, dt))
        sem = lambda name: ctx.enter_context(semaphore(nc, "E_" + name))
        w1 = sb("w1", [128, 2, F2])
        w2 = sb("w2", [128, 2, 2, D])
        b1 = sb("b1", [128, 2, 2])
        b2 = sb("b2", [SR, 2, D])
        xin = sb("xin", [SR, XB, ST, D])
        xT = sb("xT", [128, 2, UT])
        hid = sb("hid", [128, 2, 2, UT])
        y = sb("y", [SR, 2, ST, D])
        pT = ps("pT", [128, 2, 512])
        pH = ps("pH", [128, 2, 2, 512])
        pY = ps("pY", [128, 2, 512])
        s_w = [sem(f"weights_in{k}") for k in range(2)]
        s_x = [sem(f"rows_in{k}") for k in range(XB)]
        s_z = sem("zero_rows")
        s_st = [sem(f"stored{k}") for k in range(2)]
        s_T, s_xT, s_h, s_ra, s_rd, s_y, s_out = (sem(x) for x in (
            "turned", "features", "hidden", "relu_act", "relu_dve", "products", "out"))
        bv = buf[0:EX * CAP, :].rearrange("(u p s) c -> u p s c", p=SR, s=ST)
        yv = ybuf.rearrange("(u p s) c -> u p s c", p=SR, s=ST)
        w1v = ins["w1"].rearrange("e d f -> e d f")
        w2v = ins["w2"].rearrange("e (x f) d -> e f x d", x=2)
        b1v = ins["b1"].rearrange("e (x f) -> e f x", x=2)
        block = ctx.enter_context(nc.Block())

        def wait(eng, s, n):
            if not (isinstance(n, int) and n <= 0):
                eng.wait_ge(s, n)

        def run(eng, step):
            step(-1, 7, mid=False, back=False)
            step(0, 0, back=False)
            for u in range(1, 8):
                step(u, u)
            with eng.Fori(1, EX // 2 - 1) as m:
                for q in range(8):
                    step(8 * m + q, q)
            for q in range(7):
                step(NU - 8 + q, q)
            step(NU - 1, 7, front=False)
            step(NU, 0, front=False, mid=False)

        @block.sync
        def _(sp):
            def load_w(e, k):
                sp.dma_start(w1[0:D, k, :], w1v[e]).then_inc(s_w[k], 16)
                sp.dma_start(w2[:, k], w2v[e]).then_inc(s_w[k], 16)
                sp.dma_start(b1[:, k, :], b1v[e], allow_slow_non_contiguous=True).then_inc(s_w[k], 16)
                sp.dma_start(b2[:, k, :], ins["b2"][e:e + 1, :].broadcast_to([SR, D]) if isinstance(e, int)
                             else ins["b2"][bass.ds(e, 1), :].broadcast_to([SR, D])).then_inc(s_w[k], 16)
            def unit(u, q, load=True, store=True):
                if load:
                    sp.wait_ge(s_T, u + 1)
                    sp.dma_start(xin[:, q % XB], bv[u + XB]).then_inc(s_x[q % XB], 16)
                if store:
                    sp.wait_ge(s_out, u - 1)
                    sp.dma_start(yv[u - 2], y[:, q % 2]).then_inc(s_st[q % 2], 16)

            load_w(0, 0)
            for k in range(XB):
                sp.dma_start(xin[:, k], bv[k]).then_inc(s_x[k], 16)
            load_w(1, 1)
            for q in range(8):
                unit(q, q, store=q >= 2)
                if q == 6:
                    load_w(2, 0)
            with sp.Fori(1, EX // 2 - 1) as m:
                for q in range(8):
                    unit(8 * m + q, q)
                    if q % 4 == 2:
                        load_w(2 * m + q // 4 + 1, (q // 4 + 1) % 2)
            for q in range(8):
                unit(NU - 8 + q, q, load=q < 8 - XB)
                if q == 2:
                    load_w(EX - 1, 1)
            for q in range(2):
                unit(NU + q, q, load=False)
            for k in range(2):
                sp.wait_ge(s_st[k], 16 * (NU // 2) + 16)

        @block.tensor
        def _(pe):
            def turn(u, q):
                k = q % 2
                wait(pe, s_xT, u - 1)
                x = q % XB
                if isinstance(u, int):
                    pe.wait_ge(s_x[x], 16 * (u // XB) + 16)
                else:
                    pe.wait_ge(s_x[x], (u - q) * (16 // XB) + 16 * (q // XB) + 16)
                for s in range(ST // 2):
                    pe.transpose(pT[:, k, s * SR:s * SR + SR], xin[:, x, 2 * s:2 * s + 2, :], eye[0:SR, 0:SR])
                pe.transpose(pT[0:D, k, 2 * SR:3 * SR], xin[:, x, ST - 1, :], eye[0:SR, 0:SR]).then_inc(s_T, 1)

            def hidden(u, q):
                k, kw = q % 2, q // 4
                pe.wait_ge(s_xT, u + 1)
                if isinstance(u, int) and u == 0:
                    pe.wait_ge(s_z, 1)
                wait(pe, s_ra, u - 1)
                wait(pe, s_rd, u - 1)
                if q % 4 == 0:
                    pe.wait_ge(s_w[kw], 64 * (u // 8) + 64 if isinstance(u, int) else (u - q) * 8 + 64)
                for f in range(2):
                    pe.matmul(pH[:, k, f, 0:UT], w1[:, kw, f * 128:f * 128 + 128], xT[:, k, :], start=True, stop=True).then_inc(s_h, 1)

            def multiply(u, q):
                k, kw = q % 2, q // 4
                pe.wait_ge(s_ra, u + 1)
                pe.wait_ge(s_rd, u + 1)
                wait(pe, s_out, u - 1)
                for s in range(ST):
                    for f in range(2):
                        m = pe.matmul(pY[0:SR, k, s * D:s * D + D], hid[:, k, f, s * SR:s * SR + SR], w2[:, kw, f, :],
                                      start=(f == 0), stop=(f == 1))
                m.then_inc(s_y, 1)

            def step(u, q, front=True, mid=True, back=True):
                if front: turn(u + 1, (q + 1) % 8)
                if mid: hidden(u, q)
                if back: multiply(u - 1, (q - 1) % 8)
            run(pe, step)

        @block.scalar
        def _(act):
            act.preload_act_table(ACT.Exp)

            def step(u, q, front=True, mid=True, back=True):
                if front:
                    k = (q + 1) % 2
                    act.wait_ge(s_T, u + 2)
                    wait(act, s_h, 2 * u)
                    pairs = lambda x: xT[0:D, k, 0:4 * SR].rearrange("p (j x n) -> p x j n", x=2, n=SR)[:, x]
                    act.activation(pairs(0), pT[0:D, k, 0:2 * SR].rearrange("p (j n) -> p j n", n=SR), ACT.Copy)
                    act.activation(pairs(1), pT[D:128, k, 0:2 * SR].rearrange("p (j n) -> p j n", n=SR), ACT.Copy)
                    act.activation(xT[0:D, k, 4 * SR:UT], pT[0:D, k, 2 * SR:3 * SR], ACT.Copy).then_inc(s_xT, 1)
                if mid:
                    k = q % 2
                    act.wait_ge(s_h, 2 * u + 1)
                    wait(act, s_y, u - 1)
                    act.activation(hid[:, k, 0, :], pH[:, k, 0, 0:UT], ACT.Relu, bias=b1[:, q // 4, 0:1]).then_inc(s_ra, 1)
            run(act, step)

        @block.vector
        def _(dve):
            for k in range(2):
                dve.sem_inc(s_st[k], 16)
            dve.memset(w1[D:128, :, :], 0.0)
            dve.memset(xT[D:128, :, :], 0.0).then_inc(s_z, 1)

            def step(u, q, front=True, mid=True, back=True):
                if mid:
                    k = q % 2
                    dve.wait_ge(s_h, 2 * u + 2)
                    wait(dve, s_y, u - 1)
                    dve.tensor_scalar(hid[:, k, 1, :], pH[:, k, 1, 0:UT], b1[:, q // 4, 1:2], 0.0, ALU.add, ALU.max).then_inc(s_rd, 1)
                if back:
                    v, r = u - 1, (q - 1) % 8
                    k = r % 2
                    dve.wait_ge(s_y, v + 1)
                    dve.wait_ge(s_st[k], 16 * (v // 2) + 16 if isinstance(v, int) else (u - q) * 8 + (16 * ((q - 1) // 2) + 16))
                    dve.tensor_tensor(y[:, k], pY[0:SR, k, 0:ST * D].rearrange("p (s c) -> p s c", c=D),
                                      rep(b2[:, r // 4, :], ST), ALU.add).then_inc(s_out, 1)
            run(dve, step)


def combine(nc, h, hout, ybuf, src, wt):
    with ExitStack() as ctx:
        sb = lambda name, shape, dt=F32: ctx.enter_context(nc.sbuf_tensor("G_" + name, shape, dt))
        sem = lambda name: ctx.enter_context(semaphore(nc, "G_" + name))
        hin = sb("hin", [128, 2, GRP, D])
        ho = sb("ho", [128, 2, GRP, D])
        gy = sb("gy", [128, 2, GRP, D])
        yy = sb("yy", [128, GRP, D])
        ok = sb("ok", [128, GRP, D], U32)
        hi = sb("hi", [128, GRP, D], U32)
        lo = sb("lo", [128, GRP, D], U32)
        big = sb("big", [128, 2, GRP, D])
        tick = sb("tick", [128, 1])
        s_in = [sem(f"h_in{k}") for k in range(2)]
        s_st = [sem(f"stored{k}") for k in range(2)]
        s_g = [sem(f"gathered{k}") for k in range(2)]
        s_l, s_k, s_out, s_used = sem("step"), sem("constants"), sem("out"), sem("gather_used")
        hv = h.rearrange("(g j p) c -> g p j c", p=128, j=GRP)
        ov = hout.rearrange("(g j p) c -> g p j c", p=128, j=GRP)
        block = ctx.enter_context(nc.Block())

        @block.gpsimd
        def _(pool):
            for g in range(NG):
                if g >= 2:
                    pool.wait_ge(s_used, g - 1)
                for j in range(GRP):
                    pool.indirect_dma_start(gy[:, g % 2, j, :], None, ybuf,
                                            bass.IndirectOffsetOnAxis(ap=src[:, g * GRP + j:g * GRP + j + 1], axis=0)).then_inc(s_g[g % 2], 16)

        LINKS = 9

        @block.sync
        def _(sp):
            for k in range(2):
                sp.dma_start(hin[:, k], hv[k]).then_inc(s_in[k], 16)
            with sp.Fori(0, NG // 2 - 1) as gg:
                for k in range(2):
                    sp.wait_ge(s_out, 2 * gg + k + 1)
                    sp.dma_start(hin[:, k], hv[2 * gg + 2 + k]).then_inc(s_in[k], 16)
                    sp.dma_start(ov[2 * gg + k], ho[:, k]).then_inc(s_st[k], 16)
            for k in range(2):
                sp.wait_ge(s_out, NG - 2 + k + 1)
                sp.dma_start(ov[NG - 2 + k], ho[:, k]).then_inc(s_st[k], 16)
            for k in range(2):
                sp.wait_ge(s_st[k], 16 * (NG // 2) + 16)

        @block.vector
        def _(dve):
            for k in range(2):
                dve.sem_inc(s_st[k], 16)
            dve.memset(big[:, 0], 10000.0)
            dve.memset(big[:, 1], -10000.0).then_inc(s_k, 1)
            dve.wait_ge(s_k, 1)
            with dve.Fori(0, NG // 2) as gg:
                for k in range(2):
                    g = 2 * gg + k
                    link = linker(dve, s_l, g * LINKS)
                    dve.wait_ge(s_g[k], 16 * GRP * gg + 16 * GRP)
                    link(dve.tensor_tensor(gy[:, k], gy[:, k], bc(wt[:, bass.ds(g * GRP, GRP)], D), ALU.mult))
                    link(dve.tensor_tensor(ok[:, :, :], gy[:, k], gy[:, k], ALU.is_equal))
                    link(dve.tensor_scalar(hi[:, :, :], gy[:, k], FMAX, None, ALU.is_gt))
                    link(dve.tensor_scalar(lo[:, :, :], gy[:, k], -FMAX, None, ALU.is_lt))
                    link(dve.memset(yy[:, :, :], 0.0))
                    dve.memset(tick[:, :], 0.0)
                    link(dve.copy_predicated(yy[:, :, :], ok[:, :, :], gy[:, k]))
                    dve.sem_inc(s_used, 1)
                    dve.memset(tick[:, :], 0.0)
                    link(dve.copy_predicated(yy[:, :, :], hi[:, :, :], big[:, 0]))
                    dve.memset(tick[:, :], 0.0)
                    link(dve.copy_predicated(yy[:, :, :], lo[:, :, :], big[:, 1]))
                    dve.wait_ge(s_in[k], 16 * gg + 16)
                    dve.wait_ge(s_st[k], 16 * gg + 16)
                    link(dve.tensor_tensor(ho[:, k], hin[:, k], yy[:, :, :], ALU.add))
                    dve.sem_inc(s_out, 1)
                    assert link.count[0] == LINKS


def unit_vectors(nc, h, Fhl, ftok, ident):
    with ExitStack() as ctx:
        sb = lambda name, shape, dt=F32: ctx.enter_context(nc.sbuf_tensor(name, shape, dt))
        ps = lambda name, shape, dt=F32: ctx.enter_context(nc.psum_tensor(name, shape, dt))
        sem = lambda name: ctx.enter_context(semaphore(nc, name))
        hin = sb("D_hin", [128, 2, GRP, D])
        xc = sb("D_xc", [128, 2, GRP, D])
        sq = sb("D_sq", [128, 2, GRP, D])
        st = sb("D_st", [128, 2, 8, GRP])
        pT = ps("D_pT", [128, 2, GRP * 128 + 128], F16)
        s_in = [sem(f"D_h_in{k}") for k in range(2)]
        s_link = sem("D_norm_step")
        s_sqrt = sem("D_root")
        s_T = sem("D_transposed")
        s_ev = sem("D_features")
        hv = h.rearrange("(g p j) c -> g p j c", p=128, j=GRP)
        block = ctx.enter_context(nc.Block())

        LINKS = 15
        CENTERED, VAR, SQUARE, PARTS = 2, 6, 8, LINKS - 1

        @block.sync
        def _(sp):
            sp.dma_start(hin[:, 0], hv[0]).then_inc(s_in[0], 16)
            sp.dma_start(hin[:, 1], hv[1]).then_inc(s_in[1], 16)
            with sp.Fori(0, NG // 2 - 1) as g:
                for k in range(2):
                    sp.wait_ge(s_link, g * (2 * LINKS) + done(CENTERED, k))
                    sp.dma_start(hin[:, k], hv[2 * g + 2 + k]).then_inc(s_in[k], 16)

        @block.vector
        def _(dve):
            with dve.Fori(0, NG // 2) as gg:
                both = pairs(dve, s_link, gg * (2 * LINKS))
                S = lambda k, i: st[:, k, i, :]
                js = lambda k: bass.ds((2 * gg + k) * GRP, GRP)
                both(lambda k: dve.tensor_reduce(S(k, 0), hin[:, k], AX.X, ALU.add),
                     lambda k: dve.wait_ge(s_in[k], 16 * gg + 16))
                both(lambda k: dve.tensor_scalar(S(k, 1), S(k, 0), 1.0 / D, None, ALU.mult))
                both(lambda k: dve.tensor_tensor(xc[:, k], hin[:, k], bc(S(k, 1), D), ALU.subtract))
                both(lambda k: dve.tensor_tensor(sq[:, k], xc[:, k], xc[:, k], ALU.mult))
                both(lambda k: dve.tensor_reduce(S(k, 2), sq[:, k], AX.X, ALU.add))
                both(lambda k: dve.tensor_scalar(S(k, 3), S(k, 2), 1.0 / D, LN_EPS, ALU.mult, ALU.add))
                both(lambda k: dve.reciprocal(S(k, 3), S(k, 3)))
                both(lambda k: dve.tensor_tensor(S(k, 4), S(k, 2), S(k, 3), ALU.mult),
                     lambda k: dve.wait_ge(s_sqrt, 4 * gg + k + 1))
                both(lambda k: dve.tensor_tensor(S(k, 4), S(k, 4), S(k, 3), ALU.mult))
                both(lambda k: dve.tensor_scalar(S(k, 4), S(k, 4), N_EPS, None, ALU.max),
                     lambda k: dve.wait_ge(s_sqrt, 4 * gg + k + 3))
                both(lambda k: dve.reciprocal(S(k, 5), S(k, 4)))
                both(lambda k: dve.scalar_tensor_tensor(out=S(k, 5), in0=S(k, 5), scalar=FS, in1=S(k, 3),
                                                        op0=ALU.mult, op1=ALU.mult))
                both(lambda k: dve.tensor_tensor(xc[:, k], xc[:, k], bc(S(k, 5), D), ALU.mult))
                both(lambda k: dve.tensor_copy(ftok[:, js(k), 0:D], xc[:, k]))
                both(lambda k: dve.tensor_tensor(ftok[:, js(k), D:2 * D], xc[:, k], ftok[:, js(k), 0:D], ALU.subtract))
                assert both.count[0] == LINKS

        @block.tensor
        def _(pe):
            with pe.Fori(0, NG // 2) as gg:
                for k in range(2):
                    g = 2 * gg + k
                    pe.wait_ge(s_link, gg * (2 * LINKS) + done(PARTS, k))
                    pe.wait_ge(s_ev, g + 1)
                    for j in range(GRP):
                        m = pe.transpose(pT[:, k, j * 128:j * 128 + 128], ftok[:, g * GRP + j, :], ident[:, :])
                    m.then_inc(s_T, 1)

        @block.scalar
        def _(act):
            act.preload_act_table(ACT.Sqrt)
            act.sem_inc(s_ev, 2)
            with act.Fori(0, NG // 2) as gg:
                for i, op in enumerate((VAR, SQUARE)):
                    for k in range(2):
                        act.wait_ge(s_link, gg * (2 * LINKS) + done(op, k))
                        act.activation(st[:, k, 3 + i, :], st[:, k, 3 + i, :], ACT.Sqrt).then_inc(s_sqrt, 1)
                for k in range(2):
                    g = 2 * gg + k
                    act.wait_ge(s_T, g + 1)
                    act.activation(Fhl[:, bass.ds(g * QB, QB)], pT[:, k, 0:QB], ACT.Copy).then_inc(s_ev, 1)


def attention(nc, Fhl, ftok, OT, den):
    U = 2 * NTT
    with ExitStack() as ctx:
        sb = lambda name, shape, dt=F32: ctx.enter_context(nc.sbuf_tensor(name, shape, dt))
        ps = lambda name, shape, dt=F32: ctx.enter_context(nc.psum_tensor(name, shape, dt))
        sem = lambda name: ctx.enter_context(semaphore(nc, name))
        qhi = sb("D_qhi", [128, 2, QB], F16)
        qlo = sb("D_qlo", [128, 2, QB], F16)
        E = sb("D_E", [128, 4, QH])
        Eh = sb("D_Eh", [128, 4, QH], F16)
        El = sb("D_El", [128, 4, QH], F16)
        pS = ps("D_pS", [128, 4, 512])
        pO = ps("D_pO", [128, 2, 2, 512])
        s_q = [sem(f"D_queries_in{k}") for k in range(2)]
        s_S = sem("D_scores")
        s_E = sem("D_exp")
        s_hD = sem("D_exp_high")
        s_lo = sem("D_exp_low")
        s_pv = sem("D_weighted")
        s_ev = sem("D_out_copied")
        block = ctx.enter_context(nc.Block())

        @block.sync
        def _(sp):
            def load(k, b):
                cols = bass.ds(b * QB, QB)
                for dst, p in ((qhi, 0), (qlo, D)):
                    for half in range(2):
                        sp.dma_start(dst[half * D:half * D + D, k, :], Fhl[p:p + D, cols]).then_inc(s_q[k], 16)
            load(0, 0)
            load(1, 1)
            with sp.Fori(0, NG // 2 - 1) as bb:
                for k in range(2):
                    sp.wait_ge(s_pv, bb * (2 * U) + (k + 1) * U + 4)
                    load(k, 2 * bb + 2 + k)

        @block.tensor
        def _(pe):
            def scores(r, k, j, half):
                keys = Fhl[:, bass.ds(j * 128, 128)]
                cols = slice(half * QH, half * QH + QH)
                pe.matmul(pS[:, r, 0:QH], keys, qhi[:, k, cols], start=True, stop=False)
                pe.matmul(pS[:, r, 0:QH], keys, qlo[:, k, cols], start=False, stop=True).then_inc(s_S, 1)

            def weigh(r, k, j, half, first, last, u):
                pe.wait_ge(s_lo, u + 1)
                f = ftok[:, j, :]
                pe.matmul(pO[:, k, half, 0:QH], f, Eh[:, r, :], start=first, stop=False)
                pe.matmul(pO[:, k, half, 0:QH], f, El[:, r, :], start=False, stop=last).then_inc(s_pv, 1)

            def four(k, base, j, first=False, last=False, next_load=None, end=False):
                for r in range(4):
                    ahead = r + 3
                    if not (end and ahead >= 4):
                        pe.wait_ge(s_E, base + r + 1)
                        if last and ahead >= 4:
                            if r == 1:
                                pe.wait_ge(s_q[1 - k], next_load)
                            scores(ahead % 4, 1 - k, (ahead - 4) // 2, ahead % 2)
                        else:
                            scores(ahead % 4, k, j + ahead // 2, ahead % 2)
                    weigh(r, k, j + r // 2, r % 2, first and r < 2, last and r >= 2, base + r)

            def query_block(k, b, next_load, end=False):
                pe.wait_ge(s_ev, b + 1)
                four(k, b * U, 0, first=True)
                with pe.Fori(1, NTT // 2 - 1) as m:
                    four(k, b * U + 4 * m, 2 * m)
                four(k, b * U + U - 4, NTT - 2, last=True, next_load=next_load, end=end)

            pe.wait_ge(s_q[0], 64)
            for r in range(3):
                scores(r, 0, r // 2, r % 2)
            with pe.Fori(0, NG // 2 - 1) as bb:
                query_block(0, 2 * bb, 64 * bb + 64)
                query_block(1, 2 * bb + 1, 64 * bb + 128)
            query_block(0, NG - 2, 64 * (NG // 2))
            query_block(1, NG - 1, None, end=True)

        @block.scalar
        def _(act):
            act.preload_act_table(ACT.Exp)
            act.sem_inc(s_E, 1)
            act.sem_inc(s_pv, 4)
            with act.Fori(0, NG * NTT // 2) as m:
                for r in range(4):
                    act.wait_ge(s_S, 4 * m + r + 1)
                    act.wait_ge(s_pv, 4 * m + r + 1)
                    if r % 2 == 0:
                        act.activation(Eh[:, r, :], pS[:, r, 0:QH], ACT.Exp, scale=1.0 / (FS * FS))
                    act.activation(E[:, r, :], pS[:, r, 0:QH], ACT.Exp, scale=1.0 / (FS * FS),
                                   accum_out=den[:, bass.ds(4 * m + r, 1)]).then_inc(s_E, 1)

        @block.vector
        def _(dve):
            dve.sem_inc(s_ev, 2)

            def four(m):
                for r in range(4):
                    dve.wait_ge(s_E, 4 * m + r + 2)
                    if r % 2 == 1:
                        dve.tensor_copy(Eh[:, r, :], E[:, r, :]).then_inc(s_hD, 1)
                        dve.wait_ge(s_hD, 2 * m + r // 2 + 1)
                    dve.tensor_tensor(El[:, r, :], E[:, r, :], Eh[:, r, :], ALU.subtract).then_inc(s_lo, 1)

            def copy_out(b, k):
                dve.wait_ge(s_pv, b * U + U + 4)
                dve.tensor_copy(OT[:, bass.ds(b * QB, QB)].rearrange("p (a n) -> p a n", a=2),
                                pO[:, k, :, 0:QH]).then_inc(s_ev, 1)

            M = NTT // 2
            with dve.Fori(0, M) as m:
                four(m)
            with dve.Fori(0, NG // 2 - 1) as bb:
                for k in range(2):
                    four((2 * bb + k + 1) * M)
                    copy_out(2 * bb + k, k)
                    with dve.Fori(1, M) as m:
                        four((2 * bb + k + 1) * M + m)
            four((NG - 1) * M)
            copy_out(NG - 2, 0)
            with dve.Fori(1, M) as m:
                four((NG - 1) * M + m)
            copy_out(NG - 1, 1)


def blend(nc, h, hout, ftok, OT, den, fold):
    with ExitStack() as ctx:
        sb = lambda name, shape, dt=F32: ctx.enter_context(nc.sbuf_tensor(name, shape, dt))
        ps = lambda name, shape, dt=F32: ctx.enter_context(nc.psum_tensor(name, shape, dt))
        sem = lambda name: ctx.enter_context(semaphore(nc, name))
        hin = sb("F_hin", [128, 2, GRP, D])
        f8 = sb("F_f8", [128, 2, GRP, D])
        fc = sb("F_fc", [128, 2, GRP, D])
        sq = sb("F_sq", [128, 2, GRP, D])
        ho = sb("F_ho", [128, 2, GRP, D])
        rden = sb("F_rden", [128, NTT])
        st = sb("F_st", [128, 2, 2, GRP])
        pt = ps("F_pt", [128, 2, 512])
        ot = sb("F_ot", [128, 2, QB])
        s_in = [sem(f"F_h_in{k}") for k in range(2)]
        s_link = sem("F_step")
        s_den = sem("F_sum_step")
        s_root = sem("F_root")
        s_ot = sem("F_sums_moved")
        s_T = sem("F_token_rows")
        s_st = [sem(f"F_stored{k}") for k in range(2)]
        hv = h.rearrange("(g p j) c -> g p j c", p=128, j=GRP)
        ov = hout.rearrange("(g p j) c -> g p j c", p=128, j=GRP)
        block = ctx.enter_context(nc.Block())

        LINKS = 9
        SQUARE, OUT = 4, 8

        @block.sync
        def _(sp):
            sp.dma_start(hin[:, 0], hv[0]).then_inc(s_in[0], 16)
            sp.dma_start(hin[:, 1], hv[1]).then_inc(s_in[1], 16)
            with sp.Fori(0, NG // 2 - 1) as gg:
                for k in range(2):
                    sp.wait_ge(s_link, gg * (2 * LINKS) + done(OUT, k))
                    sp.dma_start(hin[:, k], hv[2 * gg + 2 + k]).then_inc(s_in[k], 16)
                    sp.dma_start(ov[2 * gg + k], ho[:, k]).then_inc(s_st[k], 16)
            for k in range(2):
                sp.wait_ge(s_link, (NG // 2 - 1) * 2 * LINKS + done(OUT, k))
                sp.dma_start(ov[NG - 2 + k], ho[:, k]).then_inc(s_st[k], 16)
            for k in range(2):
                sp.wait_ge(s_st[k], 16 * (NG // 2) + 16)

        @block.tensor
        def _(pe):
            with pe.Fori(0, NG // 2) as gg:
                for k in range(2):
                    pe.wait_ge(s_link, gg * (2 * LINKS) + done(0, k))
                    pe.wait_ge(s_ot, 2 * gg + k + 1)
                    for j in range(GRP):
                        m = pe.matmul(pt[:, k, j * D:j * D + D], ot[:, k, j * 128:j * 128 + 128], fold[:, :], start=True, stop=True)
                    m.then_inc(s_T, 1)

        @block.scalar
        def _(act):
            act.preload_act_table(ACT.Sqrt)
            act.sem_inc(s_T, 2)
            with act.Fori(0, NG // 2) as gg:
                for k in range(2):
                    g = 2 * gg + k
                    act.wait_ge(s_T, g + 1)
                    act.activation(ot[:, k, :], OT[:, bass.ds(g * QB, QB)], ACT.Copy).then_inc(s_ot, 1)
                for k in range(2):
                    act.wait_ge(s_link, gg * (2 * LINKS) + done(SQUARE, k))
                    act.activation(st[:, k, 0, :], st[:, k, 0, :], ACT.Sqrt).then_inc(s_root, 1)


        @block.vector
        def _(dve):
            for k in range(2):
                dve.sem_inc(s_st[k], 16)
            link = linker(dve, s_den)
            link(dve.tensor_reduce(rden[:, :], den[:, :].rearrange("p (b j a) -> p j b a", j=NTT, a=2), AX.XY, ALU.add))
            link(dve.reciprocal(rden[:, :], rden[:, :]))
            link(dve.tensor_scalar(rden[:, :], rden[:, :], (1.0 - BLEND) / FS, None, ALU.mult))
            with dve.Fori(0, NG // 2) as gg:
                both = pairs(dve, s_link, gg * (2 * LINKS))
                js = lambda k: bass.ds((2 * gg + k) * GRP, GRP)
                both(lambda k: dve.tensor_tensor(f8[:, k], ftok[:, js(k), 0:D], ftok[:, js(k), D:2 * D], ALU.add))
                both(lambda k: dve.tensor_tensor(fc[:, k], pt[:, k, 0:GRP * D].rearrange("p (j c) -> p j c", c=D),
                                                 bc(rden[:, js(k)], D), ALU.mult),
                     lambda k: dve.wait_ge(s_T, 2 * gg + k + 3))
                both(lambda k: dve.scalar_tensor_tensor(out=fc[:, k], in0=f8[:, k], scalar=BLEND / FS, in1=fc[:, k],
                                                        op0=ALU.mult, op1=ALU.add))
                both(lambda k: dve.tensor_tensor(sq[:, k], fc[:, k], fc[:, k], ALU.mult))
                both(lambda k: dve.tensor_reduce(st[:, k, 0, :], sq[:, k], AX.X, ALU.add))
                both(lambda k: dve.tensor_scalar(st[:, k, 0, :], st[:, k, 0, :], N_EPS, None, ALU.max),
                     lambda k: dve.wait_ge(s_root, 2 * gg + k + 1))
                both(lambda k: dve.reciprocal(st[:, k, 1, :], st[:, k, 0, :]))
                both(lambda k: dve.tensor_tensor(fc[:, k], fc[:, k], bc(st[:, k, 1, :], D), ALU.mult))

                def ready(k):
                    dve.wait_ge(s_in[k], 16 * gg + 16)
                    dve.wait_ge(s_st[k], 16 * gg + 16)
                both(lambda k: dve.tensor_tensor(ho[:, k], hin[:, k], fc[:, k], ALU.add), ready)
                assert both.count[0] == LINKS


RWKV_INS = ("x_mix", "W_r", "W_k", "W_v", "W_o", "A_w", "B_w", "b_w", "A_a", "B_a", "b_a", "A_g", "B_g",
            "k_k", "k_a", "r_k", "gn_w", "gn_b")


def network(nc, ins, cst, out):
    dram = lambda name, shape: nc.dram_tensor(name, shape, F32, kind="Internal").ap()
    hA, hB, hC, hD = (dram(f"h_{x}", [TOK, D]) for x in ("tokens", "rwkv", "experts1", "attention"))
    buf = dram("expert_rows", [EX * CAP + TOK, D])
    ybuf = dram("expert_outputs", [EX * CAP, D])
    part = lambda pre: {k[len(pre):]: v for k, v in ins.items() if k.startswith(pre)}

    tk = part("L0_tok_")
    tokenizer(nc, ins["x"], tk["W1"], tk["b1"], tk["W2"], tk["b2"], tk["W3"], tk["b3"], hA)

    with ExitStack() as ctx:
        sb = lambda name, shape, dt=F32: ctx.enter_context(nc.sbuf_tensor(name, shape, dt))
        w, c = weights(nc, ctx, part("L0_attn_"), cst)
        rkv = sb("rkv", [128, NTT, 3 * D])
        rn = sb("rn", [128, NTT])
        ga = sb("ga", [128, NTT, D])
        with nc.sbuf_tensor("Z2", [128, TOK], F32) as Z2:
            norm_features(nc, hA, Z2, c["eye"])
            project(nc, w, Z2, rkv, rn)
            recurrence(nc, w, c, Z2, rkv, ga, rn)
        outputs(nc, w, hA, hB, rkv, ga, c["eye"])

    with ExitStack() as ctx:
        sb = lambda name, shape, dt=F32: ctx.enter_context(nc.sbuf_tensor(name, shape, dt))
        eye = sb("eye", [128, 128])
        XT = sb("XT1", [128, TOK])
        cw = sb("cw1", [128, NTT, EX])
        load_all(nc, "C", [(eye[:, :], cst["eye"])], zero=[XT[D:128, :]])
        w = moe1_weights(nc, ctx, part("L0_ffn_"), cst)
        layer_norm(nc, "C0_", hB, XT, eye)
        gating(nc, "C1_", XT, w["gate"][:, :], w["gb"][:, :], w["less"][:, :], 2, cw)
        experts_dense(nc, hB, hC, XT, cw, w, eye)

    with ExitStack() as ctx:
        sb = lambda name, shape, dt=F32: ctx.enter_context(nc.sbuf_tensor(name, shape, dt))
        Fhl = sb("Fhl", [128, TOK], F16)
        ftok = sb("ftok", [128, NTT, 128], F16)
        OT = sb("OT", [128, TOK])
        den = sb("den", [128, NG * NTT * 2])
        eye16 = sb("eye16", [128, 128], F16)
        fold = sb("fold", [128, D])
        load_all(nc, "D", [(eye16[:, :], cst["eye16"]), (fold[:, :], cst["fold"])])
        unit_vectors(nc, hC, Fhl, ftok, eye16)
        attention(nc, Fhl, ftok, OT, den)
        blend(nc, hC, hD, ftok, OT, den, fold)

    with ExitStack() as ctx:
        sb = lambda name, shape, dt=F32: ctx.enter_context(nc.sbuf_tensor(name, shape, dt))
        p = part("L1_ffn_")
        eye = sb("eye2", [128, 128])
        cw = sb("cw2", [128, NTT, EX])
        chosen = sb("chosen", [128, NTT, EX])
        rows = sb("rows", [128, NTT, D])
        dest = sb("dest", [128, NTT], U32)
        src = sb("src", [128, NTT], U32)
        wt = sb("wt", [128, NTT])
        gw = sb("gate_w2", [D, EX])
        gb = sb("gate_b2", [128, EX])
        c = {k: sb(f"c_{k}", list(v.shape)) for k, v in cst.items() if k in MOE_CONSTANTS}
        load_all(nc, "E", [(eye[:, :], cst["eye"]), (gw[:, :], p["gate_w"]),
                           (gb[:, :], p["gate_b"].rearrange("(a c) -> a c", a=1).broadcast_to([128, EX]))]
                 + [(c[k][:, :], cst[k]) for k in MOE_CONSTANTS])
        with nc.sbuf_tensor("XT2", [D, TOK], F32) as XT:
            layer_norm(nc, "E0_", hD, XT, eye, rows)
            gating(nc, "E1_", XT, gw[:, :], gb[:, :], c["less"][:, :], 1, cw, chosen)
        slots(nc, c, chosen, cw, dest, src, wt)
        dispatch(nc, rows, dest, buf)
        experts_sparse(nc, p, buf, ybuf, eye)
        combine(nc, hD, out, ybuf, src, wt)


MOE_CONSTANTS = ("less", "base", "dump", "upto")


def load_all(nc, name, pairs, zero=()):
    with semaphore(nc, name + "_loaded") as s, semaphore(nc, name + "_zeroed") as z, nc.Block() as block:
        @block.sync
        def _(sp):
            for dst, src in pairs:
                sp.dma_start(dst, src).then_inc(s, 16)
            sp.wait_ge(s, 16 * len(pairs))

        @block.vector
        def _(dve):
            for dst in zero:
                dve.memset(dst, 0.0).then_inc(z, 1)


def all_constants():
    c = dict(constants())
    c.update(moe_constants())
    c["eye16"] = np.eye(128).astype(np.float16)
    c["fold"] = np.tile(np.eye(D), (2, 1)).astype(np.float32)
    return c


def tap_rows(W):
    W = W.reshape(CH, 9, -1).transpose(1, 0, 2)[[3 * i + j for i, j in TAPS]].reshape(9 * CH, -1)
    return np.concatenate([W, np.zeros((NCH * 128 - 9 * CH, W.shape[1]), W.dtype)])


def kernel(**inputs):
    import concourse.bacc as _bacc
    from concourse.bass_utils import run_bass_kernel_spmd as _run

    data = {k: np.asarray(v) for k, v in inputs.items()}
    data["x"] = data["x"].reshape(BATCH, CH, IMG, IMG)
    data["L0_tok_W1"] = tap_rows(data["L0_tok_W1"])
    data["L0_tok_W2"] = tap_rows(data["L0_tok_W2"].T).T
    data["L0_tok_b2"] = tap_rows(data["L0_tok_b2"][:, None])[:, 0]
    data["L0_tok_W3"] = tap_rows(data["L0_tok_W3"])

    nc = _bacc.Bacc("TRN2", target_bir_lowering=False, num_devices=1)
    arrays = {}

    def place(name, a):
        arrays[name] = np.ascontiguousarray(a)
        return nc.dram_tensor(name, a.shape, mybir.dt.from_np(a.dtype), kind="ExternalInput").ap()
    ins = {k: place("in_" + k, v) for k, v in data.items()}
    cst = {k: place("const_" + k, v) for k, v in all_constants().items()}
    out = nc.dram_tensor("out", (TOK, D), F32, kind="ExternalOutput").ap()
    network(nc, ins, cst, out)
    r = _run(nc, [arrays], core_ids=[0])
    return r.results[0]["out"].reshape(BATCH, SEQ, D)
```

```python
from contextlib import ExitStack, contextmanager
import numpy as np
from concourse import bass, mybir
F32 = mybir.dt.float32
F16 = mybir.dt.float16
U32 = mybir.dt.uint32
ALU = mybir.AluOpType
ACT = mybir.ActivationFunctionType
AX = mybir.AxisListType

BATCH, CH, IMG = 4, 64, 56
D = CH
SEQ = IMG * IMG
TOK = BATCH * SEQ
NTT = TOK // 128
GRP = 7
NG = NTT // GRP
QB = GRP * 128
QH = QB // 2
LN_EPS = 1e-5
N_EPS = 1e-12
FMAX = 3.4028234663852886e38

PAD = IMG + 2
ROWS = 8
TILE = ROWS * IMG
NT = IMG // ROWS
SUB = TILE // 4
TAPS = [(0, 0), (0, 1), (1, 0), (1, 1), (2, 0), (2, 1), (0, 2), (1, 2), (2, 2)]
NCH = 5

GN_EPS = D * 1e-5
DECAY = -0.6065306597126334
CS = 64
NIT = NTT // 2
LEVELS = 5

EX = 8
F1 = 128
F2 = 256
CAP = -(-5 * TOK // (4 * EX))
CU = 4
UT = CAP // CU
ST = 5
SR = UT // ST

FS = 64.0
BLEND = 0.8


@contextmanager
def semaphore(nc, name):
    s = nc.alloc_semaphore(name=name)
    yield s
    nc.gpsimd.sem_clear(s)
    nc.release_semaphore(s)


def pairs(eng, sem, base):
    n = [0]

    def both(op, before=None):
        for k in range(2):
            if n[0]:
                eng.wait_ge(sem, base + done(n[0] - 1, k))
            if before is not None:
                before(k)
            op(k).then_inc(sem, 1)
        n[0] += 1
    both.count = n
    return both


def done(n, k):
    return 2 * n + k + 1


def constants():
    s, t = np.meshgrid(np.arange(128), np.arange(128), indexing="ij")
    same = s // CS == t // CS
    up, upi = same & (s < t), same & (s <= t)
    c = {"tri": np.concatenate([upi, same & (s > t)], 1),
         "ind": np.stack([np.arange(128) // CS == k for k in range(2)], 1),
         "mask": np.concatenate([up, upi, up, upi], 1),
         "neg0": -np.concatenate([(s % 2 == 1) & (t == s - 1), (t % 2 == 1) & (s == t - 1)], 1).astype(np.float32),
         "lev": np.concatenate([(s >> (l + 1) == t >> (l + 1)) & ((t >> l) & 1 == 1) & ((s >> l) & 1 == 0)
                                for l in range(1, LEVELS + 1)], 1),
         "eye": s == t,
         "keep": np.tile((np.arange(1, NTT + 1) % (SEQ // CS) != 0)[None], (D, 1))}
    return {k: np.ascontiguousarray(v.astype(np.float32)) for k, v in c.items()}


def linker(eng, sem, base=0):
    n = [0]

    def link(ins):
        n[0] += 1
        ins.then_inc(sem, 1)
        eng.wait_ge(sem, base + n[0])
    link.count = n
    return link


def bc(ap, n):
    p, g = ap.shape
    return ap.rearrange("p (g a) -> p g a", a=1).broadcast_to([p, g, n])


def rep(ap, n):
    p, c = ap.shape
    return ap.rearrange("p (a c) -> p a c", a=1).broadcast_to([p, n, c])


def norm_features(nc, h, Z2, eye):
    with ExitStack() as ctx:
        sb = lambda name, shape, dt=F32: ctx.enter_context(nc.sbuf_tensor(name, shape, dt))
        sem = lambda name: ctx.enter_context(semaphore(nc, name))
        hin = sb("B0_hin", [128, 2, GRP, D])
        xc = sb("B0_xc", [128, 2, GRP, D])
        xn = sb("B0_xn", [128, 2, GRP, D])
        sq = sb("B0_sq", [128, 2, GRP, D])
        st = sb("B0_st", [128, 2, 4, GRP])
        pT = ctx.enter_context(nc.psum_tensor("B0_pT", [128, 2, 512], F32))
        s_in = [sem(f"B0_h_in{k}") for k in range(2)]
        s_link, s_sqrt, s_sq, s_x = sem("B0_step"), sem("B0_root"), sem("B0_squares"), sem("B0_normed")
        s_T, s_ev, s_z, s_sh = sem("B0_transposed"), sem("B0_features"), sem("B0_starts"), sem("B0_shifted")
        hv = h.rearrange("(g j p) c -> g p j c", p=128, j=GRP)
        block = ctx.enter_context(nc.Block())

        LINKS = 6
        CENTERED, VAR = 2, 5

        @block.sync
        def _(sp):
            for k in range(2):
                sp.dma_start(hin[:, k], hv[k]).then_inc(s_in[k], 16)
            with sp.Fori(0, NG // 2 - 1) as g:
                for k in range(2):
                    sp.wait_ge(s_link, g * (2 * LINKS) + done(CENTERED, k))
                    sp.dma_start(hin[:, k], hv[2 * g + 2 + k]).then_inc(s_in[k], 16)
            for b in range(BATCH):
                sp.wait_ge(s_ev, 2 + min(NG, -(-(b + 1) * SEQ // QB)))
                sp.dma_start(Z2[D:2 * D, b * SEQ + 1:(b + 1) * SEQ], Z2[0:D, b * SEQ:(b + 1) * SEQ - 1]).then_inc(s_sh, 16)
            sp.wait_ge(s_sh, 16 * BATCH)

        @block.gpsimd
        def _(pool):
            for b in range(BATCH):
                m = pool.memset(Z2[D:2 * D, b * SEQ:b * SEQ + 1], 0.0)
            m.then_inc(s_z, 1)
            pool.wait_ge(s_z, 1)
            pool.sem_inc(s_x, 2)
            with pool.Fori(0, NG // 2) as gg:
                for k in range(2):
                    pool.wait_ge(s_sqrt, 2 * gg + k + 1)
                    pool.wait_ge(s_T, 2 * gg + k + 1)
                    pool.tensor_tensor(xn[:, k], xc[:, k], bc(st[:, k, 3, :], D), ALU.mult).then_inc(s_x, 1)

        @block.vector
        def _(dve):
            with dve.Fori(0, NG // 2) as gg:
                both = pairs(dve, s_link, gg * (2 * LINKS))
                S = lambda k, i: st[:, k, i, :]
                both(lambda k: dve.tensor_reduce(S(k, 0), hin[:, k], AX.X, ALU.add),
                     lambda k: dve.wait_ge(s_in[k], 16 * gg + 16))
                both(lambda k: dve.tensor_scalar(S(k, 1), S(k, 0), 1.0 / D, None, ALU.mult))
                both(lambda k: dve.tensor_tensor(xc[:, k], hin[:, k], bc(S(k, 1), D), ALU.subtract),
                     lambda k: dve.wait_ge(s_x, 2 * gg + k + 1))
                both(lambda k: dve.tensor_reduce(S(k, 2), sq[:, k], AX.X, ALU.add),
                     lambda k: dve.wait_ge(s_sq, 2 * gg + k + 1))
                both(lambda k: dve.tensor_scalar(S(k, 2), S(k, 2), 1.0 / D, LN_EPS, ALU.mult, ALU.add))
                both(lambda k: dve.reciprocal(S(k, 3), S(k, 2)))
                assert both.count[0] == LINKS

        @block.tensor
        def _(pe):
            pe.sem_inc(s_T, 2)
            with pe.Fori(0, NG // 2) as gg:
                for k in range(2):
                    g = 2 * gg + k
                    pe.wait_ge(s_x, g + 3)
                    pe.wait_ge(s_ev, g + 1)
                    for j in range(GRP // 2):
                        pe.transpose(pT[:, k, j * 128:j * 128 + 128], xn[:, k, 2 * j:2 * j + 2, :], eye[:, :])
                    m = pe.transpose(pT[0:D, k, 384:512], xn[:, k, GRP - 1, :], eye[:, :])
                    m.then_inc(s_T, 1)

        @block.scalar
        def _(act):
            act.preload_act_table(ACT.Sqrt)
            act.sem_inc(s_ev, 2)

            def statistics(gg):
                for k in range(2):
                    act.wait_ge(s_link, gg * (2 * LINKS) + done(CENTERED, k))
                    act.activation(sq[:, k], xc[:, k], ACT.Square).then_inc(s_sq, 1)
                for k in range(2):
                    act.wait_ge(s_link, gg * (2 * LINKS) + done(VAR, k))
                    act.activation(st[:, k, 3, :], st[:, k, 3, :], ACT.Sqrt).then_inc(s_sqrt, 1)

            def features(gg):
                for k in range(2):
                    act.wait_ge(s_T, 2 * gg + k + 3)
                    z = Z2[0:D, bass.ds((2 * gg + k) * QB, QB)]
                    pair = lambda x: z[:, 0:768].rearrange("p (j x n) -> p x j n", x=2, n=128)[:, x]
                    act.activation(pair(0), pT[0:D, k, 0:384].rearrange("p (j n) -> p j n", n=128), ACT.Copy)
                    act.activation(pair(1), pT[D:128, k, 0:384].rearrange("p (j n) -> p j n", n=128), ACT.Copy)
                    act.activation(z[:, 768:896], pT[0:D, k, 384:512], ACT.Copy).then_inc(s_ev, 1)

            statistics(0)
            with act.Fori(1, NG // 2) as gg:
                statistics(gg)
                features(gg - 1)
            features(NG // 2 - 1)


def project(nc, w, Z2, rkv, rn):
    with ExitStack() as ctx:
        sb = lambda name, shape, dt=F32: ctx.enter_context(nc.sbuf_tensor(name, shape, dt))
        sem = lambda name: ctx.enter_context(semaphore(nc, name))
        zs = sb("P_zs", [128, 2, QB])
        kk = sb("P_kk", [128, GRP, D])
        pR = ctx.enter_context(nc.psum_tensor("P_pR", [128, 2, 4, 512], F32))
        s_zs, s_p, s_rkv, s_kk, s_n, s_end, s_root = (sem("P_" + x) for x in (
            "tile_moved", "projected", "rows_copied", "keys_scaled", "norms", "norms_done", "root"))
        block = ctx.enter_context(nc.Block())

        @block.scalar
        def _(act):
            act.preload_act_table(ACT.Sqrt)
            act.sem_inc(s_rkv, 2)

            def move(g, k):
                act.wait_ge(s_p, g + 1)
                act.activation(zs[:, k, :], Z2[:, bass.ds(g * QB, QB)], ACT.Copy).then_inc(s_zs, 1)

            def keep(g, k):
                act.wait_ge(s_p, g + 3)
                act.activation(rkv[:, bass.ds(g * GRP, 6), :].rearrange("p (b j) c -> p b j c", j=2),
                               pR[:, k, 0:3, 0:384].rearrange("p b (j c) -> p b j c", j=2), ACT.Copy)
                act.activation(rkv[:, bass.ds(g * GRP + 6, 1), :].rearrange("p a c -> p (a c)"),
                               pR[:, k, 3, 0:192], ACT.Copy).then_inc(s_rkv, 1)

            move(0, 0)
            with act.Fori(0, NG // 2 - 1) as gg:
                for k in range(2):
                    move(2 * gg + k + 1, 1 - k)
                    keep(2 * gg + k, k)
            move(NG - 1, 1)
            keep(NG - 2, 0)
            keep(NG - 1, 1)
            act.wait_ge(s_end, 1)
            act.activation(rn[:, :], rn[:, :], ACT.Sqrt).then_inc(s_root, 1)

        @block.tensor
        def _(pe):
            pe.sem_inc(s_p, 2)
            with pe.Fori(0, NG // 2) as gg:
                for k in range(2):
                    g = 2 * gg + k
                    pe.wait_ge(s_zs, g + 1)
                    pe.wait_ge(s_rkv, g + 1)
                    for j in range(GRP):
                        m = pe.matmul(pR[:, k, j // 2, (j % 2) * 192:(j % 2) * 192 + 192],
                                      zs[:, k, j * 128:j * 128 + 128], w["rkv"][:, :], start=True, stop=True)
                    m.then_inc(s_p, 1)

        @block.vector
        def _(dve):
            with dve.Fori(0, NG // 2) as gg:
                for k in range(2):
                    g = 2 * gg + k
                    dve.wait_ge(s_rkv, g + 3)
                    dve.tensor_tensor(kk[:, :, :], rkv[:, bass.ds(g * GRP, GRP), D:2 * D], rep(w["k_k"][:, :], GRP),
                                      ALU.mult).then_inc(s_kk, 1)
                    dve.wait_ge(s_kk, 2 * g + 1)
                    dve.tensor_tensor(kk[:, :, :], kk[:, :, :], kk[:, :, :], ALU.mult).then_inc(s_kk, 1)
                    dve.wait_ge(s_kk, 2 * g + 2)
                    dve.tensor_reduce(rn[:, bass.ds(g * GRP, GRP)], kk[:, :, :], AX.X, ALU.add).then_inc(s_n, 1)
                    dve.wait_ge(s_n, g + 1)
            dve.sem_inc(s_end, 1)
            dve.wait_ge(s_root, 1)
            dve.tensor_scalar(rn[:, :], rn[:, :], N_EPS, None, ALU.max).then_inc(s_end, 1)
            dve.wait_ge(s_end, 2)
            dve.reciprocal(rn[:, :], rn[:, :]).then_inc(s_end, 1)


def recurrence(nc, w, c, Z2, rkv, gate_, rn):
    with ExitStack() as ctx:
        sb = lambda name, shape, dt=F32: ctx.enter_context(nc.sbuf_tensor(name, shape, dt))
        sem = lambda name: ctx.enter_context(semaphore(nc, "R_" + name))
        hid = sb("R_hid", [128, 256])
        gh = sb("R_gh", [128, 256])
        wa = sb("R_wa", [128, 2, 128])
        lw = sb("R_lw", [128, 2, D])
        a_ = sb("R_a", [128, 2, D])
        ex = sb("R_ex", [128, 2, D])
        eP = sb("R_eP", [128, 2, D])
        eN = sb("R_eN", [128, 2, D])
        eS = sb("R_eS", [128, 2, D])
        eX = sb("R_eX", [128, 2, D])
        kn = sb("R_kn", [128, 2, D])
        kp = sb("R_kp", [128, 2, D])
        bt = sb("R_bt", [128, 2, D])
        rk = sb("R_rk", [128, 2, D])
        rs = sb("R_rs", [128, 2])
        V = sb("R_V", [128, 2, 2, D])
        DC = sb("R_DC", [D, 2, 4])
        QN = sb("R_QN", [128, 2, 2, 128])
        RBK = sb("R_QRBK", [128, 4, 2, D])
        Bh = sb("R_Bh", [128, 2, 2, 2, D])
        Kh = sb("R_Kh", [128, 2, 2, 2, D])
        FT = sb("R_FT", [D, 2, 2, 512])
        PM = sb("R_PM", [128, 2, 2, 512])
        ML = sb("R_ML", [128, LEVELS, 2, 128])
        XX = sb("R_XX", [128, 2, 2, 128])
        XT = sb("R_XT", [128, 2, 2, 128])
        Ys = sb("R_Ys", [128, 2, 128])
        WU = sb("R_WU", [128, 2, 128])
        RpT = sb("R_RpT", [D, 256])
        GT = sb("R_GT", [D, 4, D])
        Z = sb("R_Z", [D, 2, 2, D])
        bank = [ctx.enter_context(nc.psum_tensor(f"R_b{i}", [128, 512], F32)) for i in range(8)]
        pH = bank[0]
        pW = bank[1][:, 0:384].rearrange("p (t c) -> p t c", t=2)
        pN = bank[1][:, 384:512].rearrange("p (t c) -> p t c", t=2)
        pC = bank[2][:, 0:256].rearrange("p (t c) -> p t c", t=2)
        pD = bank[2][0:D, 256:260]
        pO = bank[2][:, 264:392].rearrange("p (t c) -> p t c", t=2)
        pT = bank[3:5]
        pL = [bank[b][:, 0:128] for b in (5, 7)]
        pY = [bank[b][:, 128:256] for b in (5, 7)]
        pX = [bank[b][:, 256:512].rearrange("p (x c) -> p x c", x=2) for b in (5, 7)]
        pZ = bank[6][0:D, 0:256].rearrange("p (n t c) -> p n t c", n=2, t=2)
        pWU = bank[6][:, 256:512].rearrange("p (t c) -> p t c", t=2)
        pR = bank[0][0:D, 0:256]
        pG = bank[0][0:D, 256:512].rearrange("p (n c) -> p n c", n=4)
        (s_hp, s_hid, s_gs, s_wp, s_wa, s_th, s_V, s_g, s_lw, s_cum, s_ex, s_exp, s_el, s_T, s_FT, s_prod, s_mask,
         s_ML, s_X, s_Y, s_Ys, s_pX, s_pN, s_QN, s_pWU, s_WU, s_pRG, s_RG, s_pZ, s_Z, s_pO, s_O, s_dve, s_xl, s_X0, s_dI, s_qn, s_bk) = (
            sem(x) for x in ("hidden", "hidden_copied", "gate_hidden", "lora", "lora_biased", "lora_tanh", "v_copied",
                             "gate_stored", "log_decay", "cumulated", "exclusive", "exponentials", "scaled", "turned",
                             "turned_copied", "products", "masked", "level_masks", "inverse", "inner", "inner_copied",
                             "merge", "nv", "nv_copied", "wu", "wu_copied", "rg", "rg_copied", "state_sum", "state",
                             "out", "out_stored", "token_step", "first_blocks", "first_inverse", "decay_diagonal", "q_copied", "state_factors"))
        block = ctx.enter_context(nc.Block())

        halves = lambda x: x.rearrange("p (s j) c -> p s j c", s=2)
        rkv_, gates_, rn_ = halves(rkv[:, :, :]), halves(gate_[:, :, :]), rn[:, :].rearrange("p (s j) -> p s j", s=2)
        Z2_ = Z2[:, :].rearrange("p (s n) -> p s n", s=2)

        TL = 8

        def wait(eng, s, n):
            if not (isinstance(n, int) and n <= 0):
                eng.wait_ge(s, n)

        def run(eng, step):
            step(-1, 1, inv=False, state=False)
            step(0, 0, state=False)
            step(1, 1)
            step(2, 0)
            with eng.Fori(1, (NIT - 3) // 2) as m:
                step(2 * m + 1, 1)
                step(2 * m + 2, 0)
            step(NIT - 2, 1)
            step(NIT - 1, 0, front=False)
            step(NIT, 1, front=False, inv=False)

        @block.tensor
        def _(pe):
            def hidden(i, p):
                wait(pe, s_hid, i)
                wait(pe, s_RG, i - 2)
                z = Z2_[:, :, bass.ds(128 * i, 128)]
                two = lambda x: x.rearrange("p (s n) -> p s n", s=2)
                pe.matmul(two(pH[:, 0:256]), w["Awa"][:, :], z, start=True, stop=True)
                pe.matmul(two(pH[:, 256:512]), w["Ag"][:, :], z, start=True, stop=True).then_inc(s_hp, 1)

            def lora(i, p):
                pe.wait_ge(s_gs, i + 1)
                wait(pe, s_wa, i)
                wait(pe, s_g, i)
                wait(pe, s_QN, i - 1)
                for t in range(2):
                    pe.matmul(pW[:, t, 0:128], hid[:, t * 128:t * 128 + 128], w["Bwa"][:, :], start=True, stop=True)
                    m = pe.matmul(pW[:, t, 128:192], gh[:, t * 128:t * 128 + 128], w["Bg"][:, :], start=True, stop=True)
                m.then_inc(s_wp, 1)

            def cumulate(i, p):
                pe.wait_ge(s_lw, i + 1)
                wait(pe, s_exp, i)
                wait(pe, s_O, i - 2)
                for t in range(2):
                    for x in range(2):
                        pe.matmul(pC[:, t, x * D:x * D + D], c["tri"][:, x * 128:x * 128 + 128], lw[:, t, :], start=True, stop=True)
                    m = pe.matmul(pD[:, 2 * t:2 * t + 2], lw[:, t, :], c["ind"][:, :], start=True, stop=True)
                m.then_inc(s_cum, 1)

            def turn(i, p):
                pe.wait_ge(s_el, i + 1)
                wait(pe, s_mask, 2 * i)
                for x in range(4):
                    m = pe.transpose(pT[0][:, x * 128:x * 128 + 128], RBK[:, x], c["eye"][:, :])
                m.then_inc(s_T, 1)

            def products(i, p):
                pe.wait_ge(s_FT, 2 * i + 2)
                wait(pe, s_X, 11 * i)
                for t in range(2):
                    F = lambda x, n=1: FT[:, p, t, x * 128:(x + n) * 128]
                    pe.matmul(pT[t][:, 0:256], F(2), F(0, 2), start=True, stop=True)
                    pe.matmul(pT[t][:, 256:512], F(3), F(0, 2), start=True, stop=True)
                    pe.matmul(pL[t], F(0), F(2), start=True, stop=True).then_inc(s_prod, 1)

            def inner(i, p, l):
                pe.wait_ge(s_ML, 5 * i + l)
                if l == 1:
                    pe.wait_ge(s_X0, i + 1)
                for t in range(2):
                    if l > 1:
                        pe.wait_ge(s_X, 11 * i + 1 + 2 * (l - 2) + t + 1)
                    pe.matmul(pY[t], ML[:, l - 1, t, :], XX[:, t, 0, :], start=True, stop=True).then_inc(s_Y, 1)

            def merge(i, p, l):
                if l == 1:
                    pe.wait_ge(s_X, 11 * i + 1)
                for t in range(2):
                    pe.wait_ge(s_Ys, 10 * i + 2 * (l - 1) + t + 1)
                    if l < LEVELS:
                        pe.matmul(pX[t][:, 0, :], XX[:, t, 1, :], Ys[:, t, :], start=True, stop=True)
                    pe.matmul(pX[t][:, 1, :], Ys[:, t, :], XX[:, t, 1, :], start=True, stop=True).then_inc(s_pX, 1)

            def nv(i, p, fronts):
                pe.wait_ge(s_X, 11 * i + 11)
                pe.wait_ge(s_g, fronts)
                pe.wait_ge(s_wa, fronts)
                for t in range(2):
                    m = pe.matmul(pN[:, t, :], PM[:, p, t, 256:384], V[:, p, t, :], start=True, stop=True)
                m.then_inc(s_pN, 1)

            def wu(i, p):
                pe.wait_ge(s_QN, i + 1)
                pe.wait_ge(s_qn, i + 1)
                wait(pe, s_Z, 2 * i + 1)
                for t in range(2):
                    m = pe.matmul(pWU[:, t, :], XT[:, p, t, :], QN[:, p, t, :], start=True, stop=True)
                m.then_inc(s_pWU, 1)

            def rg(i, p, fronts):
                pe.wait_ge(s_WU, i + 1)
                pe.wait_ge(s_hid, fronts)
                pe.wait_ge(s_bk, i + 1)
                for t in range(2):
                    pe.matmul(pR[:, t * 128:t * 128 + 128], WU[:, t, 0:D], PM[:, p, t, 128:256], start=True, stop=True)
                for t in range(2):
                    m = pe.matmul(pG[:, 2 * t:2 * t + 2, :], WU[:, t, 0:D], Bh[:, p, t], start=True, stop=True)
                m.then_inc(s_pRG, 1)

            def out_chunk(i, p, n, fronts):
                if n == 0:
                    pe.wait_ge(s_RG, i + 1)
                    pe.wait_ge(s_exp, fronts)
                    wait(pe, s_O, i)
                pe.wait_ge(s_Z, 2 * i + n + 1)
                for t in range(2):
                    pe.matmul(pZ[:, n, t, :], Kh[:, p, t, n, :], V[:, p, t, :], start=True, stop=False)
                    pe.matmul(pZ[:, n, t, :], Bh[:, p, t, n, :], WU[:, t, D:128], start=False, stop=False)
                    m = pe.matmul(pZ[:, n, t, :], GT[:, 2 * t + n, :], Z[:, 1 - n, t, :], start=False, stop=True)
                m.then_inc(s_pZ, 1)
                for t in range(2):
                    o, r = pO[n * CS:n * CS + CS, t, :], slice(n * CS, n * CS + CS)
                    pe.matmul(o, PM[:, p, t, 384 + n * CS:384 + n * CS + CS], V[:, p, t, :], start=True, stop=False)
                    pe.matmul(o, PM[:, p, t, 128 + n * CS:128 + n * CS + CS], WU[:, t, D:128], start=False, stop=False)
                    m = pe.matmul(o, RpT[:, t * 128 + n * CS:t * 128 + n * CS + CS], Z[:, 1 - n, t, :], start=False, stop=True)
                if n == 1:
                    m.then_inc(s_pO, 1)

            def step(i, p, front=True, inv=True, state=True):
                f, s = (i + 1, 1 - p), (i - 1, 1 - p)
                fronts = i + 2 if front else NIT
                if state: nv(*s, min(i + 1, NIT) if isinstance(i, int) else i + 1)
                if inv: products(i, p)
                if front: hidden(*f)
                if state: wu(*s)
                if inv: inner(i, p, 1)
                if front: lora(*f)
                if inv: merge(i, p, 1)
                if state: rg(*s, fronts)
                if inv: inner(i, p, 2)
                if front: cumulate(*f)
                if inv:
                    merge(i, p, 2)
                    inner(i, p, 3)
                    merge(i, p, 3)
                    inner(i, p, 4)
                if inv: merge(i, p, 4)
                if state: out_chunk(*s, 0, fronts)
                if inv: inner(i, p, 5)
                if front: turn(*f)
                if inv: merge(i, p, 5)
                if state: out_chunk(*s, 1, fronts)

            run(pe, step)

        @block.scalar
        def _(act):
            act.preload_act_table(ACT.Exp)

            def hidden(i, p):
                act.wait_ge(s_hp, i + 1)
                wait(act, s_wp, i)
                act.activation(hid[0:D, :], pH[0:D, 0:256], ACT.Tanh)
                act.activation(hid[D:128, :], pH[D:128, 0:256], ACT.Copy)
                act.activation(gh[:, :], pH[:, 256:512], ACT.Tanh, scale=0.5).then_inc(s_hid, 1)

            def values(i, p):
                wait(act, s_O, i - 1)
                act.activation(V[:, p], rkv_[:, :, i, 2 * D:3 * D], ACT.Copy).then_inc(s_V, 1)

            def tanh(i, p):
                act.wait_ge(s_wa, i + 1)
                wait(act, s_lw, i)
                act.activation(wa[:, :, :], wa[:, :, :], ACT.Tanh, scale=0.5).then_inc(s_th, 1)

            def exps(i, p):
                act.wait_ge(s_ex, i + 1)
                wait(act, s_el, i)
                wait(act, s_bk, i)
                wait(act, s_qn, i)
                wait(act, s_RG, i - 1)
                act.activation(eP[:, :, :], pC[:, :, 0:D], ACT.Exp)
                act.activation(eN[:, :, :], pC[:, :, 0:D], ACT.Exp, scale=-1.0)
                act.activation(eS[:, :, :], pC[:, :, D:128], ACT.Exp)
                act.activation(eX[:, :, :], ex[:, :, :], ACT.Exp)
                act.activation(DC[:, p, :], pD, ACT.Exp).then_inc(s_exp, 1)

            def turned(i, p):
                act.wait_ge(s_T, i + 1)
                wait(act, s_RG, i - 1)
                act.activation(FT[:, p, 0, :], pT[0][0:D, :], ACT.Copy).then_inc(s_FT, 1)

            def inner(i, p, l):
                for t in range(2):
                    act.wait_ge(s_Y, 10 * i + 2 * (l - 1) + t + 1)
                    act.activation(Ys[:, t, :], pY[t], ACT.Copy).then_inc(s_Ys, 1)

            def gates(i, p):
                act.wait_ge(s_wp, i + 1)
                act.activation(gates_[:, :, i, :], pW[:, :, 128:192], ACT.Copy).then_inc(s_g, 1)

            def nv(i, p):
                act.wait_ge(s_pN, i + 1)
                act.activation(QN[:, p, :, D:128], pN[:, :, :], ACT.Copy).then_inc(s_QN, 1)

            def wu(i, p):
                act.wait_ge(s_pWU, i + 1)
                wait(act, s_O, i)
                act.activation(WU[:, :, :], pWU[:, :, :], ACT.Copy, scale=-1.0).then_inc(s_WU, 1)

            def store(i, p):
                act.wait_ge(s_pO, i + 1)
                act.activation(rkv_[:, :, i, 0:D], pO[:, :, :], ACT.Copy).then_inc(s_O, 1)

            def step(i, p, front=True, inv=True, state=True):
                f, s = (i + 1, 1 - p), (i - 1, 1 - p)
                if state: nv(*s)
                if front: hidden(*f)
                if state: wu(*s)
                if inv: inner(i, p, 1)
                if front:
                    tanh(*f)
                    gates(*f)
                if inv:
                    inner(i, p, 2)
                    inner(i, p, 3)
                if front:
                    exps(*f)
                if inv:
                    inner(i, p, 4)
                    inner(i, p, 5)
                if front: turned(*f)
                if state: store(*s)
                if front: values(*f)

            run(act, step)

        @block.gpsimd
        def _(pool):
            def step(i, p, front=True, inv=True, state=True):
                if inv:
                    pool.wait_ge(s_mask, 2 * i + 2)
                    wait(pool, s_X, 11 * i)
                    for l in range(LEVELS):
                        pool.tensor_tensor(ML[:, l], PM[:, p, :, 0:128], rep(c["lev"][:, l * 128:l * 128 + 128], 2), ALU.mult).then_inc(s_ML, 1)
                if front:
                    f, q = i + 1, 1 - p
                    pool.wait_ge(s_exp, f + 1)
                    pool.wait_ge(s_dve, TL * f + 2)
                    wait(pool, s_pWU, f - 1)
                    pool.tensor_tensor(QN[:, q, :, 0:D], kn[:, :, :], eX[:, :, :], ALU.mult).then_inc(s_qn, 1)
            run(pool, step)

        @block.vector
        def _(dve):
            dve.memset(Z[:, 1, :, :], 0.0).then_inc(s_Z, 1)
            for n in range(2):
                r = slice(CS - n * CS, 2 * CS - n * CS)
                dve.memset(Bh[r, :, :, n, :], 0.0)
                dve.memset(Kh[r, :, :, n, :], 0.0)

            def gate(i, p):
                dve.wait_ge(s_hid, i + 1)
                dve.tensor_scalar(gh[:, :], gh[:, :], 0.5, 0.5, ALU.mult, ALU.add).then_inc(s_gs, 1)

            def lora(i, p):
                dve.wait_ge(s_wp, i + 1)
                dve.tensor_tensor(wa[:, :, :], pW[:, :, 0:128], rep(w["bwa"][:, :], 2), ALU.add).then_inc(s_wa, 1)

            def bonus(i, p):
                dve.wait_ge(s_V, i + 1)
                dve.tensor_tensor(rkv_[:, :, i, D:2 * D], V[:, p], bc(rs[:, :], D), ALU.mult)

            def decay(i, p):
                dve.wait_ge(s_th, i + 1)
                dve.tensor_scalar(lw[:, :, :], wa[:, :, 0:D], 0.5 * DECAY, 0.5 * DECAY, ALU.mult, ALU.add)
                dve.tensor_scalar(a_[:, :, :], wa[:, :, D:128], 0.5, 0.5, ALU.mult, ALU.add).then_inc(s_lw, 1)

            def tokens(i, p):
                link = linker(dve, s_dve, i * TL)
                k = rkv_[:, :, i, D:2 * D]
                wait(dve, s_qn, i)
                dve.wait_ge(s_lw, i + 1)
                link(dve.tensor_tensor(kn[:, :, :], k, rep(w["k_k"][:, :], 2), ALU.mult))
                link(dve.tensor_tensor(kn[:, :, :], kn[:, :, :], bc(rn_[:, :, i], D), ALU.mult))
                link(dve.tensor_tensor(bt[:, :, :], kn[:, :, :], a_[:, :, :], ALU.mult))
                link(dve.scalar_tensor_tensor(out=kp[:, :, :], in0=a_[:, :, :], scalar=-1.0, in1=rep(w["k_a"][:, :], 2),
                                              op0=ALU.add, op1=ALU.mult))
                link(dve.scalar_tensor_tensor(out=kp[:, :, :], in0=kp[:, :, :], scalar=1.0, in1=k, op0=ALU.add, op1=ALU.mult))
                assert link.count[0] == 5

            def bonus_sum(i, p):
                link = linker(dve, s_dve, i * TL + 5)
                r = rkv_[:, :, i, 0:D]
                link(dve.tensor_tensor(rk[:, :, :], r, rep(w["r_k"][:, :], 2), ALU.mult))
                link(dve.tensor_tensor(rk[:, :, :], rk[:, :, :], kp[:, :, :], ALU.mult))
                link(dve.tensor_reduce(rs[:, :], rk[:, :, :], AX.X, ALU.add))
                assert link.count[0] == TL - 5

            def exclusive(i, p):
                dve.wait_ge(s_cum, i + 1)
                dve.tensor_tensor(ex[:, :, :], pC[:, :, 0:D], lw[:, :, :], ALU.subtract).then_inc(s_ex, 1)

            def scale(i, p):
                dve.wait_ge(s_exp, i + 1)
                wait(dve, s_T, i)
                dve.tensor_tensor(RBK[:, 0], kn[:, :, :], eX[:, :, :], ALU.mult)
                dve.tensor_tensor(RBK[:, 1], rkv_[:, :, i, 0:D], eP[:, :, :], ALU.mult)
                dve.tensor_tensor(RBK[:, 2], bt[:, :, :], eN[:, :, :], ALU.mult)
                dve.tensor_tensor(RBK[:, 3], kp[:, :, :], eN[:, :, :], ALU.mult).then_inc(s_el, 1)

            def factors(i, p):
                wait(dve, s_O, i - 1)
                for n in range(2):
                    r = slice(n * CS, n * CS + CS)
                    dve.tensor_tensor(Bh[r, p, :, n, :], bt[r, :, :], eS[r, :, :], ALU.mult)
                    m = dve.tensor_tensor(Kh[r, p, :, n, :], kp[r, :, :], eS[r, :, :], ALU.mult)
                m.then_inc(s_bk, 1)

            def turned(i, p):
                dve.wait_ge(s_T, i + 1)
                dve.tensor_copy(FT[:, p, 1, :], pT[0][D:2 * D, :]).then_inc(s_FT, 1)

            def mask(i, p):
                wait(dve, s_O, i - 1)
                for t in range(2):
                    dve.wait_ge(s_prod, 2 * i + t + 1)
                    dve.tensor_tensor(PM[:, p, t, :], pT[t][:, :], c["mask"][:, :], ALU.mult).then_inc(s_mask, 1)
                for t in range(2):
                    m = dve.tensor_tensor(XX[:, t, 0, :], pL[t], c["neg0"][:, 0:128], ALU.mult)
                m.then_inc(s_xl, 1)
                dve.wait_ge(s_mask, 2 * i + 2)
                dve.tensor_tensor(XX[:, :, 1, :], PM[:, p, :, 0:128], rep(c["neg0"][:, 128:256], 2), ALU.mult).then_inc(s_xl, 1)
                dve.wait_ge(s_xl, 2 * i + 1)
                dve.tensor_tensor(XX[:, :, 0, :], XX[:, :, 0, :], rep(c["eye"][:, :], 2), ALU.add).then_inc(s_X0, 1)
                dve.wait_ge(s_xl, 2 * i + 2)
                dve.tensor_tensor(XX[:, :, 1, :], XX[:, :, 1, :], rep(c["eye"][:, :], 2), ALU.add).then_inc(s_X, 1)

            def merged(i, p, l):
                for t in range(2):
                    dve.wait_ge(s_pX, 10 * i + 2 * (l - 1) + t + 1)
                    if l < LEVELS:
                        dve.tensor_tensor(XX[:, t], XX[:, t], pX[t], ALU.subtract).then_inc(s_X, 1)
                    else:
                        dve.tensor_tensor(XT[:, p, t], XX[:, t, 1, :], pX[t][:, 1, :], ALU.subtract).then_inc(s_X, 1)

            def rg(i, p):
                dve.wait_ge(s_exp, i + 1)
                wait(dve, s_pO, i)
                dve.tensor_tensor(GT[:, :, :], rep(c["eye"][0:D, 0:D], 4), bc(DC[:, p, :], D), ALU.mult).then_inc(s_dI, 1)
                dve.wait_ge(s_pRG, i + 1)
                dve.tensor_tensor(RpT[:, :].rearrange("p (t n) -> p t n", t=2), pR.rearrange("p (t n) -> p t n", t=2),
                                  FT[:, p, :, 128:256], ALU.add)
                dve.wait_ge(s_dI, i + 1)
                dve.tensor_tensor(GT[:, :, :], pG, GT[:, :, :], ALU.add).then_inc(s_RG, 1)

            def new_state(i, p, n):
                dve.wait_ge(s_pZ, 2 * i + n + 1)
                dve.tensor_scalar(Z[:, n], pZ[:, n], c["keep"][:, bass.ds(2 * i + n, 1)], None, ALU.mult).then_inc(s_Z, 1)

            def step(i, p, front=True, inv=True, state=True):
                f, s = (i + 1, 1 - p), (i - 1, 1 - p)
                if inv:
                    factors(i, p)
                    bonus(i, p)
                    mask(i, p)
                if front:
                    gate(*f)
                    lora(*f)
                if inv: merged(i, p, 1)
                if front:
                    decay(*f)
                    tokens(*f)
                if inv: merged(i, p, 2)
                if front: exclusive(*f)
                if state: rg(*s)
                if inv: merged(i, p, 3)
                if front: bonus_sum(*f)
                if inv: merged(i, p, 4)
                if front: scale(*f)
                if state: new_state(*s, 0)
                if inv: merged(i, p, 5)
                if front: turned(*f)
                if state: new_state(*s, 1)

            run(dve, step)


def outputs(nc, w, h, hout, rkv, gate_, eye):
    with ExitStack() as ctx:
        sb = lambda name, shape, dt=F32: ctx.enter_context(nc.sbuf_tensor(name, shape, dt))
        sem = lambda name: ctx.enter_context(semaphore(nc, name))
        hin = sb("O_hin", [128, 2, GRP, D])
        xc = sb("O_xc", [128, 2, GRP, D])
        xn = sb("O_xn", [128, 2, GRP, D])
        sq = sb("O_sq", [128, 2, GRP, D])
        st = sb("O_st", [128, 2, 4, GRP])
        oT = sb("O_oT", [D, 2, QB])
        ho = sb("O_ho", [128, 2, GRP, D])
        pT = ctx.enter_context(nc.psum_tensor("O_pT", [128, 2, 512], F32))
        pO = ctx.enter_context(nc.psum_tensor("O_pO", [128, 2, 512], F32))
        s_in = [sem(f"O_h_in{k}") for k in range(2)]
        s_st = [sem(f"O_stored{k}") for k in range(2)]
        s_link, s_sq, s_gn, s_sqrt, s_T, s_ev, s_p, s_out = (sem("O_" + x) for x in (
            "step", "squares", "affine", "root", "turned", "turned_copied", "projected", "summed"))
        hv = h.rearrange("(g j p) c -> g p j c", p=128, j=GRP)
        ov = hout.rearrange("(g j p) c -> g p j c", p=128, j=GRP)
        block = ctx.enter_context(nc.Block())

        LINKS = 10
        CENTERED, VAR, SCALED, GATED = 2, 5, 6, 9

        @block.sync
        def _(sp):
            for k in range(2):
                sp.dma_start(hin[:, k], hv[k]).then_inc(s_in[k], 16)
            with sp.Fori(0, NG // 2 - 1) as gg:
                for k in range(2):
                    sp.wait_ge(s_out, 2 * gg + k + 3)
                    sp.dma_start(hin[:, k], hv[2 * gg + 2 + k]).then_inc(s_in[k], 16)
                    sp.dma_start(ov[2 * gg + k], ho[:, k]).then_inc(s_st[k], 16)
            for k in range(2):
                sp.wait_ge(s_out, NG - 2 + k + 3)
                sp.dma_start(ov[NG - 2 + k], ho[:, k]).then_inc(s_st[k], 16)
            for k in range(2):
                sp.wait_ge(s_st[k], 16 * (NG // 2) + 16)

        @block.vector
        def _(dve):
            for k in range(2):
                dve.sem_inc(s_st[k], 16)
            dve.sem_inc(s_out, 2)

            def finish(gg):
                for k in range(2):
                    dve.wait_ge(s_p, 2 * gg + k + 1)
                    dve.wait_ge(s_in[k], 16 * gg + 16)
                    dve.wait_ge(s_st[k], 16 * gg + 16)
                    dve.tensor_tensor(ho[:, k], hin[:, k], pO[:, k, 0:GRP * D].rearrange("p (j c) -> p j c", c=D),
                                      ALU.add).then_inc(s_out, 1)

            def normalize(gg, last=None):
                both = pairs(dve, s_link, gg * (2 * LINKS))
                js = lambda k: bass.ds((2 * gg + k) * GRP, GRP)
                S = lambda k, i: st[:, k, i, :]
                both(lambda k: dve.tensor_reduce(S(k, 0), rkv[:, js(k), 0:D], AX.X, ALU.add))
                both(lambda k: dve.tensor_scalar(S(k, 1), S(k, 0), 1.0 / D, None, ALU.mult))
                both(lambda k: dve.tensor_tensor(xc[:, k], rkv[:, js(k), 0:D], bc(S(k, 1), D), ALU.subtract),
                     lambda k: dve.wait_ge(s_gn, 2 * gg + k + 1))
                both(lambda k: dve.tensor_reduce(S(k, 2), sq[:, k], AX.X, ALU.add),
                     lambda k: dve.wait_ge(s_sq, 2 * gg + k + 1))
                both(lambda k: dve.tensor_scalar(S(k, 2), S(k, 2), 1.0 / D, GN_EPS, ALU.mult, ALU.add))
                both(lambda k: dve.reciprocal(S(k, 3), S(k, 2)))
                both(lambda k: dve.tensor_tensor(xc[:, k], xc[:, k], bc(S(k, 3), D), ALU.mult),
                     lambda k: dve.wait_ge(s_sqrt, 2 * gg + k + 1))
                both(lambda k: dve.tensor_tensor(xn[:, k], xn[:, k], rep(w["gn_b"][:, :], GRP), ALU.add),
                     lambda k: dve.wait_ge(s_gn, 2 * gg + k + 3))
                both(lambda k: dve.tensor_tensor(xn[:, k], xn[:, k], rkv[:, js(k), D:2 * D], ALU.add))
                both(lambda k: dve.tensor_tensor(xn[:, k], xn[:, k], gate_[:, js(k), :], ALU.mult))
                if last is not None:
                    finish(last)
                assert both.count[0] == LINKS

            normalize(0)
            with dve.Fori(1, NG // 2) as gg:
                normalize(gg, gg - 1)
            finish(NG // 2 - 1)

        @block.gpsimd
        def _(pool):
            pool.sem_inc(s_gn, 2)
            with pool.Fori(0, NG // 2) as gg:
                for k in range(2):
                    pool.wait_ge(s_link, gg * (2 * LINKS) + done(SCALED, k))
                    pool.wait_ge(s_T, 2 * gg + k + 1)
                    pool.tensor_tensor(xn[:, k], xc[:, k], rep(w["gn_w"][:, :], GRP), ALU.mult).then_inc(s_gn, 1)

        @block.scalar
        def _(act):
            act.preload_act_table(ACT.Sqrt)

            def statistics(gg):
                for k in range(2):
                    act.wait_ge(s_link, gg * (2 * LINKS) + done(CENTERED, k))
                    act.activation(sq[:, k], xc[:, k], ACT.Square).then_inc(s_sq, 1)
                for k in range(2):
                    act.wait_ge(s_link, gg * (2 * LINKS) + done(VAR, k))
                    act.activation(st[:, k, 3, :], st[:, k, 3, :], ACT.Sqrt).then_inc(s_sqrt, 1)

            def turned(gg):
                for k in range(2):
                    act.wait_ge(s_T, 2 * gg + k + 3)
                    pair = lambda x: oT[:, k, 0:768].rearrange("p (j x n) -> p x j n", x=2, n=128)[:, x]
                    act.activation(pair(0), pT[0:D, k, 0:384].rearrange("p (j n) -> p j n", n=128), ACT.Copy)
                    act.activation(pair(1), pT[D:128, k, 0:384].rearrange("p (j n) -> p j n", n=128), ACT.Copy)
                    act.activation(oT[:, k, 768:896], pT[0:D, k, 384:512], ACT.Copy).then_inc(s_ev, 1)

            statistics(0)
            with act.Fori(1, NG // 2) as gg:
                statistics(gg)
                turned(gg - 1)
            turned(NG // 2 - 1)

        @block.tensor
        def _(pe):
            pe.sem_inc(s_T, 2)
            with pe.Fori(0, NG // 2) as gg:
                for k in range(2):
                    pe.wait_ge(s_link, gg * (2 * LINKS) + done(GATED, k))
                    for j in range(GRP // 2):
                        pe.transpose(pT[:, k, j * 128:j * 128 + 128], xn[:, k, 2 * j:2 * j + 2, :], eye[:, :])
                    pe.transpose(pT[0:D, k, 384:512], xn[:, k, GRP - 1, :], eye[:, :]).then_inc(s_T, 1)
                for k in range(2):
                    pe.wait_ge(s_ev, 2 * gg + k + 1)
                    pe.wait_ge(s_out, 2 * gg + k + 1)
                    for j in range(GRP):
                        m = pe.matmul(pO[:, k, j * D:j * D + D], oT[:, k, j * 128:j * 128 + 128], w["Wo"][:, :], start=True, stop=True)
                    m.then_inc(s_p, 1)


def weights(nc, ctx, ins, cst):
    sb = lambda name, shape, dt=F32: ctx.enter_context(nc.sbuf_tensor(name, shape, dt))
    w = {"rkv": sb("W_rkv", [128, 192]), "Awa": sb("W_Awa", [128, 128]), "Ag": sb("W_Ag", [128, 128]),
         "Bwa": sb("W_Bwa", [128, 128]), "Bg": sb("W_Bg", [128, D]), "bwa": sb("W_bwa", [128, 128]),
         "Wo": sb("W_Wo", [D, D])}
    for n in ("k_k", "k_a", "r_k", "gn_w", "gn_b"):
        w[n] = sb("W_" + n, [128, D])
    mix = sb("W_mix", [128, 6])
    shapes = {"tri": [128, 256], "ind": [128, 2], "mask": [128, 512], "neg0": [128, 256], "lev": [128, LEVELS * 128],
              "eye": [128, 128], "keep": [D, NTT]}
    c = {k: sb("K_" + k, v) for k, v in shapes.items()}
    with semaphore(nc, "W_in") as s_in, semaphore(nc, "W_zero") as s_z, semaphore(nc, "W_mixed") as s_m, nc.Block() as block:
        n = [0]

        @block.gpsimd
        def _(pool):
            pool.memset(w["Bwa"][:, :], 0.0).then_inc(s_z, 1)

        @block.sync
        def _(sp):
            def load(dst, src, slow=False):
                n[0] += 16
                sp.dma_start(dst, src, allow_slow_non_contiguous=slow).then_inc(s_in, 16)
            for k in c:
                load(c[k][:, :], cst[k])
            row = lambda a: a.rearrange("(a c) -> a c", a=1).broadcast_to([128, D])
            for p in (0, D):
                load(mix[p:p + D, :], ins["x_mix"].rearrange("i d -> d i"), True)
                for j, k in enumerate(("W_r", "W_k", "W_v")):
                    load(w["rkv"][p:p + D, j * D:j * D + D], ins[k])
                load(w["Awa"][p:p + D, 0:D], ins["A_w"])
                load(w["Awa"][p:p + D, D:128], ins["A_a"])
                load(w["Ag"][p:p + D, :], ins["A_g"])
            load(w["bwa"][:, 0:D], row(ins["b_w"]))
            load(w["bwa"][:, D:128], row(ins["b_a"]))
            load(w["Bg"][:, :], ins["B_g"])
            load(w["Wo"][:, :], ins["W_o"])
            for k in ("k_k", "k_a", "r_k", "gn_w", "gn_b"):
                load(w[k][:, :], row(ins[k]))
            sp.wait_ge(s_z, 1)
            load(w["Bwa"][0:D, 0:D], ins["B_w"])
            load(w["Bwa"][D:128, D:128], ins["B_a"])
            sp.wait_ge(s_in, n[0])

        @block.vector
        def _(dve):
            dve.wait_ge(s_in, n[0])
            dve.tensor_scalar(mix[0:D, :], mix[0:D, :], -1.0, 1.0, ALU.mult, ALU.add).then_inc(s_m, 1)
            dve.wait_ge(s_m, 1)
            for t, col, m in (("rkv", 0, 0), ("rkv", D, 2), ("rkv", 2 * D, 3), ("Awa", 0, 1), ("Awa", D, 4), ("Ag", 0, 5)):
                v = w[t][:, col:col + (128 if t == "Ag" else D)]
                dve.tensor_scalar(v, v, mix[:, m:m + 1], None, ALU.mult)
    return w, c


def tokenizer(nc, x, W1p, b1, W2p, b2p, W3p, b3, hA):
    with ExitStack() as ctx:
        sb = lambda name, shape, dt=F32: ctx.enter_context(nc.sbuf_tensor(name, shape, dt))
        ps = lambda name, shape, dt=F32: ctx.enter_context(nc.psum_tensor(name, shape, dt))
        sem = lambda name: ctx.enter_context(semaphore(nc, name))
        IMGSZ = PAD * PAD
        xa = sb("A_xa", [128, 2, IMGSZ])
        xb = sb("A_xb", [128, 2, IMGSZ])
        w1 = sb("A_w1", [128, NCH, CH])
        w2f = sb("A_w2f", [128, NCH * 128])
        w2 = sb("A_w2", [128, 2, NCH * 128], F16)
        w3 = sb("A_w3", [128, NCH, CH])
        b1s = sb("A_b1", [CH, 1])
        b2s = sb("A_b2", [128, NCH])
        b3s = sb("A_b3", [SUB, CH])
        h1f = sb("A_h1f", [CH, TILE])
        h1 = sb("A_h1", [128, TILE], F16)
        sg = sb("A_sg", [128, NCH, TILE])
        u = sb("A_u", [128, NCH, TILE])
        hst = sb("A_hst", [SUB, 4, CH])
        pc = ps("A_pc", [CH, 512])
        pS = [ps(f"A_pS{q}", [128, 512]) for q in range(NCH)]
        po = ps("A_po", [128, 512])
        s_w = sem("A_weights_in")
        s_zero = sem("A_borders_zero")
        s_zero_a = sem("A_borders_zero_a")
        s_low = sem("A_low_part")
        s_split = sem("A_weights_split")
        s_x = [sem(f"A_image_in{k}") for k in range(2)]
        s_conv = sem("A_conv")
        s_relu = sem("A_relu")
        s_gate = sem("A_gate_logits")
        s_sig = sem("A_gates")
        s_u = sem("A_gated")
        s_out = sem("A_out")
        s_ev = sem("A_out_copied")
        s_st = sem("A_stored")
        hA_v = hA.rearrange("(t g p) c -> p t g c", g=4, p=SUB)
        block = ctx.enter_context(nc.Block())

        def view(buf, half, K, t, tap):
            v = buf[0:K, half, :].rearrange("p (r c) -> p r c", c=PAD)
            return v[:, bass.ds(tap[0] + t * ROWS, ROWS), tap[1]:tap[1] + IMG]

        def taps(half, t, whole=False):
            for q in range(NCH):
                tap = TAPS[2 * q]
                K = 128 if q < NCH - 1 or whole else CH
                yield q, K, view(xa if q < 3 else xb, half, K, t, tap)

        @block.sync
        def _(sp):
            sp.dma_start(w1[:, :, :], W1p.rearrange("(q p) c -> p q c", p=128)).then_inc(s_w, 16)
            sp.dma_start(b1s[:, :], b1.rearrange("(c a) -> c a", a=1)).then_inc(s_w, 16)
            for p in (0, CH):
                sp.dma_start(w2f[p:p + CH, :], W2p).then_inc(s_w, 16)
            sp.dma_start(b2s[:, :], b2p.rearrange("(q p) -> p q", p=128), allow_slow_non_contiguous=True).then_inc(s_w, 16)
            sp.dma_start(w3[:, :, :], W3p.rearrange("(q p) c -> p q c", p=128)).then_inc(s_w, 16)
            sp.dma_start(b3s[:, :], b3.rearrange("(a c) -> a c", a=1).broadcast_to([SUB, CH])).then_inc(s_w, 16)
            def load_image(b):
                for buf, shift in ((xa, 0), (xb, 0), (xa, 1), (xb, PAD)):
                    p0 = 0 if shift == 0 else CH
                    o = PAD + 1 - shift
                    v = buf[p0:p0 + CH, b % 2, o:o + IMG * PAD].rearrange("p (r c) -> p r c", c=PAD)
                    sp.dma_start(v[:, :, 0:IMG], x[b]).then_inc(s_x[b % 2], 16)

            for k in range(2):
                sp.wait_ge(s_zero, k + 1)
                sp.wait_ge(s_zero_a, k + 1)
                load_image(k)
            for b in range(BATCH):
                with sp.Fori(b * NT, b * NT + NT) as n:
                    sp.wait_ge(s_ev, n + 2)
                    sp.dma_start(hA_v[:, n], hst[:, :, :]).then_inc(s_st, 16)
                if b + 2 < BATCH:
                    load_image(b + 2)
            sp.wait_ge(s_st, 16 * BATCH * NT + 16)

        @block.gpsimd
        def _(pool):
            for k in range(2):
                pool.memset(xb[:, k, :], 0.0).then_inc(s_zero, 1)

        @block.tensor
        def _(pe):
            pe.wait_ge(s_w, 112)
            pe.sem_inc(s_ev, 1)
            pe.wait_ge(s_split, 3)
            pe.wait_ge(s_zero_a, 2)

            def conv(half, t):
                for q, K, v in taps(half, t, whole=True):
                    m = pe.matmul(pc[:, 0:TILE], w1[0:K, q, :], v, start=(q == 0), stop=(q == NCH - 1))
                m.then_inc(s_conv, 1)

            def gates(n):
                pe.wait_ge(s_low, n + 1)
                for q in range(NCH):
                    M = 128 if q < NCH - 1 else CH
                    for x in range(2):
                        m = pe.matmul(pS[q][0:M, 0:TILE], w2[:, x, q * 128:q * 128 + M], h1[:, :], start=(x == 0), stop=(x == 1))
                    m.then_inc(s_gate, 1)

            def out(n):
                pe.wait_ge(s_ev, n + 1)
                pe.wait_ge(s_u, NCH * n + NCH)
                for g in range(4):
                    for q in range(NCH):
                        K = 128 if q < NCH - 1 else CH
                        m = pe.matmul(po[0:SUB, g * CH:(g + 1) * CH], u[0:K, q, g * SUB:(g + 1) * SUB],
                                      w3[0:K, q, :], start=(q == 0), stop=(q == NCH - 1))
                m.then_inc(s_out, 1)

            for b in range(BATCH):
                pe.wait_ge(s_x[b % 2], 64 * (b // 2 + 1))
                conv(b % 2, 0)
                with pe.Fori(0, NT - 1) as t:
                    gates(t + b * NT)
                    conv(b % 2, t + 1)
                    out(t + b * NT)
                gates(b * NT + NT - 1)
                out(b * NT + NT - 1)

        @block.scalar
        def _(act):
            act.wait_ge(s_w, 112)
            act.preload_act_table(ACT.Sigmoid)
            with act.Fori(0, BATCH * NT) as n:
                act.wait_ge(s_conv, n + 1)
                act.activation(h1f[:, :], pc[:, 0:TILE], ACT.Relu, bias=b1s[:, 0:1])
                act.activation(h1[0:CH, :], pc[:, 0:TILE], ACT.Relu, bias=b1s[:, 0:1]).then_inc(s_relu, 1)
                for q in range(NCH):
                    M = 128 if q < NCH - 1 else CH
                    act.wait_ge(s_gate, n * NCH + q + 1)
                    act.activation(sg[0:M, q, :], pS[q][0:M, 0:TILE], ACT.Sigmoid,
                                   bias=b2s[0:M, q:q + 1], scale=1.0 / FS).then_inc(s_sig, 1)

        @block.vector
        def _(dve):
            for k in range(2):
                dve.memset(xa[:, k, :], 0.0).then_inc(s_zero_a, 1)
            dve.wait_ge(s_w, 112)
            dve.tensor_scalar(w2f[:, :], w2f[:, :], FS, None, ALU.mult).then_inc(s_split, 1)
            dve.wait_ge(s_split, 1)
            dve.tensor_copy(w2[:, 0, :], w2f[:, :]).then_inc(s_split, 1)
            dve.wait_ge(s_split, 2)
            dve.tensor_tensor(w2[:, 1, :], w2f[:, :], w2[:, 0, :], ALU.subtract).then_inc(s_split, 1)
            dve.sem_inc(s_st, 16)

            def low(n):
                dve.wait_ge(s_relu, n + 1)
                dve.tensor_tensor(h1[CH:128, :], h1f[:, :], h1[0:CH, :], ALU.subtract).then_inc(s_low, 1)

            def tile(b, t, last=False):
                n = t + b * NT
                for q, K, v in taps(b % 2, t):
                    dve.wait_ge(s_sig, n * NCH + q + 1)
                    dve.tensor_tensor(u[0:K, q, :].rearrange("p (r c) -> p r c", c=IMG),
                                      sg[0:K, q, :].rearrange("p (r c) -> p r c", c=IMG),
                                      v, ALU.mult).then_inc(s_u, 1)
                if not last:
                    low(n + 1)
                dve.wait_ge(s_out, n + 1)
                dve.wait_ge(s_st, n * 16 + 16)
                dve.tensor_tensor(hst[:, :, :], po[0:SUB, 0:4 * CH].rearrange("p (g c) -> p g c", c=CH),
                                  b3s[:, :].rearrange("p (a c) -> p a c", a=1).broadcast_to([SUB, 4, CH]), ALU.add).then_inc(s_ev, 1)

            for b in range(BATCH):
                dve.wait_ge(s_x[b % 2], 64 * (b // 2 + 1))
                low(b * NT)
                with dve.Fori(0, NT - 1) as t:
                    tile(b, t)
                tile(b, NT - 1, last=True)


def moe_constants():
    e = np.arange(EX)
    tok = np.arange(NTT)[None] * 128 + np.arange(128)[:, None]
    s, t = np.meshgrid(np.arange(128), np.arange(128), indexing="ij")
    c = {"less": np.tile((e[None] < e[:, None]).reshape(1, -1), (128, 1)),
         "base": np.tile(e[None] * CAP, (128, 1)),
         "dump": EX * CAP + tok,
         "upto": np.concatenate([s <= t, np.ones((128, 128))], 1)}
    return {k: np.ascontiguousarray(v.astype(np.float32)) for k, v in c.items()}


def layer_norm(nc, pre, h, XT, eye, rows=None):
    with ExitStack() as ctx:
        sb = lambda name, shape, dt=F32: ctx.enter_context(nc.sbuf_tensor(pre + name, shape, dt))
        sem = lambda name: ctx.enter_context(semaphore(nc, pre + name))
        hin = sb("hin", [128, 2, GRP, D])
        xc = sb("xc", [128, 2, GRP, D])
        xn = sb("xn", [128, 2, GRP, D])
        sq = sb("sq", [128, 2, GRP, D])
        st = sb("st", [128, 2, 4, GRP])
        pT = ctx.enter_context(nc.psum_tensor(pre + "pT", [128, 2, 512], F32))
        s_in = [sem(f"h_in{k}") for k in range(2)]
        s_link, s_sq, s_x, s_sqrt, s_T, s_ev = (sem(x) for x in (
            "step", "squares", "normed", "root", "transposed", "features"))
        hv = h.rearrange("(g p j) c -> g p j c" if rows is None else "(g j p) c -> g p j c", p=128, j=GRP)
        block = ctx.enter_context(nc.Block())

        LINKS = 6 if rows is None else 7
        CENTERED, VAR = 2, 5

        @block.sync
        def _(sp):
            for k in range(2):
                sp.dma_start(hin[:, k], hv[k]).then_inc(s_in[k], 16)
            with sp.Fori(0, NG // 2 - 1) as g:
                for k in range(2):
                    sp.wait_ge(s_link, g * (2 * LINKS) + done(CENTERED, k))
                    sp.dma_start(hin[:, k], hv[2 * g + 2 + k]).then_inc(s_in[k], 16)

        @block.vector
        def _(dve):
            with dve.Fori(0, NG // 2) as gg:
                both = pairs(dve, s_link, gg * (2 * LINKS))
                S = lambda k, i: st[:, k, i, :]
                both(lambda k: dve.tensor_reduce(S(k, 0), hin[:, k], AX.X, ALU.add),
                     lambda k: dve.wait_ge(s_in[k], 16 * gg + 16))
                both(lambda k: dve.tensor_scalar(S(k, 1), S(k, 0), 1.0 / D, None, ALU.mult))
                both(lambda k: dve.tensor_tensor(xc[:, k], hin[:, k], bc(S(k, 1), D), ALU.subtract),
                     lambda k: dve.wait_ge(s_x, 2 * gg + k + 1))
                both(lambda k: dve.tensor_reduce(S(k, 2), sq[:, k], AX.X, ALU.add),
                     lambda k: dve.wait_ge(s_sq, 2 * gg + k + 1))
                both(lambda k: dve.tensor_scalar(S(k, 2), S(k, 2), 1.0 / D, LN_EPS, ALU.mult, ALU.add))
                both(lambda k: dve.reciprocal(S(k, 3), S(k, 2)))
                if rows is not None:
                    both(lambda k: dve.tensor_tensor(rows[:, bass.ds((2 * gg + k) * GRP, GRP), :], xc[:, k], bc(S(k, 3), D), ALU.mult),
                         lambda k: dve.wait_ge(s_sqrt, 2 * gg + k + 1))
                assert both.count[0] == LINKS

        @block.gpsimd
        def _(pool):
            pool.sem_inc(s_x, 2)
            with pool.Fori(0, NG // 2) as gg:
                for k in range(2):
                    pool.wait_ge(s_sqrt, 2 * gg + k + 1)
                    pool.wait_ge(s_T, 2 * gg + k + 1)
                    pool.tensor_tensor(xn[:, k], xc[:, k], bc(st[:, k, 3, :], D), ALU.mult).then_inc(s_x, 1)

        @block.tensor
        def _(pe):
            pe.sem_inc(s_T, 2)
            with pe.Fori(0, NG // 2) as gg:
                for k in range(2):
                    g = 2 * gg + k
                    pe.wait_ge(s_x, g + 3)
                    pe.wait_ge(s_ev, g + 1)
                    for j in range(GRP // 2):
                        pe.transpose(pT[:, k, j * 128:j * 128 + 128], xn[:, k, 2 * j:2 * j + 2, :], eye[:, :])
                    pe.transpose(pT[0:D, k, 384:512], xn[:, k, GRP - 1, :], eye[:, :]).then_inc(s_T, 1)

        @block.scalar
        def _(act):
            act.preload_act_table(ACT.Sqrt)
            act.sem_inc(s_ev, 2)

            def statistics(gg):
                for k in range(2):
                    act.wait_ge(s_link, gg * (2 * LINKS) + done(CENTERED, k))
                    act.activation(sq[:, k], xc[:, k], ACT.Square).then_inc(s_sq, 1)
                for k in range(2):
                    act.wait_ge(s_link, gg * (2 * LINKS) + done(VAR, k))
                    act.activation(st[:, k, 3, :], st[:, k, 3, :], ACT.Sqrt).then_inc(s_sqrt, 1)

            def features(gg):
                for k in range(2):
                    act.wait_ge(s_T, 2 * gg + k + 3)
                    z = XT[0:D, bass.ds((2 * gg + k) * QB, QB)]
                    pair = lambda x: z[:, 0:768].rearrange("p (j x n) -> p x j n", x=2, n=128)[:, x]
                    act.activation(pair(0), pT[0:D, k, 0:384].rearrange("p (j n) -> p j n", n=128), ACT.Copy)
                    act.activation(pair(1), pT[D:128, k, 0:384].rearrange("p (j n) -> p j n", n=128), ACT.Copy)
                    act.activation(z[:, 768:896], pT[0:D, k, 384:512], ACT.Copy).then_inc(s_ev, 1)

            statistics(0)
            with act.Fori(1, NG // 2) as gg:
                statistics(gg)
                features(gg - 1)
            features(NG // 2 - 1)


def gating(nc, pre, XT, wg, gb, less, top, cw, chosen=None):
    with ExitStack() as ctx:
        sb = lambda name, shape, dt=F32: ctx.enter_context(nc.sbuf_tensor(pre + name, shape, dt))
        sem = lambda name: ctx.enter_context(semaphore(nc, pre + name))
        xs = sb("xs", [D, 2, QB])
        lg = sb("lg", [128, 2, GRP, EX])
        st = sb("st", [128, 2, 3, GRP])
        gt = sb("gt", [128, 2, GRP, EX, EX])
        eq = sb("eq", [128, 2, GRP, EX, EX])
        sel = sb("sel", [128, 2, GRP, EX])
        pL = ctx.enter_context(nc.psum_tensor(pre + "pL", [128, 2, 512], F32))
        s_xs, s_p, s_e, s_tie, s_link = (sem(x) for x in ("moved", "logits", "exp", "ties", "step"))
        block = ctx.enter_context(nc.Block())

        LINKS = 12 if chosen is None else 13
        SHIFTED, EQUAL = 2, 6

        own = lambda k: lg[:, k].rearrange("p j (e a) -> p j e a", a=1).broadcast_to([128, GRP, EX, EX])
        other = lambda k: lg[:, k].rearrange("p j (a e) -> p j a e", a=1).broadcast_to([128, GRP, EX, EX])
        lower = less.rearrange("p (a e f) -> p a e f", a=1, e=EX).broadcast_to([128, GRP, EX, EX])

        @block.scalar
        def _(act):
            act.preload_act_table(ACT.Exp)

            def move(gg):
                for k in range(2):
                    g = 2 * gg + k
                    act.wait_ge(s_p, g + 1)
                    act.activation(xs[:, k, :], XT[0:D, bass.ds(g * QB, QB)], ACT.Copy).then_inc(s_xs, 1)

            def exps(gg):
                for k in range(2):
                    act.wait_ge(s_link, gg * (2 * LINKS) + done(SHIFTED, k))
                    act.activation(lg[:, k], lg[:, k], ACT.Exp).then_inc(s_e, 1)

            move(0)
            with act.Fori(0, NG // 2 - 1) as gg:
                move(gg + 1)
                exps(gg)
            exps(NG // 2 - 1)

        @block.tensor
        def _(pe):
            pe.sem_inc(s_p, 2)

            def logits(gg, first=False):
                for k in range(2):
                    pe.wait_ge(s_xs, 2 * gg + k + 1)
                    if not first:
                        pe.wait_ge(s_link, (gg - 1) * (2 * LINKS) + done(0, k))
                    for j in range(GRP):
                        m = pe.matmul(pL[:, k, j * EX:j * EX + EX], xs[:, k, j * 128:j * 128 + 128], wg, start=True, stop=True)
                    m.then_inc(s_p, 1)
            logits(0, first=True)
            with pe.Fori(1, NG // 2) as gg:
                logits(gg)

        @block.gpsimd
        def _(pool):
            with pool.Fori(0, NG // 2) as gg:
                for k in range(2):
                    pool.wait_ge(s_link, gg * (2 * LINKS) + done(EQUAL, k))
                    pool.tensor_tensor(eq[:, k], eq[:, k], lower, ALU.mult).then_inc(s_tie, 1)

        @block.vector
        def _(dve):
            with dve.Fori(0, NG // 2) as gg:
                both = pairs(dve, s_link, gg * (2 * LINKS))
                js = lambda k: bass.ds((2 * gg + k) * GRP, GRP)
                both(lambda k: dve.tensor_tensor(lg[:, k], pL[:, k, 0:GRP * EX].rearrange("p (j e) -> p j e", e=EX), rep(gb, GRP), ALU.add),
                     lambda k: dve.wait_ge(s_p, 2 * gg + k + 3))
                both(lambda k: dve.tensor_reduce(st[:, k, 0, :], lg[:, k], AX.X, ALU.max))
                both(lambda k: dve.tensor_tensor(lg[:, k], lg[:, k], bc(st[:, k, 0, :], EX), ALU.subtract))
                both(lambda k: dve.tensor_reduce(st[:, k, 1, :], lg[:, k], AX.X, ALU.add),
                     lambda k: dve.wait_ge(s_e, 2 * gg + k + 1))
                both(lambda k: dve.reciprocal(st[:, k, 2, :], st[:, k, 1, :]))
                both(lambda k: dve.tensor_tensor(lg[:, k], lg[:, k], bc(st[:, k, 2, :], EX), ALU.mult))
                both(lambda k: dve.tensor_tensor(eq[:, k], other(k), own(k), ALU.is_equal))
                both(lambda k: dve.tensor_tensor(gt[:, k], other(k), own(k), ALU.is_gt))
                both(lambda k: dve.tensor_tensor(gt[:, k], gt[:, k], eq[:, k], ALU.add),
                     lambda k: dve.wait_ge(s_tie, 2 * gg + k + 1))
                both(lambda k: dve.tensor_reduce(sel[:, k], gt[:, k], AX.X, ALU.add))
                both(lambda k: dve.tensor_scalar(sel[:, k], sel[:, k], float(top), None, ALU.is_lt))
                if chosen is not None:
                    both(lambda k: dve.tensor_copy(chosen[:, js(k), :], sel[:, k]))
                both(lambda k: dve.tensor_tensor(cw[:, js(k), :], lg[:, k], sel[:, k], ALU.mult))
                assert both.count[0] == LINKS
                dve.wait_ge(s_link, gg * (2 * LINKS) + done(LINKS - 1, 1))


def experts_dense(nc, h, hout, XT, w, eye, top):
    with ExitStack() as ctx:
        sb = lambda name, shape, dt=F32: ctx.enter_context(nc.sbuf_tensor("C_" + name, shape, dt))
        ps = lambda name, shape, dt=F32: ctx.enter_context(nc.psum_tensor("C_" + name, shape, dt))
        sem = lambda name: ctx.enter_context(semaphore(nc, "C_" + name))
        G = sb("G", [128, 2, EX, QB])
        cs = sb("cs", [128, 2, GRP, EX])
        cT = sb("cT", [GRP * EX, 2, 128])
        pr = sb("pr", [128, 2, EX, D])
        acc = sb("acc", [128, GRP, D])
        hin = sb("hin", [128, 2, GRP, D])
        ho = sb("ho", [128, 2, GRP, D])
        pH = ps("pH", [128, 4, 512])
        pY = ps("pY", [128, 2, 512])
        pB = ps("pB", [128, 512])
        pC = ps("pC", [128, 512])
        pL = [pC[:, x:x + GRP * EX] for x in (128, 256)]
        cw = sb("cw", [128, 2, GRP, EX])
        lg = sb("lg", [128, 2, GRP, EX])
        sg = sb("sg", [128, 2, 3, GRP])
        gt = sb("gt", [128, 2, GRP, EX, EX])
        eq = sb("eq", [128, 2, GRP, EX, EX])
        sel = sb("sel", [128, 2, GRP, EX])
        s_lg, s_e, s_tie, s_gate = (sem(x) for x in ("logits", "exp", "ties", "gate_step"))
        LINKS = 12
        LOGITS, SHIFTED, EQUAL = 0, 2, 6
        s_in = [sem(f"h_in{k}") for k in range(2)]
        s_st = [sem(f"stored{k}") for k in range(2)]
        s_h, s_G, s_y, s_pr, s_red, s_cs, s_cT, s_cTs, s_b, s_acc, s_out = (sem(x) for x in (
            "hidden", "gelu", "products", "weighted", "summed", "weights_moved", "weights_turned", "weights_copied",
            "bias", "accumulated", "out"))
        hv = h.rearrange("(g p j) c -> g p j c", p=128, j=GRP)
        ov = hout.rearrange("(g p j) c -> g p j c", p=128, j=GRP)
        block = ctx.enter_context(nc.Block())

        @block.sync
        def _(sp):
            for k in range(2):
                sp.dma_start(hin[:, k], hv[k]).then_inc(s_in[k], 16)
            with sp.Fori(0, NG // 2 - 1) as gg:
                for k in range(2):
                    sp.wait_ge(s_out, 2 * gg + k + 1)
                    sp.dma_start(hin[:, k], hv[2 * gg + 2 + k]).then_inc(s_in[k], 16)
                    sp.dma_start(ov[2 * gg + k], ho[:, k]).then_inc(s_st[k], 16)
            for k in range(2):
                sp.wait_ge(s_out, NG - 2 + k + 1)
                sp.dma_start(ov[NG - 2 + k], ho[:, k]).then_inc(s_st[k], 16)
            for k in range(2):
                sp.wait_ge(s_st[k], 16 * (NG // 2) + 16)

        @block.gpsimd
        def _(pool):
            lower = w["less"][:, :].rearrange("p (a e f) -> p a e f", a=1, e=EX).broadcast_to([128, GRP, EX, EX])
            with pool.Fori(0, NG // 2) as q:
                for k in range(2):
                    pool.wait_ge(s_gate, q * (2 * LINKS) + done(EQUAL, k))
                    pool.tensor_tensor(eq[:, k], eq[:, k], lower, ALU.mult).then_inc(s_tie, 1)

        @block.tensor
        def _(pe):
            pe.sem_inc(s_G, 4)
            pe.sem_inc(s_pr, 2)

            def hidden(g, k, e):
                for half in range(2):
                    u = g * (2 * EX) + 2 * e + half
                    pe.wait_ge(s_G, u + 1)
                    pe.matmul(pH[:, (2 * e + half) % 4, 0:QH], w["W1"][:, 0, e, :], XT[:, bass.ds(g * QB + half * QH, QH)],
                              start=True, stop=False)
                    pe.matmul(pH[:, (2 * e + half) % 4, 0:QH], w["W1"][:, 1, e, :], XT[:, bass.ds(g * QB + half * QH, QH)],
                              start=False, stop=True).then_inc(s_h, 1)

            def tile(g, k, j):
                if j == 0:
                    pe.wait_ge(s_G, g * (2 * EX) + 2 * EX + 4)
                pe.wait_ge(s_pr, g * GRP + j + 1)
                y = (k + j) % 2
                for e in range(EX):
                    m = pe.matmul(pY[:, y, e * D:e * D + D], G[:, k, e, j * 128:j * 128 + 128], w["W2"][:, e, :],
                                  start=True, stop=True)
                m.then_inc(s_y, 1)

            def logits(q):
                for k in range(2):
                    for j in range(GRP):
                        for x in range(2):
                            m = pe.matmul(pL[k][:, j * EX:j * EX + EX], XT[:, bass.ds((2 * q + k) * QB + j * 128, 128)],
                                          w["gate"][:, x, :], start=(x == 0), stop=(x == 1))
                m.then_inc(s_lg, 1)

            def turn_weights(g, k, q):
                pe.wait_ge(s_cs, g + 1)
                if q is not None:
                    pe.wait_ge(s_gate, q * (2 * LINKS) + done(LOGITS, 1))
                if not (isinstance(g, int) and g == 0):
                    pe.wait_ge(s_cTs, g)
                pe.matmul(pC[0:GRP * EX, 0:128], cs[:, k].rearrange("p j e -> p (j e)"), eye[:, :], start=True, stop=True).then_inc(s_cT, 1)

            def bias(g, k):
                pe.wait_ge(s_cTs, g + 1)
                if not (isinstance(g, int) and g == 0):
                    pe.wait_ge(s_acc, g)
                pe.matmul(pB[:, 0:GRP * D], cT[:, k, :], w["b2"][:, :], start=True, stop=True).then_inc(s_b, 1)

            def step(g, k, q=None, ahead=True, out=True):
                for e in range(EX):
                    if ahead: hidden(g + 1, 1 - k, e)
                    if q is not None and e == 0: logits(q)
                    if out and e < GRP: tile(g, k, e)
                    if out and e == GRP - 3: turn_weights(g, k, q)
                    if out and e == EX - 1: bias(g, k)

            step(-1, 1, q=0, out=False)
            step(0, 0, q=1)
            step(1, 1)
            with pe.Fori(1, (NG - 2) // 2) as m:
                step(2 * m, 0, q=m + 1)
                step(2 * m + 1, 1)
            step(NG - 2, 0)
            step(NG - 1, 1, ahead=False)

        @block.scalar
        def _(act):
            act.preload_act_table(ACT.Gelu)

            def gate_exp(q):
                for k in range(2):
                    act.wait_ge(s_gate, q * (2 * LINKS) + done(SHIFTED, k))
                    act.activation(lg[:, k], lg[:, k], ACT.Exp).then_inc(s_e, 1)

            def step(g, k, pair=None, ahead=True, out=True):
                f, q = g + 1, 1 - k
                if ahead and not (isinstance(g, int) and g <= 0):
                    act.wait_ge(s_y, g * GRP)
                for e in range(EX):
                    for half in range(2):
                        if ahead:
                            act.wait_ge(s_h, f * (2 * EX) + 2 * e + half + 1)
                            act.activation(G[:, q, e, half * QH:half * QH + QH], pH[:, (2 * e + half) % 4, 0:QH],
                                           ACT.Gelu, bias=w["b1"][:, e:e + 1], scale=1.0 / (FS * FS)).then_inc(s_G, 1)
                    if pair is not None and e == 4: gate_exp(pair)
                    if out and e == GRP - 1:
                        act.wait_ge(s_cT, g + 1)
                        act.activation(cT[:, k, :], pC[0:GRP * EX, 0:128], ACT.Copy).then_inc(s_cTs, 1)

            gate_exp(0)
            step(-1, 1, out=False)
            step(0, 0, pair=1)
            step(1, 1)
            with act.Fori(1, (NG - 2) // 2) as m:
                step(2 * m, 0, pair=m + 1)
                step(2 * m + 1, 1)
            step(NG - 2, 0)
            step(NG - 1, 1, ahead=False)

        @block.vector
        def _(dve):
            for k in range(2):
                dve.sem_inc(s_st[k], 16)
            own = lambda k: lg[:, k].rearrange("p j (e a) -> p j e a", a=1).broadcast_to([128, GRP, EX, EX])
            other = lambda k: lg[:, k].rearrange("p j (a e) -> p j a e", a=1).broadcast_to([128, GRP, EX, EX])
            gate_ops = (
                lambda k: dve.scalar_tensor_tensor(out=lg[:, k], in0=pL[k].rearrange("p (j e) -> p j e", e=EX),
                                                   scalar=1.0 / (FS * FS), in1=rep(w["gb"][:, :], GRP), op0=ALU.mult, op1=ALU.add),
                lambda k: dve.tensor_reduce(sg[:, k, 0, :], lg[:, k], AX.X, ALU.max),
                lambda k: dve.tensor_tensor(lg[:, k], lg[:, k], bc(sg[:, k, 0, :], EX), ALU.subtract),
                lambda k: dve.tensor_reduce(sg[:, k, 1, :], lg[:, k], AX.X, ALU.add),
                lambda k: dve.reciprocal(sg[:, k, 2, :], sg[:, k, 1, :]),
                lambda k: dve.tensor_tensor(lg[:, k], lg[:, k], bc(sg[:, k, 2, :], EX), ALU.mult),
                lambda k: dve.tensor_tensor(eq[:, k], other(k), own(k), ALU.is_equal),
                lambda k: dve.tensor_tensor(gt[:, k], other(k), own(k), ALU.is_gt),
                lambda k: dve.tensor_tensor(gt[:, k], gt[:, k], eq[:, k], ALU.add),
                lambda k: dve.tensor_reduce(sel[:, k], gt[:, k], AX.X, ALU.add),
                lambda k: dve.tensor_scalar(sel[:, k], sel[:, k], float(top), None, ALU.is_lt),
                lambda k: dve.tensor_tensor(cw[:, k], lg[:, k], sel[:, k], ALU.mult))
            assert len(gate_ops) == LINKS

            def gate(both, q, n):
                def before(k):
                    if n == LOGITS:
                        dve.wait_ge(s_lg, q + 1)
                    if n == SHIFTED + 1:
                        dve.wait_ge(s_e, 2 * q + k + 1)
                    if n == EQUAL + 2:
                        dve.wait_ge(s_tie, 2 * q + k + 1)
                both(gate_ops[n], before)

            def gated(q):
                dve.wait_ge(s_gate, q * (2 * LINKS) + done(LINKS - 1, 1))

            def pair(gg, last=False):
                both = pairs(dve, s_gate, (gg + 1) * (2 * LINKS))
                gated(gg)
                for k in range(2):
                    dve.tensor_copy(cs[:, k], cw[:, k]).then_inc(s_cs, 1)
                dve.wait_ge(s_cs, 2 * gg + 2)
                for k in range(2):
                    g = 2 * gg + k
                    for j in range(GRP):
                        y = (k + j) % 2
                        dve.wait_ge(s_y, g * GRP + j + 1)
                        cb = cs[:, k, j, :].rearrange("p (e a) -> p e a", a=1).broadcast_to([128, EX, D])
                        dve.tensor_tensor(pr[:, y], pY[:, y, :].rearrange("p (e c) -> p e c", e=EX), cb, ALU.mult).then_inc(s_pr, 1)
                        dve.wait_ge(s_pr, g * GRP + j + 3)
                        dve.tensor_reduce(acc[:, j, :], pr[:, y].rearrange("p e c -> p c e"), AX.X, ALU.add).then_inc(s_red, 1)
                        slot = k * GRP + j
                        if not last and slot not in (3, 4):
                            gate(both, gg + 1, slot if slot < 3 else slot - 2)
                    dve.wait_ge(s_red, g * GRP + GRP)
                    dve.wait_ge(s_b, g + 1)
                    dve.tensor_tensor(acc[:, :, :], acc[:, :, :], pB[:, 0:GRP * D].rearrange("p (j c) -> p j c", c=D),
                                      ALU.add).then_inc(s_acc, 1)
                    dve.wait_ge(s_acc, g + 1)
                    dve.wait_ge(s_in[k], 16 * gg + 16)
                    dve.wait_ge(s_st[k], 16 * gg + 16)
                    dve.tensor_tensor(ho[:, k], hin[:, k], acc[:, :, :], ALU.add).then_inc(s_out, 1)

            first = pairs(dve, s_gate, 0)
            for n in range(LINKS):
                gate(first, 0, n)
            with dve.Fori(0, NG // 2 - 1) as gg:
                pair(gg)
            pair(NG // 2 - 1, last=True)


def moe1_weights(nc, ctx, ins, cst):
    sb = lambda name, shape, dt=F32: ctx.enter_context(nc.sbuf_tensor("CW_" + name, shape, dt))
    w = {"gate": sb("gate", [128, 2, EX], F16), "gb": sb("gb", [128, EX]), "W1": sb("W1", [128, 2, EX, F1], F16), "b1": sb("b1", [F1, EX]),
         "W2": sb("W2", [F1, EX, D]), "b2": sb("b2", [GRP * EX, GRP * D]), "less": sb("less", [128, EX * EX])}
    W1f = ctx.enter_context(nc.sbuf_tensor("CW_W1f", [128, EX, F1], F32))
    gatef = ctx.enter_context(nc.sbuf_tensor("CW_gatef", [128, EX], F32))
    n = [0]
    with semaphore(nc, "CW_in") as s_in, semaphore(nc, "CW_zero") as s_z, semaphore(nc, "CW_split") as s_split, nc.Block() as block:
        @block.gpsimd
        def _(pool):
            pool.memset(w["b2"][:, :], 0.0).then_inc(s_z, 1)

        @block.sync
        def _(sp):
            def load(dst, src, slow=False):
                n[0] += 16
                sp.dma_start(dst, src, allow_slow_non_contiguous=slow).then_inc(s_in, 16)
            load(w["less"][:, :], cst["less"])
            for p in (0, D):
                load(gatef[p:p + D, :], ins["gate_w"])
                load(W1f[p:p + D, :, :], ins["W1"].rearrange("e d f -> d e f"))
            load(w["gb"][:, :], ins["gate_b"].rearrange("(a c) -> a c", a=1).broadcast_to([128, EX]))
            load(w["b1"][:, :], ins["b1"].rearrange("e f -> f e"), True)
            load(w["W2"][:, :, :], ins["W2"].rearrange("e f d -> f e d"))
            sp.wait_ge(s_z, 1)
            for j in range(GRP):
                load(w["b2"][j * EX:j * EX + EX, j * D:j * D + D], ins["b2"])
            sp.wait_ge(s_in, n[0])

        @block.vector
        def _(dve):
            dve.wait_ge(s_in, n[0])
            parts = ((W1f[:, :, :], w["W1"]), (gatef[:, :], w["gate"]))
            for f, _ in parts:
                dve.tensor_scalar(f, f, FS, None, ALU.mult).then_inc(s_split, 1)
            dve.wait_ge(s_split, 2)
            for f, p in parts:
                dve.tensor_copy(p[:, 0], f).then_inc(s_split, 1)
            dve.wait_ge(s_split, 4)
            for f, p in parts:
                dve.tensor_tensor(p[:, 1], f, p[:, 0], ALU.subtract)
    return w


def slots(nc, c, chosen, cw, dest, src, wt):
    N = NTT * EX
    with ExitStack() as ctx:
        sb = lambda name, shape, dt=F32: ctx.enter_context(nc.sbuf_tensor("S_" + name, shape, dt))
        sem = lambda name: ctx.enter_context(semaphore(nc, "S_" + name))
        cnt = sb("cnt", [128, NTT, EX])
        tot = sb("tot", [128, NTT, EX])
        run_ = sb("run", [128, NTT, EX])
        one = sb("one", [128, NTT])
        T = sb("T", [128, NTT])
        B = sb("B", [128, NTT])
        kept = sb("kept", [128, NTT])
        df = sb("df", [128, NTT])
        sf = sb("sf", [128, NTT])
        pI = ctx.enter_context(nc.psum_tensor("S_pI", [128, 4, 512], F32))
        s_p, s_l = sem("counted"), sem("step")
        block = ctx.enter_context(nc.Block())
        flat = chosen[:, :, :].rearrange("p j e -> p (j e)")

        @block.tensor
        def _(pe):
            for x in range(2):
                for half in range(2):
                    m = pe.matmul(pI[:, 2 * x + half, 0:N // 2], c["upto"][:, x * 128:x * 128 + 128],
                                  flat[:, half * (N // 2):(half + 1) * (N // 2)], start=True, stop=True)
            m.then_inc(s_p, 1)

        @block.vector
        def _(dve):
            link = linker(dve, s_l)
            dve.wait_ge(s_p, 1)
            v = lambda t: t[:, :, :].rearrange("p (x j) e -> p x (j e)", x=2)
            link(dve.tensor_copy(v(cnt), pI[:, 0:2, 0:N // 2]))
            link(dve.tensor_copy(v(tot), pI[:, 2:4, 0:N // 2]))
            link(dve.memset(one[:, :], 1.0))
            for e in range(EX):
                m = dve.tensor_tensor_scan(run_[:, :, e], one[:, :], tot[:, :, e], 0.0, ALU.mult, ALU.add)
            link(m)
            link(dve.tensor_tensor(run_[:, :, :], run_[:, :, :], tot[:, :, :], ALU.subtract))
            link(dve.tensor_tensor(cnt[:, :, :], cnt[:, :, :], run_[:, :, :], ALU.add))
            link(dve.tensor_tensor(cnt[:, :, :], cnt[:, :, :], chosen[:, :, :], ALU.mult))
            link(dve.tensor_reduce(T[:, :], cnt[:, :, :], AX.X, ALU.add))
            link(dve.tensor_tensor(tot[:, :, :], chosen[:, :, :], rep(c["base"][:, :], NTT), ALU.mult))
            link(dve.tensor_reduce(B[:, :], tot[:, :, :], AX.X, ALU.add))
            link(dve.tensor_scalar(kept[:, :], T[:, :], CAP + 0.5, None, ALU.is_lt))
            link(dve.tensor_reduce(wt[:, :], cw[:, :, :], AX.X, ALU.add))
            link(dve.tensor_tensor(wt[:, :], wt[:, :], kept[:, :], ALU.mult))
            link(dve.scalar_tensor_tensor(out=df[:, :], in0=T[:, :], scalar=-1.0, in1=B[:, :], op0=ALU.add, op1=ALU.add))
            link(dve.tensor_tensor(df[:, :], df[:, :], c["dump"][:, :], ALU.subtract))
            link(dve.tensor_tensor(df[:, :], df[:, :], kept[:, :], ALU.mult))
            link(dve.tensor_tensor(df[:, :], df[:, :], c["dump"][:, :], ALU.add))
            link(dve.tensor_scalar(sf[:, :], T[:, :], -1.0, float(CAP - 1), ALU.add, ALU.min))
            link(dve.tensor_tensor(sf[:, :], sf[:, :], B[:, :], ALU.add))
            link(dve.tensor_copy(dest[:, :], df[:, :]))
            link(dve.tensor_copy(src[:, :], sf[:, :]))


def clear_rows(nc, buf, z, s_z, s_zero):
    with nc.Block() as block:
        @block.vector
        def _(dve):
            dve.memset(z[:, :], 0.0).then_inc(s_z, 1)

        @block.sync
        def _(sp):
            sp.wait_ge(s_z, 1)
            bv = buf[0:EX * CAP, :].rearrange("(e p r) c -> e p (r c)", e=EX, p=SR)
            for e in range(EX):
                sp.dma_start(bv[e], z[:, :]).then_inc(s_zero, 16)


def dispatch(nc, rows, dest, buf, s_zero):
    with semaphore(nc, "X_sent") as s_sent, nc.Block() as block:
        @block.gpsimd
        def _(pool):
            pool.wait_ge(s_zero, 16 * EX)
            for j in range(NTT):
                pool.indirect_dma_start(buf, bass.IndirectOffsetOnAxis(ap=dest[:, j:j + 1], axis=0), rows[:, j, :], None).then_inc(s_sent, 16)
            pool.wait_ge(s_sent, 16 * NTT)


def experts_sparse(nc, ins, buf, ybuf, eye):
    NU = EX * CU
    XB = 4
    with ExitStack() as ctx:
        sb = lambda name, shape, dt=F32: ctx.enter_context(nc.sbuf_tensor("E_" + name, shape, dt))
        ps = lambda name, shape, dt=F32: ctx.enter_context(nc.psum_tensor("E_" + name, shape, dt))
        sem = lambda name: ctx.enter_context(semaphore(nc, "E_" + name))
        w1 = sb("w1", [128, 2, F2])
        w2 = sb("w2", [128, 2, 2, D])
        b1 = sb("b1", [128, 2, 2])
        b2 = sb("b2", [SR, 2, D])
        xin = sb("xin", [SR, XB, ST, D])
        xT = sb("xT", [128, 2, UT])
        hid = sb("hid", [128, 2, 2, UT])
        y = sb("y", [SR, 2, ST, D])
        pT = ps("pT", [128, 2, 512])
        pH = ps("pH", [128, 2, 2, 512])
        pY = ps("pY", [128, 2, 512])
        s_w = [sem(f"weights_in{k}") for k in range(2)]
        s_x = [sem(f"rows_in{k}") for k in range(XB)]
        s_z = sem("zero_rows")
        s_st = [sem(f"stored{k}") for k in range(2)]
        s_T, s_xT, s_h, s_ra, s_rd, s_y, s_out = (sem(x) for x in (
            "turned", "features", "hidden", "relu_act", "relu_dve", "products", "out"))
        bv = buf[0:EX * CAP, :].rearrange("(u p s) c -> u p s c", p=SR, s=ST)
        yv = ybuf.rearrange("(u p s) c -> u p s c", p=SR, s=ST)
        w1v = ins["w1"].rearrange("e d f -> e d f")
        w2v = ins["w2"].rearrange("e (x f) d -> e f x d", x=2)
        b1v = ins["b1"].rearrange("e (x f) -> e f x", x=2)
        block = ctx.enter_context(nc.Block())

        def wait(eng, s, n):
            if not (isinstance(n, int) and n <= 0):
                eng.wait_ge(s, n)

        def run(eng, step):
            step(-1, 7, mid=False, back=False)
            step(0, 0, back=False)
            for u in range(1, 8):
                step(u, u)
            with eng.Fori(1, EX // 2 - 1) as m:
                for q in range(8):
                    step(8 * m + q, q)
            for q in range(7):
                step(NU - 8 + q, q)
            step(NU - 1, 7, front=False)
            step(NU, 0, front=False, mid=False)

        @block.sync
        def _(sp):
            def load_w(e, k):
                sp.dma_start(w1[0:D, k, :], w1v[e]).then_inc(s_w[k], 16)
                sp.dma_start(w2[:, k], w2v[e]).then_inc(s_w[k], 16)
                sp.dma_start(b1[:, k, :], b1v[e], allow_slow_non_contiguous=True).then_inc(s_w[k], 16)
                sp.dma_start(b2[:, k, :], ins["b2"][e:e + 1, :].broadcast_to([SR, D]) if isinstance(e, int)
                             else ins["b2"][bass.ds(e, 1), :].broadcast_to([SR, D])).then_inc(s_w[k], 16)
            def unit(u, q, load=True, store=True):
                if load:
                    sp.wait_ge(s_T, u + 1)
                    sp.dma_start(xin[:, q % XB], bv[u + XB]).then_inc(s_x[q % XB], 16)
                if store:
                    sp.wait_ge(s_out, u - 1)
                    sp.dma_start(yv[u - 2], y[:, q % 2]).then_inc(s_st[q % 2], 16)

            load_w(0, 0)
            for k in range(XB):
                sp.dma_start(xin[:, k], bv[k]).then_inc(s_x[k], 16)
            load_w(1, 1)
            for q in range(8):
                unit(q, q, store=q >= 2)
                if q == 6:
                    load_w(2, 0)
            with sp.Fori(1, EX // 2 - 1) as m:
                for q in range(8):
                    unit(8 * m + q, q)
                    if q % 4 == 2:
                        load_w(2 * m + q // 4 + 1, (q // 4 + 1) % 2)
            for q in range(8):
                unit(NU - 8 + q, q, load=q < 8 - XB)
                if q == 2:
                    load_w(EX - 1, 1)
            for q in range(2):
                unit(NU + q, q, load=False)
            for k in range(2):
                sp.wait_ge(s_st[k], 16 * (NU // 2) + 16)

        @block.tensor
        def _(pe):
            def turn(u, q):
                k = q % 2
                wait(pe, s_xT, u - 1)
                x = q % XB
                if isinstance(u, int):
                    pe.wait_ge(s_x[x], 16 * (u // XB) + 16)
                else:
                    pe.wait_ge(s_x[x], (u - q) * (16 // XB) + 16 * (q // XB) + 16)
                for s in range(ST // 2):
                    pe.transpose(pT[:, k, s * SR:s * SR + SR], xin[:, x, 2 * s:2 * s + 2, :], eye[0:SR, 0:SR])
                pe.transpose(pT[0:D, k, 2 * SR:3 * SR], xin[:, x, ST - 1, :], eye[0:SR, 0:SR]).then_inc(s_T, 1)

            def hidden(u, q):
                k, kw = q % 2, q // 4
                pe.wait_ge(s_xT, u + 1)
                if isinstance(u, int) and u == 0:
                    pe.wait_ge(s_z, 1)
                wait(pe, s_ra, u - 1)
                wait(pe, s_rd, u - 1)
                if q % 4 == 0:
                    pe.wait_ge(s_w[kw], 64 * (u // 8) + 64 if isinstance(u, int) else (u - q) * 8 + 64)
                for f in range(2):
                    pe.matmul(pH[:, k, f, 0:UT], w1[:, kw, f * 128:f * 128 + 128], xT[:, k, :], start=True, stop=True).then_inc(s_h, 1)

            def multiply(u, q):
                k, kw = q % 2, q // 4
                pe.wait_ge(s_ra, u + 1)
                pe.wait_ge(s_rd, u + 1)
                wait(pe, s_out, u - 1)
                for s in range(ST):
                    for f in range(2):
                        m = pe.matmul(pY[0:SR, k, s * D:s * D + D], hid[:, k, f, s * SR:s * SR + SR], w2[:, kw, f, :],
                                      start=(f == 0), stop=(f == 1))
                m.then_inc(s_y, 1)

            def step(u, q, front=True, mid=True, back=True):
                if front: turn(u + 1, (q + 1) % 8)
                if mid: hidden(u, q)
                if back: multiply(u - 1, (q - 1) % 8)
            run(pe, step)

        @block.scalar
        def _(act):
            act.preload_act_table(ACT.Exp)

            def step(u, q, front=True, mid=True, back=True):
                if front:
                    k = (q + 1) % 2
                    act.wait_ge(s_T, u + 2)
                    wait(act, s_h, 2 * u)
                    pairs = lambda x: xT[0:D, k, 0:4 * SR].rearrange("p (j x n) -> p x j n", x=2, n=SR)[:, x]
                    act.activation(pairs(0), pT[0:D, k, 0:2 * SR].rearrange("p (j n) -> p j n", n=SR), ACT.Copy)
                    act.activation(pairs(1), pT[D:128, k, 0:2 * SR].rearrange("p (j n) -> p j n", n=SR), ACT.Copy)
                    act.activation(xT[0:D, k, 4 * SR:UT], pT[0:D, k, 2 * SR:3 * SR], ACT.Copy).then_inc(s_xT, 1)
                if mid:
                    k = q % 2
                    act.wait_ge(s_h, 2 * u + 1)
                    wait(act, s_y, u - 1)
                    act.activation(hid[:, k, 0, :], pH[:, k, 0, 0:UT], ACT.Relu, bias=b1[:, q // 4, 0:1]).then_inc(s_ra, 1)
            run(act, step)

        @block.vector
        def _(dve):
            for k in range(2):
                dve.sem_inc(s_st[k], 16)
            dve.memset(w1[D:128, :, :], 0.0)
            dve.memset(xT[D:128, :, :], 0.0).then_inc(s_z, 1)

            def step(u, q, front=True, mid=True, back=True):
                if mid:
                    k = q % 2
                    dve.wait_ge(s_h, 2 * u + 2)
                    wait(dve, s_y, u - 1)
                    dve.tensor_scalar(hid[:, k, 1, :], pH[:, k, 1, 0:UT], b1[:, q // 4, 1:2], 0.0, ALU.add, ALU.max).then_inc(s_rd, 1)
                if back:
                    v, r = u - 1, (q - 1) % 8
                    k = r % 2
                    dve.wait_ge(s_y, v + 1)
                    dve.wait_ge(s_st[k], 16 * (v // 2) + 16 if isinstance(v, int) else (u - q) * 8 + (16 * ((q - 1) // 2) + 16))
                    dve.tensor_tensor(y[:, k], pY[0:SR, k, 0:ST * D].rearrange("p (s c) -> p s c", c=D),
                                      rep(b2[:, r // 4, :], ST), ALU.add).then_inc(s_out, 1)
            run(dve, step)


def combine(nc, h, hout, ybuf, src, wt):
    with ExitStack() as ctx:
        sb = lambda name, shape, dt=F32: ctx.enter_context(nc.sbuf_tensor("G_" + name, shape, dt))
        sem = lambda name: ctx.enter_context(semaphore(nc, "G_" + name))
        hin = sb("hin", [128, 2, GRP, D])
        ho = sb("ho", [128, 2, GRP, D])
        gy = sb("gy", [128, 2, GRP, D])
        yy = sb("yy", [128, GRP, D])
        ok = sb("ok", [128, GRP, D], U32)
        hi = sb("hi", [128, GRP, D], U32)
        lo = sb("lo", [128, GRP, D], U32)
        big = sb("big", [128, 2, GRP, D])
        tick = sb("tick", [128, 1])
        s_in = [sem(f"h_in{k}") for k in range(2)]
        s_st = [sem(f"stored{k}") for k in range(2)]
        s_g = [sem(f"gathered{k}") for k in range(2)]
        s_l, s_k, s_out, s_used = sem("step"), sem("constants"), sem("out"), sem("gather_used")
        hv = h.rearrange("(g j p) c -> g p j c", p=128, j=GRP)
        ov = hout.rearrange("(g j p) c -> g p j c", p=128, j=GRP)
        block = ctx.enter_context(nc.Block())

        @block.gpsimd
        def _(pool):
            for g in range(NG):
                if g >= 2:
                    pool.wait_ge(s_used, g - 1)
                for j in range(GRP):
                    pool.indirect_dma_start(gy[:, g % 2, j, :], None, ybuf,
                                            bass.IndirectOffsetOnAxis(ap=src[:, g * GRP + j:g * GRP + j + 1], axis=0)).then_inc(s_g[g % 2], 16)

        LINKS = 9

        @block.sync
        def _(sp):
            for k in range(2):
                sp.dma_start(hin[:, k], hv[k]).then_inc(s_in[k], 16)
            with sp.Fori(0, NG // 2 - 1) as gg:
                for k in range(2):
                    sp.wait_ge(s_out, 2 * gg + k + 1)
                    sp.dma_start(hin[:, k], hv[2 * gg + 2 + k]).then_inc(s_in[k], 16)
                    sp.dma_start(ov[2 * gg + k], ho[:, k]).then_inc(s_st[k], 16)
            for k in range(2):
                sp.wait_ge(s_out, NG - 2 + k + 1)
                sp.dma_start(ov[NG - 2 + k], ho[:, k]).then_inc(s_st[k], 16)
            for k in range(2):
                sp.wait_ge(s_st[k], 16 * (NG // 2) + 16)

        @block.vector
        def _(dve):
            for k in range(2):
                dve.sem_inc(s_st[k], 16)
            dve.memset(big[:, 0], 10000.0)
            dve.memset(big[:, 1], -10000.0).then_inc(s_k, 1)
            dve.wait_ge(s_k, 1)
            with dve.Fori(0, NG // 2) as gg:
                for k in range(2):
                    g = 2 * gg + k
                    link = linker(dve, s_l, g * LINKS)
                    dve.wait_ge(s_g[k], 16 * GRP * gg + 16 * GRP)
                    link(dve.tensor_tensor(gy[:, k], gy[:, k], bc(wt[:, bass.ds(g * GRP, GRP)], D), ALU.mult))
                    link(dve.tensor_tensor(ok[:, :, :], gy[:, k], gy[:, k], ALU.is_equal))
                    link(dve.tensor_scalar(hi[:, :, :], gy[:, k], FMAX, None, ALU.is_gt))
                    link(dve.tensor_scalar(lo[:, :, :], gy[:, k], -FMAX, None, ALU.is_lt))
                    link(dve.memset(yy[:, :, :], 0.0))
                    dve.memset(tick[:, :], 0.0)
                    link(dve.copy_predicated(yy[:, :, :], ok[:, :, :], gy[:, k]))
                    dve.sem_inc(s_used, 1)
                    dve.memset(tick[:, :], 0.0)
                    link(dve.copy_predicated(yy[:, :, :], hi[:, :, :], big[:, 0]))
                    dve.memset(tick[:, :], 0.0)
                    link(dve.copy_predicated(yy[:, :, :], lo[:, :, :], big[:, 1]))
                    dve.wait_ge(s_in[k], 16 * gg + 16)
                    dve.wait_ge(s_st[k], 16 * gg + 16)
                    link(dve.tensor_tensor(ho[:, k], hin[:, k], yy[:, :, :], ALU.add))
                    dve.sem_inc(s_out, 1)
                    assert link.count[0] == LINKS


def split_features(nc, pre, h, Fhl, ident, ftok=None):
    unit = ftok is not None
    with ExitStack() as ctx:
        sb = lambda name, shape, dt=F32: ctx.enter_context(nc.sbuf_tensor(name, shape, dt))
        ps = lambda name, shape, dt=F32: ctx.enter_context(nc.psum_tensor(name, shape, dt))
        sem = lambda name: ctx.enter_context(semaphore(nc, name))
        hin = sb(pre + "hin", [128, 2, GRP, D])
        xc = sb(pre + "xc", [128, 2, GRP, D])
        sq = sb(pre + "sq", [128, 2, GRP, D])
        st = sb(pre + "st", [128, 2, 8, GRP])
        pT = ps(pre + "pT", [128, 2, GRP * 128 + 128], F16)
        tk = None if unit else sb(pre + "tk", [128, 2, GRP, 2 * D], F16)
        s_in = [sem(f"{pre}h_in{k}") for k in range(2)]
        s_link = sem(pre + "norm_step")
        s_sqrt = sem(pre + "root")
        s_sq = sem(pre + "squares")
        s_T = sem(pre + "transposed")
        s_ev = sem(pre + "features")
        hv = h.rearrange("(g p j) c -> g p j c", p=128, j=GRP)
        block = ctx.enter_context(nc.Block())

        LINKS = 14 if unit else 10
        CENTERED, VAR, SQUARE, PARTS = 2, 5, 7, LINKS - 1
        roots = 4 if unit else 2

        @block.sync
        def _(sp):
            sp.dma_start(hin[:, 0], hv[0]).then_inc(s_in[0], 16)
            sp.dma_start(hin[:, 1], hv[1]).then_inc(s_in[1], 16)
            with sp.Fori(0, NG // 2 - 1) as g:
                for k in range(2):
                    sp.wait_ge(s_link, g * (2 * LINKS) + done(CENTERED, k))
                    sp.dma_start(hin[:, k], hv[2 * g + 2 + k]).then_inc(s_in[k], 16)

        @block.vector
        def _(dve):
            with dve.Fori(0, NG // 2) as gg:
                both = pairs(dve, s_link, gg * (2 * LINKS))
                S = lambda k, i: st[:, k, i, :]
                js = lambda k: bass.ds((2 * gg + k) * GRP, GRP)
                both(lambda k: dve.tensor_reduce(S(k, 0), hin[:, k], AX.X, ALU.add),
                     lambda k: dve.wait_ge(s_in[k], 16 * gg + 16))
                both(lambda k: dve.tensor_scalar(S(k, 1), S(k, 0), 1.0 / D, None, ALU.mult))
                both(lambda k: dve.tensor_tensor(xc[:, k], hin[:, k], bc(S(k, 1), D), ALU.subtract))
                both(lambda k: dve.tensor_reduce(S(k, 2), sq[:, k], AX.X, ALU.add),
                     lambda k: dve.wait_ge(s_sq, 2 * gg + k + 1))
                both(lambda k: dve.tensor_scalar(S(k, 3), S(k, 2), 1.0 / D, LN_EPS, ALU.mult, ALU.add))
                both(lambda k: dve.reciprocal(S(k, 3), S(k, 3)))
                if unit:
                    both(lambda k: dve.tensor_tensor(S(k, 4), S(k, 2), S(k, 3), ALU.mult),
                         lambda k: dve.wait_ge(s_sqrt, roots * gg + k + 1))
                    both(lambda k: dve.tensor_tensor(S(k, 4), S(k, 4), S(k, 3), ALU.mult))
                    both(lambda k: dve.tensor_scalar(S(k, 4), S(k, 4), N_EPS, None, ALU.max),
                         lambda k: dve.wait_ge(s_sqrt, roots * gg + k + 3))
                    both(lambda k: dve.reciprocal(S(k, 5), S(k, 4)))
                    both(lambda k: dve.scalar_tensor_tensor(out=S(k, 5), in0=S(k, 5), scalar=FS, in1=S(k, 3),
                                                            op0=ALU.mult, op1=ALU.mult))
                else:
                    both(lambda k: dve.tensor_scalar(S(k, 5), S(k, 3), FS, None, ALU.mult),
                         lambda k: dve.wait_ge(s_sqrt, roots * gg + k + 1))
                both(lambda k: dve.tensor_tensor(xc[:, k], xc[:, k], bc(S(k, 5), D), ALU.mult))
                part = lambda k, x: (ftok[:, js(k), x * D:x * D + D] if unit else tk[:, k, :, x * D:x * D + D])

                def free(k):
                    if not unit:
                        dve.wait_ge(s_T, 2 * gg + k + 1)
                both(lambda k: dve.tensor_copy(part(k, 0), xc[:, k]), free)
                both(lambda k: dve.tensor_tensor(part(k, 1), xc[:, k], part(k, 0), ALU.subtract))
                assert both.count[0] == LINKS

        @block.tensor
        def _(pe):
            pe.sem_inc(s_T, 2)
            with pe.Fori(0, NG // 2) as gg:
                for k in range(2):
                    g = 2 * gg + k
                    pe.wait_ge(s_link, gg * (2 * LINKS) + done(PARTS, k))
                    pe.wait_ge(s_ev, g + 1)
                    for j in range(GRP):
                        m = pe.transpose(pT[:, k, j * 128:j * 128 + 128], ftok[:, g * GRP + j, :] if unit else tk[:, k, j, :], ident[:, :])
                    m.then_inc(s_T, 1)

        @block.scalar
        def _(act):
            act.preload_act_table(ACT.Sqrt)
            act.sem_inc(s_ev, 2)

            def statistics(gg):
                for k in range(2):
                    act.wait_ge(s_link, gg * (2 * LINKS) + done(CENTERED, k))
                    act.activation(sq[:, k], xc[:, k], ACT.Square).then_inc(s_sq, 1)
                for i, op in enumerate((VAR, SQUARE) if unit else (VAR,)):
                    for k in range(2):
                        act.wait_ge(s_link, gg * (2 * LINKS) + done(op, k))
                        act.activation(st[:, k, 3 + i, :], st[:, k, 3 + i, :], ACT.Sqrt).then_inc(s_sqrt, 1)

            def features(gg):
                for k in range(2):
                    act.wait_ge(s_T, 2 * gg + k + 3)
                    act.activation(Fhl[:, bass.ds((2 * gg + k) * QB, QB)], pT[:, k, 0:QB], ACT.Copy).then_inc(s_ev, 1)

            statistics(0)
            with act.Fori(1, NG // 2) as gg:
                statistics(gg)
                features(gg - 1)
            features(NG // 2 - 1)


def attention(nc, Fhl, ftok, OT, den):
    U = 2 * NTT
    with ExitStack() as ctx:
        sb = lambda name, shape, dt=F32: ctx.enter_context(nc.sbuf_tensor(name, shape, dt))
        ps = lambda name, shape, dt=F32: ctx.enter_context(nc.psum_tensor(name, shape, dt))
        sem = lambda name: ctx.enter_context(semaphore(nc, name))
        qhi = sb("D_qhi", [128, 2, QB], F16)
        qlo = sb("D_qlo", [128, 2, QB], F16)
        E = sb("D_E", [128, 4, QH])
        Eh = sb("D_Eh", [128, 4, QH], F16)
        El = sb("D_El", [128, 4, QH], F16)
        pS = ps("D_pS", [128, 4, 512])
        pO = ps("D_pO", [128, 2, 2, 512])
        s_q = [sem(f"D_queries_in{k}") for k in range(2)]
        s_S = sem("D_scores")
        s_E = sem("D_exp")
        s_hD = sem("D_exp_high")
        s_lo = sem("D_exp_low")
        s_pv = sem("D_weighted")
        s_ev = sem("D_out_copied")
        block = ctx.enter_context(nc.Block())

        @block.sync
        def _(sp):
            def load(k, b):
                cols = bass.ds(b * QB, QB)
                for dst, p in ((qhi, 0), (qlo, D)):
                    for half in range(2):
                        sp.dma_start(dst[half * D:half * D + D, k, :], Fhl[p:p + D, cols]).then_inc(s_q[k], 16)
            load(0, 0)
            load(1, 1)
            with sp.Fori(0, NG // 2 - 1) as bb:
                for k in range(2):
                    sp.wait_ge(s_pv, bb * (2 * U) + (k + 1) * U + 4)
                    load(k, 2 * bb + 2 + k)

        @block.tensor
        def _(pe):
            def scores(r, k, j, half):
                keys = Fhl[:, bass.ds(j * 128, 128)]
                cols = slice(half * QH, half * QH + QH)
                pe.matmul(pS[:, r, 0:QH], keys, qhi[:, k, cols], start=True, stop=False)
                pe.matmul(pS[:, r, 0:QH], keys, qlo[:, k, cols], start=False, stop=True).then_inc(s_S, 1)

            def weigh(r, k, j, half, first, last, u):
                pe.wait_ge(s_lo, u + 1)
                f = ftok[:, j, :]
                pe.matmul(pO[:, k, half, 0:QH], f, Eh[:, r, :], start=first, stop=False)
                pe.matmul(pO[:, k, half, 0:QH], f, El[:, r, :], start=False, stop=last).then_inc(s_pv, 1)

            def four(k, base, j, first=False, last=False, next_load=None, end=False):
                for r in range(4):
                    ahead = r + 3
                    if not (end and ahead >= 4):
                        pe.wait_ge(s_E, base + r + 1)
                        if last and ahead >= 4:
                            if r == 1:
                                pe.wait_ge(s_q[1 - k], next_load)
                            scores(ahead % 4, 1 - k, (ahead - 4) // 2, ahead % 2)
                        else:
                            scores(ahead % 4, k, j + ahead // 2, ahead % 2)
                    weigh(r, k, j + r // 2, r % 2, first and r < 2, last and r >= 2, base + r)

            def query_block(k, b, next_load, end=False):
                pe.wait_ge(s_ev, b + 1)
                four(k, b * U, 0, first=True)
                with pe.Fori(1, NTT // 2 - 1) as m:
                    four(k, b * U + 4 * m, 2 * m)
                four(k, b * U + U - 4, NTT - 2, last=True, next_load=next_load, end=end)

            pe.wait_ge(s_q[0], 64)
            for r in range(3):
                scores(r, 0, r // 2, r % 2)
            with pe.Fori(0, NG // 2 - 1) as bb:
                query_block(0, 2 * bb, 64 * bb + 64)
                query_block(1, 2 * bb + 1, 64 * bb + 128)
            query_block(0, NG - 2, 64 * (NG // 2))
            query_block(1, NG - 1, None, end=True)

        @block.scalar
        def _(act):
            act.preload_act_table(ACT.Exp)
            act.sem_inc(s_E, 1)
            act.sem_inc(s_pv, 4)
            with act.Fori(0, NG * NTT // 2) as m:
                for r in range(4):
                    act.wait_ge(s_S, 4 * m + r + 1)
                    act.wait_ge(s_pv, 4 * m + r + 1)
                    if r % 2 == 0:
                        act.activation(Eh[:, r, :], pS[:, r, 0:QH], ACT.Exp, scale=1.0 / (FS * FS))
                    act.activation(E[:, r, :], pS[:, r, 0:QH], ACT.Exp, scale=1.0 / (FS * FS),
                                   accum_out=den[:, bass.ds(4 * m + r, 1)]).then_inc(s_E, 1)

        @block.vector
        def _(dve):
            dve.sem_inc(s_ev, 2)

            def four(m):
                for r in range(4):
                    dve.wait_ge(s_E, 4 * m + r + 2)
                    if r % 2 == 1:
                        dve.tensor_copy(Eh[:, r, :], E[:, r, :]).then_inc(s_hD, 1)
                        dve.wait_ge(s_hD, 2 * m + r // 2 + 1)
                    dve.tensor_tensor(El[:, r, :], E[:, r, :], Eh[:, r, :], ALU.subtract).then_inc(s_lo, 1)

            def copy_out(b, k):
                dve.wait_ge(s_pv, b * U + U + 4)
                dve.tensor_copy(OT[:, bass.ds(b * QB, QB)].rearrange("p (a n) -> p a n", a=2),
                                pO[:, k, :, 0:QH]).then_inc(s_ev, 1)

            M = NTT // 2
            with dve.Fori(0, M) as m:
                four(m)
            with dve.Fori(0, NG // 2 - 1) as bb:
                for k in range(2):
                    four((2 * bb + k + 1) * M)
                    copy_out(2 * bb + k, k)
                    with dve.Fori(1, M) as m:
                        four((2 * bb + k + 1) * M + m)
            four((NG - 1) * M)
            copy_out(NG - 2, 0)
            with dve.Fori(1, M) as m:
                four((NG - 1) * M + m)
            copy_out(NG - 1, 1)


def blend(nc, h, hout, ftok, OT, den, fold):
    with ExitStack() as ctx:
        sb = lambda name, shape, dt=F32: ctx.enter_context(nc.sbuf_tensor(name, shape, dt))
        ps = lambda name, shape, dt=F32: ctx.enter_context(nc.psum_tensor(name, shape, dt))
        sem = lambda name: ctx.enter_context(semaphore(nc, name))
        hin = sb("F_hin", [128, 2, GRP, D])
        f8 = sb("F_f8", [128, 2, GRP, D])
        fc = sb("F_fc", [128, 2, GRP, D])
        sq = sb("F_sq", [128, 2, GRP, D])
        ho = sb("F_ho", [128, 2, GRP, D])
        rden = sb("F_rden", [128, NTT])
        st = sb("F_st", [128, 2, 2, GRP])
        pt = ps("F_pt", [128, 2, 512])
        ot = sb("F_ot", [128, 2, QB])
        s_in = [sem(f"F_h_in{k}") for k in range(2)]
        s_link = sem("F_step")
        s_den = sem("F_sum_step")
        s_root = sem("F_root")
        s_used = sem("F_rows_used")
        s_sq = sem("F_squares")
        s_out = sem("F_out")
        s_ot = sem("F_sums_moved")
        s_T = sem("F_token_rows")
        s_st = [sem(f"F_stored{k}") for k in range(2)]
        hv = h.rearrange("(g p j) c -> g p j c", p=128, j=GRP)
        ov = hout.rearrange("(g p j) c -> g p j c", p=128, j=GRP)
        block = ctx.enter_context(nc.Block())

        LINKS = 7
        BLENDED, SQUARE, SCALED = 2, 3, 6

        @block.sync
        def _(sp):
            sp.dma_start(hin[:, 0], hv[0]).then_inc(s_in[0], 16)
            sp.dma_start(hin[:, 1], hv[1]).then_inc(s_in[1], 16)
            with sp.Fori(0, NG // 2 - 1) as gg:
                for k in range(2):
                    sp.wait_ge(s_out, 2 * gg + k + 3)
                    sp.dma_start(hin[:, k], hv[2 * gg + 2 + k]).then_inc(s_in[k], 16)
                    sp.dma_start(ov[2 * gg + k], ho[:, k]).then_inc(s_st[k], 16)
            for k in range(2):
                sp.wait_ge(s_out, NG - 2 + k + 3)
                sp.dma_start(ov[NG - 2 + k], ho[:, k]).then_inc(s_st[k], 16)
            for k in range(2):
                sp.wait_ge(s_st[k], 16 * (NG // 2) + 16)

        @block.tensor
        def _(pe):
            with pe.Fori(0, NG // 2) as gg:
                for k in range(2):
                    pe.wait_ge(s_used, 2 * gg + 2)
                    pe.wait_ge(s_ot, 2 * gg + k + 1)
                    for j in range(GRP):
                        m = pe.matmul(pt[:, k, j * D:j * D + D], ot[:, k, j * 128:j * 128 + 128], fold[:, :], start=True, stop=True)
                    m.then_inc(s_T, 1)

        @block.gpsimd
        def _(pool):
            pool.sem_inc(s_out, 2)
            for k in range(2):
                pool.sem_inc(s_st[k], 16)
            with pool.Fori(0, NG // 2) as gg:
                for k in range(2):
                    pool.wait_ge(s_link, gg * (2 * LINKS) + done(SCALED, k))
                    pool.wait_ge(s_in[k], 16 * gg + 16)
                    pool.wait_ge(s_st[k], 16 * gg + 16)
                    pool.tensor_tensor(ho[:, k], hin[:, k], fc[:, k], ALU.add).then_inc(s_out, 1)

        @block.scalar
        def _(act):
            act.preload_act_table(ACT.Sqrt)
            act.sem_inc(s_T, 2)

            def move(gg):
                for k in range(2):
                    g = 2 * gg + k
                    act.wait_ge(s_T, g + 1)
                    act.activation(ot[:, k, :], OT[:, bass.ds(g * QB, QB)], ACT.Copy).then_inc(s_ot, 1)

            def norms(gg):
                for k in range(2):
                    act.wait_ge(s_link, gg * (2 * LINKS) + done(BLENDED, k))
                    act.activation(sq[:, k], fc[:, k], ACT.Square).then_inc(s_sq, 1)
                for k in range(2):
                    act.wait_ge(s_link, gg * (2 * LINKS) + done(SQUARE, k))
                    act.activation(st[:, k, 0, :], st[:, k, 0, :], ACT.Sqrt).then_inc(s_root, 1)

            move(0)
            with act.Fori(0, NG // 2 - 1) as gg:
                move(gg + 1)
                norms(gg)
            norms(NG // 2 - 1)

        @block.vector
        def _(dve):
            dve.sem_inc(s_used, 2)
            link = linker(dve, s_den)
            link(dve.tensor_reduce(rden[:, :], den[:, :].rearrange("p (b j a) -> p j b a", j=NTT, a=2), AX.XY, ALU.add))
            link(dve.reciprocal(rden[:, :], rden[:, :]))
            link(dve.tensor_scalar(rden[:, :], rden[:, :], (1.0 - BLEND) / FS, None, ALU.mult))
            with dve.Fori(0, NG // 2) as gg:
                both = pairs(dve, s_link, gg * (2 * LINKS))
                js = lambda k: bass.ds((2 * gg + k) * GRP, GRP)

                def free(k):
                    dve.wait_ge(s_T, 2 * gg + k + 3)
                    dve.wait_ge(s_out, 2 * gg + k + 1)

                both(lambda k: dve.tensor_tensor(f8[:, k], ftok[:, js(k), 0:D], ftok[:, js(k), D:2 * D], ALU.add))
                both(lambda k: dve.tensor_tensor(fc[:, k], pt[:, k, 0:GRP * D].rearrange("p (j c) -> p j c", c=D),
                                                 bc(rden[:, js(k)], D), ALU.mult), free)
                both(lambda k: dve.scalar_tensor_tensor(out=fc[:, k], in0=f8[:, k], scalar=BLEND / FS, in1=fc[:, k],
                                                        op0=ALU.mult, op1=ALU.add))
                dve.sem_inc(s_used, 2)
                both(lambda k: dve.tensor_reduce(st[:, k, 0, :], sq[:, k], AX.X, ALU.add),
                     lambda k: dve.wait_ge(s_sq, 2 * gg + k + 1))
                both(lambda k: dve.tensor_scalar(st[:, k, 0, :], st[:, k, 0, :], N_EPS, None, ALU.max),
                     lambda k: dve.wait_ge(s_root, 2 * gg + k + 1))
                both(lambda k: dve.reciprocal(st[:, k, 1, :], st[:, k, 0, :]))
                both(lambda k: dve.tensor_tensor(fc[:, k], fc[:, k], bc(st[:, k, 1, :], D), ALU.mult))
                assert both.count[0] == LINKS


RWKV_INS = ("x_mix", "W_r", "W_k", "W_v", "W_o", "A_w", "B_w", "b_w", "A_a", "B_a", "b_a", "A_g", "B_g",
            "k_k", "k_a", "r_k", "gn_w", "gn_b")


def network(nc, ins, cst, out):
    dram = lambda name, shape: nc.dram_tensor(name, shape, F32, kind="Internal").ap()
    hA, hB, hC, hD = (dram(f"h_{x}", [TOK, D]) for x in ("tokens", "rwkv", "experts1", "attention"))
    buf = dram("expert_rows", [EX * CAP + TOK, D])
    ybuf = dram("expert_outputs", [EX * CAP, D])
    part = lambda pre: {k[len(pre):]: v for k, v in ins.items() if k.startswith(pre)}

    tk = part("L0_tok_")
    tokenizer(nc, ins["x"], tk["W1"], tk["b1"], tk["W2"], tk["b2"], tk["W3"], tk["b3"], hA)

    with ExitStack() as ctx:
        sb = lambda name, shape, dt=F32: ctx.enter_context(nc.sbuf_tensor(name, shape, dt))
        w, c = weights(nc, ctx, part("L0_attn_"), cst)
        rkv = sb("rkv", [128, NTT, 3 * D])
        rn = sb("rn", [128, NTT])
        ga = sb("ga", [128, NTT, D])
        with nc.sbuf_tensor("Z2", [128, TOK], F32) as Z2:
            norm_features(nc, hA, Z2, c["eye"])
            project(nc, w, Z2, rkv, rn)
            recurrence(nc, w, c, Z2, rkv, ga, rn)
        outputs(nc, w, hA, hB, rkv, ga, c["eye"])

    with ExitStack() as ctx:
        sb = lambda name, shape, dt=F32: ctx.enter_context(nc.sbuf_tensor(name, shape, dt))
        eye = sb("eye", [128, 128])
        eye16 = sb("eye16c", [128, 128], F16)
        XT = sb("XT1", [128, TOK], F16)
        load_all(nc, "C", [(eye[:, :], cst["eye"]), (eye16[:, :], cst["eye16"])])
        w = moe1_weights(nc, ctx, part("L0_ffn_"), cst)
        split_features(nc, "C0_", hB, XT, eye16)
        experts_dense(nc, hB, hC, XT, w, eye, 2)

    with ExitStack() as ctx:
        sb = lambda name, shape, dt=F32: ctx.enter_context(nc.sbuf_tensor(name, shape, dt))
        Fhl = sb("Fhl", [128, TOK], F16)
        ftok = sb("ftok", [128, NTT, 128], F16)
        OT = sb("OT", [128, TOK])
        den = sb("den", [128, NG * NTT * 2])
        eye16 = sb("eye16", [128, 128], F16)
        fold = sb("fold", [128, D])
        load_all(nc, "D", [(eye16[:, :], cst["eye16"]), (fold[:, :], cst["fold"])])
        split_features(nc, "D_", hC, Fhl, eye16, ftok)
        attention(nc, Fhl, ftok, OT, den)
        blend(nc, hC, hD, ftok, OT, den, fold)

    with ExitStack() as ctx:
        sb = lambda name, shape, dt=F32: ctx.enter_context(nc.sbuf_tensor(name, shape, dt))
        p = part("L1_ffn_")
        eye = sb("eye2", [128, 128])
        cw = sb("cw2", [128, NTT, EX])
        chosen = sb("chosen", [128, NTT, EX])
        rows = sb("rows", [128, NTT, D])
        dest = sb("dest", [128, NTT], U32)
        src = sb("src", [128, NTT], U32)
        wt = sb("wt", [128, NTT])
        gw = sb("gate_w2", [D, EX])
        gb = sb("gate_b2", [128, EX])
        c = {k: sb(f"c_{k}", list(v.shape)) for k, v in cst.items() if k in MOE_CONSTANTS}
        load_all(nc, "E", [(eye[:, :], cst["eye"]), (gw[:, :], p["gate_w"]),
                           (gb[:, :], p["gate_b"].rearrange("(a c) -> a c", a=1).broadcast_to([128, EX]))]
                 + [(c[k][:, :], cst[k]) for k in MOE_CONSTANTS])
        zeros = sb("zeros", [SR, CAP // SR * D])
        s_z, s_zero = (ctx.enter_context(semaphore(nc, x)) for x in ("zeros_made", "rows_cleared"))
        clear_rows(nc, buf, zeros, s_z, s_zero)
        with nc.sbuf_tensor("XT2", [D, TOK], F32) as XT:
            layer_norm(nc, "E0_", hD, XT, eye, rows)
            gating(nc, "E1_", XT, gw[:, :], gb[:, :], c["less"][:, :], 1, cw, chosen)
        slots(nc, c, chosen, cw, dest, src, wt)
        dispatch(nc, rows, dest, buf, s_zero)
        experts_sparse(nc, p, buf, ybuf, eye)
        combine(nc, hD, out, ybuf, src, wt)


MOE_CONSTANTS = ("less", "base", "dump", "upto")


def load_all(nc, name, loads):
    with semaphore(nc, name + "_loaded") as s, nc.Block() as block:
        @block.sync
        def _(sp):
            for dst, src in loads:
                sp.dma_start(dst, src).then_inc(s, 16)
            sp.wait_ge(s, 16 * len(loads))


def all_constants():
    c = dict(constants())
    c.update(moe_constants())
    c["eye16"] = np.eye(128).astype(np.float16)
    c["fold"] = np.tile(np.eye(D), (2, 1)).astype(np.float32)
    return c


def tap_rows(W):
    W = W.reshape(CH, 9, -1).transpose(1, 0, 2)[[3 * i + j for i, j in TAPS]].reshape(9 * CH, -1)
    return np.concatenate([W, np.zeros((NCH * 128 - 9 * CH, W.shape[1]), W.dtype)])


def kernel(**inputs):
    import concourse.bacc as _bacc
    from concourse.bass_utils import run_bass_kernel_spmd as _run

    data = {k: np.asarray(v) for k, v in inputs.items()}
    data["x"] = data["x"].reshape(BATCH, CH, IMG, IMG)
    data["L0_tok_W1"] = tap_rows(data["L0_tok_W1"])
    data["L0_tok_W2"] = tap_rows(data["L0_tok_W2"].T).T
    data["L0_tok_b2"] = tap_rows(data["L0_tok_b2"][:, None])[:, 0]
    data["L0_tok_W3"] = tap_rows(data["L0_tok_W3"])

    nc = _bacc.Bacc("TRN2", target_bir_lowering=False, num_devices=1)
    arrays = {}

    def place(name, a):
        arrays[name] = np.ascontiguousarray(a)
        return nc.dram_tensor(name, a.shape, mybir.dt.from_np(a.dtype), kind="ExternalInput").ap()
    ins = {k: place("in_" + k, v) for k, v in data.items()}
    cst = {k: place("const_" + k, v) for k, v in all_constants().items()}
    out = nc.dram_tensor("out", (TOK, D), F32, kind="ExternalOutput").ap()
    network(nc, ins, cst, out)
    r = _run(nc, [arrays], core_ids=[0])
    return r.results[0]["out"].reshape(BATCH, SEQ, D)
```
